# Optimizing a Trainium2 kernel written in Bass

```python
import numpy as np
import jax
import jax.numpy as jnp

def _softmax(x, axis=-1):
    return jax.nn.softmax(x, axis=axis)

def _gelu(x):
    return jax.nn.gelu(x, approximate=True)

def _silu(x):
    return jax.nn.silu(x)

def _sigmoid(x):
    return jax.nn.sigmoid(x)

def _layernorm(x, axis=-1, eps=1e-05):
    m = jnp.mean(x, axis=axis, keepdims=True)
    v = jnp.var(x, axis=axis, keepdims=True)
    return (x - m) / jnp.sqrt(v + eps)

def _scatter_add(tgt, idx, src, axis=0):
    return tgt.at[idx].add(src)

def _segment_sum(src, seg, n):
    return jax.ops.segment_sum(src, seg, n)
kernel_name = 'mk_audio_tower_d1_tok_audfeat512_r4_ef332b'

def setup_inputs(seed: int=0):
    np.random.seed(seed)
    _w = jnp.asarray

    def _rec_inputs():
        import jax
        import jax.numpy as jnp
        _rk = jax.random.key(seed)
        x = -0.000684094 + 1.00049 * jax.random.normal(jax.random.fold_in(_rk, 1), (8, 375, 23), jnp.float32)
        return x
    x = _rec_inputs()

    def _L0_tok_setup():
        import jax, jax.numpy as jnp
        import numpy as np
        CONTEXT = 5
        DILATION = 1
        BN_EPS = 1e-05
        key = jax.random.key(seed)
        k1, k2, k3 = jax.random.split(key, 3)
        B, T, D, O = (64, 500, 23, 128)
        x = jax.random.normal(k1, (B, T, D), dtype=jnp.float32)
        W = jax.random.normal(k2, (O, D * CONTEXT), dtype=jnp.float32) * 0.05
        b = jax.random.normal(k3, (O,), dtype=jnp.float32) * 0.05
        return {'x': x, 'W': W, 'b': b}
    _L0_tok_all = _L0_tok_setup()
    _L0_tok_in = {k: v for k, v in _L0_tok_all.items() if k in ('W', 'b')}
    del _L0_tok_all

    def _L0_attn_setup():
        import jax, jax.numpy as jnp
        import numpy as np
        DIM = 128
        HEADS = 8
        DIM_HEAD = 64
        INNER = HEADS * DIM_HEAD
        M = 64
        PINV_ITERS = 6
        KERNEL = 33
        SCALE = DIM_HEAD ** (-0.5)
        EPS_LN = 1e-05

        def layer_norm(x, g, b):
            mu = jnp.mean(x, axis=-1, keepdims=True)
            var = jnp.mean((x - mu) ** 2, axis=-1, keepdims=True)
            return (x - mu) * jax.lax.rsqrt(var + EPS_LN) * g + b

        def moore_penrose_pinv(x, iters=PINV_ITERS):
            abs_x = jnp.abs(x)
            col = abs_x.sum(-1)
            row = abs_x.sum(-2)
            z = jnp.swapaxes(x, -1, -2) / (jnp.max(col) * jnp.max(row))
            I = jnp.eye(x.shape[-1], dtype=x.dtype)
            for _ in range(iters):
                xz = x @ z
                z = 0.25 * z @ (13.0 * I - xz @ (15.0 * I - xz @ (7.0 * I - xz)))
            return z

        def nystrom_attention(x, w_qkv, w_out, b_out, w_res):
            b, n, _ = x.shape
            pad = -n % M
            if pad:
                x = jnp.pad(x, ((0, 0), (pad, 0), (0, 0)))
            npad = n + pad
            qkv = x @ w_qkv
            q, k, v = jnp.split(qkv, 3, axis=-1)
            split = lambda t: t.reshape(b, npad, HEADS, DIM_HEAD).transpose(0, 2, 1, 3)
            q, k, v = (split(q), split(k), split(v))
            q = q * SCALE
            l = npad // M
            q_l = q.reshape(b, HEADS, M, l, DIM_HEAD).mean(3)
            k_l = k.reshape(b, HEADS, M, l, DIM_HEAD).mean(3)
            sim1 = jnp.einsum('bhid,bhjd->bhij', q, k_l)
            sim2 = jnp.einsum('bhid,bhjd->bhij', q_l, k_l)
            sim3 = jnp.einsum('bhid,bhjd->bhij', q_l, k)
            attn1 = jax.nn.softmax(sim1, axis=-1)
            attn2 = jax.nn.softmax(sim2, axis=-1)
            attn3 = jax.nn.softmax(sim3, axis=-1)
            attn2_inv = moore_penrose_pinv(attn2)
            out = attn1 @ attn2_inv @ (attn3 @ v)
            pc = KERNEL // 2
            res = jax.lax.conv_general_dilated(v, w_res, window_strides=(1, 1), padding=((pc, pc), (0, 0)), dimension_numbers=('NCHW', 'OIHW', 'NCHW'), feature_group_count=HEADS)
            out = out + res
            out = out.transpose(0, 2, 1, 3).reshape(b, npad, INNER)
            out = out @ w_out + b_out
            out = out[:, -n:]
            attn = attn1 @ attn2_inv @ attn3
            return (out, attn)

        def _reference_tuple_inner(x, ln_g, ln_b, w_qkv, w_out, b_out, w_res):
            out1, _ = nystrom_attention(layer_norm(x, ln_g, ln_b), w_qkv, w_out, b_out, w_res)
            x2 = x + out1
            _, attn = nystrom_attention(layer_norm(x2, ln_g, ln_b), w_qkv, w_out, b_out, w_res)
            return (x2, attn)
        key = jax.random.key(seed)
        ks = jax.random.split(key, 4)
        n = 1024
        x = jax.random.normal(ks[0], (1, n, DIM), dtype=jnp.float32)
        w_qkv = jax.random.normal(ks[1], (DIM, 3 * INNER), dtype=jnp.float32) * DIM ** (-0.5)
        w_out = jax.random.normal(ks[2], (INNER, DIM), dtype=jnp.float32) * INNER ** (-0.5)
        b_out = jnp.zeros((DIM,), dtype=jnp.float32)
        w_res = jax.random.normal(ks[3], (HEADS, 1, KERNEL, 1), dtype=jnp.float32) * KERNEL ** (-0.5)
        ln_g = jnp.ones((DIM,), dtype=jnp.float32)
        ln_b = jnp.zeros((DIM,), dtype=jnp.float32)
        return {'x': x, 'ln_g': ln_g, 'ln_b': ln_b, 'w_qkv': w_qkv, 'w_out': w_out, 'b_out': b_out, 'w_res': w_res}
    _L0_attn_all = _L0_attn_setup()
    _L0_attn_in = {k: v for k, v in _L0_attn_all.items() if k in ('ln_g', 'ln_b', 'w_qkv', 'w_out', 'b_out', 'w_res')}
    del _L0_attn_all

    def _L0_ffn_setup():
        import jax, jax.numpy as jnp
        import numpy as np
        B, T, D = (4, 128, 128)
        N = 128
        key = jax.random.key(seed)
        ks = jax.random.split(key, 6)
        x = jax.random.normal(ks[0], (B, T, D), dtype=jnp.float32)
        positions = jax.random.normal(ks[1], (N, D), dtype=jnp.float32) * 0.1
        scales = jnp.ones((N,), dtype=jnp.float32) * 10.0
        value_weight = jax.random.normal(ks[2], (N, D, D), dtype=jnp.float32) * 0.02
        out_W = jax.random.normal(ks[3], (D, D), dtype=jnp.float32) * (1.0 / np.sqrt(D))
        out_b = jax.random.normal(ks[4], (D,), dtype=jnp.float32) * 0.01
        return {'x': x, 'positions': positions, 'scales': scales, 'value_weight': value_weight, 'out_W': out_W, 'out_b': out_b}
    _L0_ffn_all = _L0_ffn_setup()
    _L0_ffn_in = {k: v for k, v in _L0_ffn_all.items() if k in ('positions', 'scales', 'value_weight', 'out_W', 'out_b')}
    del _L0_ffn_all
    return {'x': x, 'L0_tok_W': _L0_tok_in['W'], 'L0_tok_b': _L0_tok_in['b'], 'L0_attn_ln_g': _L0_attn_in['ln_g'], 'L0_attn_ln_b': _L0_attn_in['ln_b'], 'L0_attn_w_qkv': _L0_attn_in['w_qkv'], 'L0_attn_w_out': _L0_attn_in['w_out'], 'L0_attn_b_out': _L0_attn_in['b_out'], 'L0_attn_w_res': _L0_attn_in['w_res'], 'L0_ffn_positions': _L0_ffn_in['positions'], 'L0_ffn_scales': _L0_ffn_in['scales'], 'L0_ffn_value_weight': _L0_ffn_in['value_weight'], 'L0_ffn_out_W': _L0_ffn_in['out_W'], 'L0_ffn_out_b': _L0_ffn_in['out_b']}

def reference(x, L0_tok_W, L0_tok_b, L0_attn_ln_g, L0_attn_ln_b, L0_attn_w_qkv, L0_attn_w_out, L0_attn_b_out, L0_attn_w_res, L0_ffn_positions, L0_ffn_scales, L0_ffn_value_weight, L0_ffn_out_W, L0_ffn_out_b):
    import jax
    import jax.numpy as jnp

    def _L0_tok_ref(x, W, b):
        import jax, jax.numpy as jnp
        import numpy as np
        CONTEXT = 5
        DILATION = 1
        BN_EPS = 1e-05
        B, T, D = x.shape
        L = T - DILATION * (CONTEXT - 1)
        windows = jnp.stack([x[:, i * DILATION:i * DILATION + L] for i in range(CONTEXT)], axis=2)
        h = jnp.einsum('blk,ok->blo', windows.reshape(B, L, CONTEXT * D), W) + b
        h = jax.nn.relu(h)
        mean = jnp.mean(h, axis=(0, 1))
        var = jnp.var(h, axis=(0, 1))
        return (h - mean) * jax.lax.rsqrt(var + BN_EPS)

    def _L0_attn_ref(x, ln_g, ln_b, w_qkv, w_out, b_out, w_res):
        import jax, jax.numpy as jnp
        import numpy as np
        DIM = 128
        HEADS = 8
        DIM_HEAD = 64
        INNER = HEADS * DIM_HEAD
        M = 64
        PINV_ITERS = 6
        KERNEL = 33
        SCALE = DIM_HEAD ** (-0.5)
        EPS_LN = 1e-05

        def layer_norm(x, g, b):
            mu = jnp.mean(x, axis=-1, keepdims=True)
            var = jnp.mean((x - mu) ** 2, axis=-1, keepdims=True)
            return (x - mu) * jax.lax.rsqrt(var + EPS_LN) * g + b

        def moore_penrose_pinv(x, iters=PINV_ITERS):
            abs_x = jnp.abs(x)
            col = abs_x.sum(-1)
            row = abs_x.sum(-2)
            z = jnp.swapaxes(x, -1, -2) / (jnp.max(col) * jnp.max(row))
            I = jnp.eye(x.shape[-1], dtype=x.dtype)
            for _ in range(iters):
                xz = x @ z
                z = 0.25 * z @ (13.0 * I - xz @ (15.0 * I - xz @ (7.0 * I - xz)))
            return z

        def nystrom_attention(x, w_qkv, w_out, b_out, w_res):
            b, n, _ = x.shape
            pad = -n % M
            if pad:
                x = jnp.pad(x, ((0, 0), (pad, 0), (0, 0)))
            npad = n + pad
            qkv = x @ w_qkv
            q, k, v = jnp.split(qkv, 3, axis=-1)
            split = lambda t: t.reshape(b, npad, HEADS, DIM_HEAD).transpose(0, 2, 1, 3)
            q, k, v = (split(q), split(k), split(v))
            q = q * SCALE
            l = npad // M
            q_l = q.reshape(b, HEADS, M, l, DIM_HEAD).mean(3)
            k_l = k.reshape(b, HEADS, M, l, DIM_HEAD).mean(3)
            sim1 = jnp.einsum('bhid,bhjd->bhij', q, k_l)
            sim2 = jnp.einsum('bhid,bhjd->bhij', q_l, k_l)
            sim3 = jnp.einsum('bhid,bhjd->bhij', q_l, k)
            attn1 = jax.nn.softmax(sim1, axis=-1)
            attn2 = jax.nn.softmax(sim2, axis=-1)
            attn3 = jax.nn.softmax(sim3, axis=-1)
            attn2_inv = moore_penrose_pinv(attn2)
            out = attn1 @ attn2_inv @ (attn3 @ v)
            pc = KERNEL // 2
            res = jax.lax.conv_general_dilated(v, w_res, window_strides=(1, 1), padding=((pc, pc), (0, 0)), dimension_numbers=('NCHW', 'OIHW', 'NCHW'), feature_group_count=HEADS)
            out = out + res
            out = out.transpose(0, 2, 1, 3).reshape(b, npad, INNER)
            out = out @ w_out + b_out
            out = out[:, -n:]
            attn = attn1 @ attn2_inv @ attn3
            return (out, attn)

        def _reference_tuple_inner(x, ln_g, ln_b, w_qkv, w_out, b_out, w_res):
            out1, _ = nystrom_attention(layer_norm(x, ln_g, ln_b), w_qkv, w_out, b_out, w_res)
            x2 = x + out1
            _, attn = nystrom_attention(layer_norm(x2, ln_g, ln_b), w_qkv, w_out, b_out, w_res)
            return (x2, attn)
        return _reference_tuple_inner(x, ln_g, ln_b, w_qkv, w_out, b_out, w_res)[0]

    def _L0_ffn_ref(x, positions, scales, value_weight, out_W, out_b):
        import jax, jax.numpy as jnp
        import numpy as np
        B, T, D = (4, 128, 128)
        N = 128
        diff = x[:, :, None, :] - positions[None, None, :, :]
        distances = jnp.linalg.norm(diff, axis=-1)
        interactions = scales / (distances + 0.1)
        attn = jax.nn.softmax(interactions, axis=-1)
        out = jnp.einsum('btn,btd,nde->bte', attn, x, value_weight)
        return out @ out_W.T + out_b
    h = _L0_tok_ref(x, L0_tok_W, L0_tok_b)
    h = h + _L0_attn_ref(_layernorm(h, axis=-1), L0_attn_ln_g, L0_attn_ln_b, L0_attn_w_qkv, L0_attn_w_out, L0_attn_b_out, L0_attn_w_res)
    h = h + _L0_ffn_ref(_layernorm(h, axis=-1), L0_ffn_positions, L0_ffn_scales, L0_ffn_value_weight, L0_ffn_out_W, L0_ffn_out_b)
    return h

_drawn_inputs = setup_inputs


def setup_inputs(seed=0):
    import zlib

    import numpy as np

    out = dict(_drawn_inputs(seed))
    spreads = {'L0_attn_ln_g': (1.0, 0.2),
     'L0_attn_ln_b': (0.0, 0.1),
     'L0_attn_b_out': (0.0, 0.1),
     'L0_ffn_scales': (10.0, 0.6)}
    factors = {'L0_ffn_positions': 8.0,
     'L0_ffn_value_weight': 5.973,
     'L0_ffn_out_W': 6.04,
     'L0_ffn_out_b': 8.0}
    for name, (base, spread) in spreads.items():
        noise = np.random.default_rng([zlib.crc32(name.encode()), seed]).standard_normal(out[name].shape)
        drawn = base * np.exp(spread * noise) if base else spread * noise
        out[name] = jnp.asarray(drawn.astype(out[name].dtype))
    for name, factor in factors.items():
        out[name] = (out[name] * factor).astype(out[name].dtype)
    return out
```

```python
from contextlib import ExitStack

import concourse.bass as bass
from concourse import mybir

F32 = mybir.dt.float32
F32R = mybir.dt.float32r
ALU = mybir.AluOpType
ACT = mybir.ActivationFunctionType
AX_X = mybir.AxisListType.X
RMAX = bass.bass_isa.ReduceOp.max

P = 128
B, T, CTX, DIN = 8, 371, 5, 23
KW = CTX * DIN
HEADS, DH, M = 8, 64, 64
PAIRS = HEADS // 2
HM = HEADS * M
PM = PAIRS * M
NP = 384
PAD = NP - T
L = NP // M
TPB = NP // P
TILES = B * TPB
TAPS = 33
HALF = TAPS // 2
CW = P + TAPS - 1
WPAD = P - 1 + TAPS + P - 1
ITERS = 6
EPS = 1e-5
GRP = 4
CHUNKS = P // GRP
YBANKS = 6
SCALE = DH ** -0.5
ZR = 4
DCH = CHUNKS // 2


def audio_tower(nc, xt, tok_wt, tok_b, ln_g, ln_b, w_qkv, w_qk_t, w_out, b_out, w_res, pos_t,
                scales, vw, out_wt, out_b, ident_in, out):
    with ExitStack() as ctx:
        def sb(name, shape, dt=F32, at=ctx):
            return at.enter_context(nc.sbuf_tensor(name, shape, dt))

        def sem(name):
            return ctx.enter_context(nc.semaphore(name))

        bank = [ctx.enter_context(nc.psum_tensor(f"bank{i}", [P, 512], F32)) for i in range(8)]

        ident = sb("ident", [P, P])
        h = sb("h", [P, TILES, P])
        st6 = sb("st6", [P, TILES, 6])
        mv = sb("mv", [P, TILES, 2])
        r0 = sb("r0", [P, TILES])
        r1 = sb("r1", [P, TILES])
        tsm = sb("tsm", [P, TILES])
        sq = sb("sq", [P, TILES])
        u2 = sb("u2", [P, TILES])
        mx24 = sb("mx24", [P, TILES])
        posT = sb("posT", [P, P])
        posT2 = sb("posT2", [P, P])
        possq = sb("possq", [P, P])
        ones = sb("ones", [P, P])
        p2row = sb("p2row", [P, P])
        scrow = sb("scrow", [P, P])
        outWT = sb("outWT", [P, P])
        outb = sb("outb", [P, P])
        bout = sb("bout", [P, P])
        vec = sb("vec", [P, 3])
        bnst = sb("bnst", [P, B, 6])
        bnmv = sb("bnmv", [P, 2])
        bnr = sb("bnr", [P, 2])
        cmx = sb("cmx", [P, 2])
        cmxa = sb("cmxa", [P, 2])
        crc = sb("crc", [P, 2])
        rsx = sb("rsx", [P, 2, B * PAIRS])

        tokW = sb("tokW", [KW, P])
        early = ExitStack()
        v_raw = sb("v_raw", [P, P, P], at=early)
        ARENA = 30600
        arena = sb("arena", [P, ARENA], at=early)
        early.close()
        v_lo = sb("v_lo", [P, P, P], F32R)
        v_hi = sb("v_hi", [P, P, P], F32R)
        uT = sb("uT", [P, TILES + 1, P])
        at_all = sb("at_all", [P, TILES + 1, P])
        zring = sb("zring", [P, ZR, GRP * P])
        xhi = sb("xhi", [P, TPB, P], F32R)
        xlo = sb("xlo", [P, TPB, P], F32R)
        a_st = sb("a_st", [P, TPB, P])
        acc = sb("acc", [P, TPB, 12, P])
        usc = acc[:, 0:2, 0:TPB, :]
        junk = acc[:, 2, 0:TPB, :]
        o_sum = sb("o_sum", [P, TPB, P])
        oT = sb("oT", [P, P])
        o_fin = sb("o_fin", [P, TPB, P])

        cursor = [0]

        def take(*dims):
            n = 1
            for d in dims:
                n *= d
            at = cursor[0]
            cursor[0] += n
            assert cursor[0] <= ARENA, cursor[0]
            v = arena[:, at:at + n]
            if len(dims) == 2:
                v = v.rearrange("p (a b) -> p a b", b=dims[1])
            elif len(dims) == 3:
                v = v.rearrange("p (a b c) -> p a b c", b=dims[1], c=dims[2])
            elif len(dims) == 4:
                v = v.rearrange("p (a b c d) -> p a b c d", b=dims[1], c=dims[2], d=dims[3])
            return v

        wv = take(HM)
        wo = take(PAIRS, P)
        toe = take(HEADS, CW)
        yT = take(B, NP)
        Aq = take(B, HEADS, M)
        Bk = take(B, HEADS, M)
        xaT = take(B, PM)
        ztt = xaT
        mark = cursor[0]
        xa = take(B, PM)
        klT = take(PAIRS, B * M)
        wqk = take(2 * HM)
        wqkT = take(2 * PAIRS, P)
        hT = take(B, NP)
        cursor[0] += PAIRS * B * P - B * NP
        win = take(B, T)
        cursor[0] -= B * T
        xin = take(TILES, P)
        ylT = take(B * M)
        qlT = hT.rearrange("p b t -> p (b t)")[:, 0:PAIRS * B * M].rearrange("p (a m) -> p a m", m=B * M)
        yn = hT.rearrange("p b (i c) -> p b i c", c=P)
        cursor[0] = mark
        Tm = take(B, PM)
        SZ = take(B, PAIRS, 2, M)
        Sb = take(B, PAIRS, P)
        Pb = take(B, PAIRS, P)
        eyes = take(3, M)
        cursor[0] = mark
        yTb = take(2, NP)
        Ab = take(2, HM)
        Bb = take(2, HM)
        ztb = take(2, PM)
        e1 = take(TPB, HEADS, M)
        a1T = take(PAIRS, NP)
        e3 = take(PAIRS, NP)
        e3T = take(TPB, PAIRS, P)
        vb = take(TPB, HM)
        resT = take(PAIRS, NP)
        uTb = take(PAIRS, M)
        uw = take(PAIRS, P)
        gw = take(PAIRS, P)
        m1 = take(TPB, HEADS)
        s1 = take(TPB, HEADS)
        rr1 = take(TPB, HEADS)
        m3 = take(PAIRS)
        s3 = take(PAIRS)
        rr3 = take(PAIRS)

        def half(x):
            return slice(64 * (x % 2), 64 * (x % 2) + 64)

        s = {n: sem(n) for n in """ld_x ld_id ld_vec ld_attn ld_ffn ld_v
        tok_mm relu_done bn_step bn_root hn_done hT_mm h_copied ln_step ln_root
        xin_done yn_done h_plus y_mm y_evac pads_zero yl_done
        qk_mm qk_evac fold_mm fold_evac sim2_mm sm2_step xa_exp xa_done xaT_mm xaT_evac
        cmax_step cmax_all z0_done const_done
        S_mm S_done T1_done T2_mm T2_done P_mm P_done z_mm zt_done zt_odd zb_mm zb_done z_done
        staged sim1_mm v_mm sim3_mm conv_mm e3T_mm uT_mm a1T_mm uw_mm gw_mm out1_mm
        s1_sub s1_norm e1_exp e3_max e3_exp v_evac conv_evac e3T_evac uT_evac rr3_done a1_norm a1T_evac
        uw_evac gw_evac h1_done
        p2_in p2_mm p2_done f_stat f_root u_done u_mm uT_done u2_done d_mm d2_step d_root f_step f_exp fs_step a_done hb_done waits_passed
        vhi_done vlo_done xhi_done xlo_done ast_done pad_tile y_done_f acc_step zact_done accp_step
        o_sum_done oT_mm oT_evac o_mm fin_done stored0 stored1 stored2""".split()}

        def need(eng, name, value):
            if not isinstance(value, int) or value > 0:
                eng.wait_ge(s[name], value)

        def linker(eng, name):
            count = [0]

            def link(ins):
                count[0] += 1
                ins.then_inc(s[name], 1)
                eng.wait_ge(s[name], count[0])
            return link

        def rounds(eng, n, body):
            body(0)
            with eng.Fori(1, n) as i:
                body(i)

        def pinv_rounds(eng, body):
            with eng.Fori(0, ITERS // 2 - 1) as j:
                body(j, False)
            body(ITERS // 2 - 1, True)

        def by_pair(x):
            return x.rearrange("p (a m) -> p a m", m=M)

        reach = [(max(0, P * i - HALF), min(NP, P * i + P + HALF), P * i - HALF) for i in range(TPB)]

        block = ctx.enter_context(nc.Block())

        @block.sync
        def _(sp):
            for i in range(CTX):
                sp.dma_start(win[i * DIN:(i + 1) * DIN], xt[:, :, i:i + T]).then_inc(s["ld_x"], 16)
            sp.dma_start(tokW[:], tok_wt).then_inc(s["ld_x"], 16)
            sp.dma_start(vec[:, 0:1], tok_b).then_inc(s["ld_vec"], 16)
            sp.dma_start(ident[:], ident_in).then_inc(s["ld_id"], 16)
            sp.dma_start(vec[:, 1:2], ln_g).then_inc(s["ld_vec"], 16)
            sp.dma_start(vec[:, 2:3], ln_b).then_inc(s["ld_vec"], 16)
            sp.dma_start(bout[:], b_out.partition_broadcast(P)).then_inc(s["ld_vec"], 16)
            sp.dma_start(posT[:], pos_t).then_inc(s["ld_ffn"], 16)
            sp.dma_start(outWT[:], out_wt).then_inc(s["ld_ffn"], 16)
            sp.dma_start(scrow[:], scales.partition_broadcast(P)).then_inc(s["ld_ffn"], 16)
            sp.dma_start(outb[:], out_b.partition_broadcast(P)).then_inc(s["ld_ffn"], 16)
            sp.wait_ge(s["tok_mm"], B)
            sp.dma_start(wqk, w_qkv[:, 0:2 * HM]).then_inc(s["ld_attn"], 16)
            sp.dma_start(wqkT, w_qk_t).then_inc(s["ld_attn"], 16)
            sp.dma_start(wv, w_qkv[:, 2 * HM:3 * HM]).then_inc(s["ld_attn"], 16)
            sp.dma_start(wo, w_out.rearrange("(a p) n -> p a n", p=P)).then_inc(s["ld_attn"], 16)
            sp.dma_start(toe, w_res).then_inc(s["ld_attn"], 16)
            for k in range(8):
                n = P // 8
                sp.dma_start(v_raw[:, k * n:(k + 1) * n, :],
                             vw[k * n:(k + 1) * n].rearrange("n d e -> d n e")).then_inc(s["ld_v"], 16)
            with sp.Fori(0, B) as b:
                for k in range(TPB):
                    sp.wait_ge(s["fin_done"], TPB * b + (k + 1))
                    lo = PAD if k == 0 else 0
                    sp.dma_start(out[bass.ds(b, 1), k * P + lo - PAD:(k + 1) * P - PAD, :]
                                 .rearrange("a t c -> (a t) c"),
                                 o_fin[lo:P, k, :]).then_inc(s[f"stored{k}"], 16)
            for k in range(TPB):
                sp.wait_ge(s[f"stored{k}"], 16 * B)

        @block.tensor
        def _(pe):
            def settle():
                pe.sem_inc(s["waits_passed"], 1)

            pe.wait_ge(s["ld_x"], 16 * (CTX + 1))
            for b in range(B):
                pe.matmul(bank[b][:, 0:T], tokW[:], win[0:KW, b, :], start=True, stop=True).then_inc(s["tok_mm"], 1)
            pe.wait_ge(s["relu_done"], 1)
            pe.wait_ge(s["p2_in"], 3)
            pe.matmul(bank[0][:, 0:P], ones[:], possq[:], start=True, stop=True).then_inc(s["p2_mm"], 1)
            pe.wait_ge(s["ld_id"], 16)
            pe.wait_ge(s["p2_done"], 1)
            for b in range(B):
                pe.wait_ge(s["hn_done"], b + 1)
                for i in range(TPB):
                    mm = pe.transpose(bank[b][:, i * P:(i + 1) * P], hT[:, b, i * P:(i + 1) * P], ident[:])
                mm.then_inc(s["hT_mm"], 1)
            for b in range(B):
                pe.wait_ge(s["h_copied"], b + 1)
                pe.wait_ge(s["yn_done"], TPB * (b + 1))
                for i in range(TPB):
                    mm = pe.transpose(bank[b][:, i * P:(i + 1) * P], yn[:, b, i, :], ident[:])
                mm.then_inc(s["y_mm"], 1)
            pe.wait_ge(s["ld_attn"], 16 * 5)
            pe.wait_ge(s["yl_done"], B)
            for k in range(2 * PAIRS):
                pe.wait_ge(s["y_evac"], k + 1)
                pe.matmul(bank[k][:], wqk[:, k * P:(k + 1) * P], ylT, start=True, stop=True).then_inc(s["qk_mm"], 1)
            pe.wait_ge(s["qk_evac"], 2 * PAIRS)
            for b in range(B):
                for hd in range(HEADS):
                    r, p = half(hd), hd // 2
                    mm = pe.matmul(bank[b][r, p * M:(p + 1) * M], qlT[r, p, b * M:(b + 1) * M],
                                   klT[r, p, b * M:(b + 1) * M], start=True, stop=True)
                mm.then_inc(s["sim2_mm"], 1)
            for b in range(B):
                pe.wait_ge(s["xa_done"], b + 1)
                for hd in range(HEADS):
                    r, p = half(hd), hd // 2
                    mm = pe.matmul(bank[b][r, p * M:(p + 1) * M], xa[r, b, p * M:(p + 1) * M],
                                   ident[r, r], start=True, stop=True)
                mm.then_inc(s["xaT_mm"], 1)
            for k in range(2 * HEADS):
                hd = k % HEADS
                r, p = half(hd), hd // 2
                pe.wait_ge(s["xaT_evac"], k + 1 if k < B else B)
                if k >= 8:
                    pe.wait_ge(s["fold_evac"], k - 7)
                src, w0 = (klT, 0) if k < HEADS else (qlT, PAIRS)
                pe.matmul(bank[k % 8][:], wqkT[r, w0 + p, :], src[r, p, :], start=True, stop=True)\
                    .then_inc(s["fold_mm"], 1)

            def pair_products(b, left, right):
                for p in range(PAIRS):
                    mm = pe.matmul(bank[b][:, p * P:(p + 1) * P], left[:, b, p, :], right(p), start=True, stop=True)
                return mm

            def twice(x):
                return x[:, None, :].to_broadcast([P, 2, M])

            def polynomial(n):
                for b in range(B):
                    pe.wait_ge(s["S_done"], n * B + (b + 1))
                    pe.wait_ge(s["T1_done"], n * B + (b + 1))
                    pair_products(b, Sb, lambda p: twice(Tm[:, b, p * M:(p + 1) * M])).then_inc(s["T2_mm"], 1)
                for b in range(B):
                    pe.wait_ge(s["T2_done"], n * B + (b + 1))
                    pair_products(b, Sb, lambda p: twice(Tm[:, b, p * M:(p + 1) * M])).then_inc(s["P_mm"], 1)

            def pinv(j, last):
                for b in range(B):
                    pe.wait_ge(s["zb_done"], j * B + (b + 1))
                    pair_products(b, Pb, lambda p: twice(xaT[:, b, p * M:(p + 1) * M])).then_inc(s["S_mm"], 1)
                polynomial(2 * j)
                for b in range(B):
                    pe.wait_ge(s["P_done"], 2 * j * B + (b + 1))
                    pair_products(b, Pb, lambda p: SZ[:, b, p].rearrange("p x m -> p (x m)")).then_inc(s["S_mm"], 1)
                polynomial(2 * j + 1)
                for b in range(B):
                    pe.wait_ge(s["P_done"], (2 * j + 1) * B + (b + 1))
                    pair_products(b, Pb, lambda p: twice(SZ[:, b, p, 1, :])).then_inc(s["z_mm"], 1)
                if not last:
                    for b in range(B):
                        pe.wait_ge(s["zt_done"], j * B + (b + 1))
                        pe.wait_ge(s["zt_odd"], j * B + (b + 1))
                        for p in range(PAIRS):
                            t = pe.transpose(bank[b][:, p * P:(p + 1) * P], Sb[:, b, p, :], ident[:])
                        t.then_inc(s["zb_mm"], 1)
            pe.wait_ge(s["fold_evac"], 2 * HEADS)
            pe.wait_ge(s["z0_done"], 1)
            pe.wait_ge(s["const_done"], 2)
            pinv_rounds(pe, pinv)
            pe.wait_ge(s["z_done"], B)

            def attend(b, par):
                pe.wait_ge(s["staged"], b + 1)
                for i in range(TPB):
                    need(pe, "a1T_evac", TPB * b + (i + 1 - TPB))
                    pe.matmul(bank[i][:], yTb[:, par, i * P:(i + 1) * P], Ab[:, par, :],
                              start=True, stop=True).then_inc(s["sim1_mm"], 1)
                need(pe, "conv_evac", PAIRS * b)
                need(pe, "uT_evac", 2 * b)
                need(pe, "uw_evac", b)
                for i in range(TPB):
                    pe.matmul(bank[3 + i][:], yTb[:, par, i * P:(i + 1) * P], wv, start=True, stop=True)\
                        .then_inc(s["v_mm"], 1)
                need(pe, "gw_evac", b)
                need(pe, "h1_done", b)
                for p in range(PAIRS):
                    if p >= 2:
                        pe.wait_ge(s["e3_exp"], PAIRS * b + (p - 1))
                    pe.matmul(bank[6 + p % 2][:, 0:NP], Bb[:, par, p * P:(p + 1) * P], yTb[:, par, :],
                              start=True, stop=True).then_inc(s["sim3_mm"], 1)
                for p in range(PAIRS):
                    if p == 3:
                        pe.wait_ge(s["conv_evac"], PAIRS * b + 1)
                    for hd in (2 * p, 2 * p + 1):
                        for i in range(TPB):
                            if p == 0:
                                pe.wait_ge(s["v_evac"], TPB * b + TPB)
                            t0, t1, tc = reach[i]
                            mm = pe.matmul(bank[3 + p % 3][half(hd), t0:t1], vb[:, i, hd * DH:(hd + 1) * DH],
                                           toe[:, hd, t0 - tc:t1 - tc], start=(i == 0), stop=(i == TPB - 1),
                                           skip_group_check=True)
                    mm.then_inc(s["conv_mm"], 1)
                for p in range(PAIRS):
                    if p < 2:
                        pe.wait_ge(s["e3_exp"], PAIRS * b + (p + 3))
                    else:
                        pe.wait_ge(s["e3T_evac"], PAIRS * b + (p - 1))
                    for i in range(TPB):
                        mm = pe.transpose(bank[6 + p % 2][:, i * P:(i + 1) * P], e3[:, p, i * P:(i + 1) * P], ident[:])
                    mm.then_inc(s["e3T_mm"], 1)
                pe.wait_ge(s["conv_evac"], PAIRS * b + 2)
                pe.wait_ge(s["e3T_evac"], PAIRS * b + PAIRS)
                for p in range(PAIRS):
                    for i in range(TPB):
                        mm = pe.matmul(bank[4][:, p * P:(p + 1) * P], vb[:, i, p * P:(p + 1) * P],
                                       e3T[:, i, p, :], start=(i == 0), stop=(i == TPB - 1))
                mm.then_inc(s["uT_mm"], 1)

                def a1_transposed(i):
                    pe.wait_ge(s["a1_norm"], TPB * b + (i + 1))
                    for p in range(PAIRS):
                        t = pe.transpose(bank[i][:, p * P:(p + 1) * P],
                                         e1[:, i, 2 * p:2 * p + 2, :].rearrange("p a m -> p (a m)"), ident[:])
                    t.then_inc(s["a1T_mm"], 1)
                a1_transposed(0)
                pe.wait_ge(s["uT_evac"], 2 * b + 2)
                pe.wait_ge(s["conv_evac"], PAIRS * b + 3)
                settle()
                for hd in range(HEADS):
                    r, p = half(hd), hd // 2
                    mm = pe.matmul(bank[5][r, p * P:(p + 1) * P], uTb[r, p, :], wo[r, p, :], start=True, stop=True)
                mm.then_inc(s["uw_mm"], 1)
                a1_transposed(1)
                pe.wait_ge(s["uw_evac"], b + 1)
                settle()
                for hd in range(HEADS):
                    r, p = half(hd), hd // 2
                    mm = pe.matmul(bank[6][r, p * P:(p + 1) * P], ztb[r, par, p * M:(p + 1) * M], uw[r, p, :],
                                   start=True, stop=True)
                mm.then_inc(s["gw_mm"], 1)
                a1_transposed(2)
                pe.wait_ge(s["conv_evac"], PAIRS * b + PAIRS)
                pe.wait_ge(s["gw_evac"], b + 1)
                pe.wait_ge(s["a1T_evac"], TPB * b + TPB)
                for i in range(TPB):
                    for p in range(PAIRS):
                        pe.matmul(bank[7][:, i * P:(i + 1) * P], resT[:, p, i * P:(i + 1) * P], wo[:, p, :],
                                  start=(p == 0), stop=False)
                    for p in range(PAIRS):
                        mm = pe.matmul(bank[7][:, i * P:(i + 1) * P], a1T[:, p, i * P:(i + 1) * P], gw[:, p, :],
                                       start=False, stop=(p == PAIRS - 1))
                mm.then_inc(s["out1_mm"], 1)

            def two(it):
                for par in range(2):
                    attend(2 * it + par, par)
            rounds(pe, B // 2, two)

            pe.wait_ge(s["h1_done"], B)
            for b in range(B):
                pe.wait_ge(s["u_done"], b + 1)
                need(pe, "uT_done", b - 1)
                for i in range(TPB):
                    mm = pe.transpose(bank[b % 2][:, i * P:(i + 1) * P], usc[:, b % 2, i, :], ident[:])
                mm.then_inc(s["u_mm"], 1)
                pe.wait_ge(s["uT_done"], b + 1)
                need(pe, "d2_step", 2 * (b - 1))
                for i in range(TPB):
                    mm = pe.matmul(bank[2 + b % 2][:, i * P:(i + 1) * P], uT[:, TPB * b + i, :], posT2[:],
                                   start=True, stop=True)
                mm.then_inc(s["d_mm"], 1)
            pe.wait_ge(s["d2_step"], 2 * B)

            def tile_products(it, k):
                tau = TPB * it + k
                first = isinstance(it, int) and k == 0
                pe.wait_ge(s["xhi_done"], tau + 1)
                pe.wait_ge(s["xlo_done"], tau + 1)
                for c in range(CHUNKS):
                    d = c // 2
                    if isinstance(it, int) and k == 0:
                        pe.wait_ge(s["vlo_done"], c + 1)
                    if c % 2 == 0:
                        need(pe, "acc_step", DCH * tau + (d - 2))
                    else:
                        need(pe, "zact_done", DCH * tau + (d - 2))
                    bk = bank[(2 * k + c) % YBANKS]
                    n = slice(GRP * c, GRP * c + GRP)
                    pe.matmul(bk[:], xhi[:, k, :], v_hi[:, n, :], start=True, stop=False)
                    pe.matmul(bk[:], xhi[:, k, :], v_lo[:, n, :], start=False, stop=False)
                    pe.matmul(bk[:], xlo[:, k, :], v_hi[:, n, :], start=False, stop=True).then_inc(s["y_done_f"], 1)
                    if c == 12 and not first:
                        turn_out(tau - 1, (k - 1) % TPB)
                    if c == 18 and not first:
                        project_out(tau - 1)

            def turn_out(tau, k):
                pe.wait_ge(s["o_sum_done"], tau + 1)
                need(pe, "oT_evac", tau)
                pe.transpose(bank[6][:, 0:P], o_sum[:, k, :], ident[:]).then_inc(s["oT_mm"], 1)

            def project_out(tau):
                pe.wait_ge(s["oT_evac"], tau + 1)
                need(pe, "fin_done", tau)
                pe.matmul(bank[7][:, 0:P], oT[:], outWT[:], start=True, stop=True).then_inc(s["o_mm"], 1)

            def three(it):
                for k in range(TPB):
                    tile_products(it, k)
            rounds(pe, B, three)
            turn_out(TILES - 1, TPB - 1)
            project_out(TILES - 1)

        @block.scalar
        def _(act):
            act.wait_ge(s["ld_vec"], 16 * 4)
            for b in range(B):
                act.wait_ge(s["tok_mm"], b + 1)
                act.activation(hT[:, b, PAD:NP], bank[b][:, 0:T], ACT.Relu, bias=vec[:, 0:1]).then_inc(s["relu_done"], 1)
            act.wait_ge(s["bn_step"], B + 2)
            act.activation(bnr[:, 1:2], bnr[:, 0:1], ACT.Sqrt).then_inc(s["bn_root"], 1)
            for b in range(B):
                act.wait_ge(s["hT_mm"], b + 1)
                act.activation(h[:, TPB * b:TPB * (b + 1), :].rearrange("p i c -> p (i c)"), bank[b][:, 0:NP],
                               ACT.Copy).then_inc(s["h_copied"], 1)
            act.wait_ge(s["ln_step"], 1)
            act.activation(sq[:], tsm[:], ACT.Sqrt).then_inc(s["ln_root"], 1)
            act.wait_ge(s["ln_step"], 5)
            act.activation(sq[:], tsm[:], ACT.Sqrt).then_inc(s["ln_root"], 1)
            for b in range(B):
                act.wait_ge(s["y_mm"], b + 1)
                act.activation(yT[:, b, PAD:NP], bank[b][:, PAD:NP], ACT.Identity, bias=vec[:, 2:3],
                               scale=vec[:, 1:2]).then_inc(s["y_evac"], 1)
            for k in range(2 * PAIRS):
                act.wait_ge(s["qk_mm"], k + 1)
                dst, scale = (qlT[:, k, :], SCALE / L) if k < PAIRS else (klT[:, k - PAIRS, :], 1.0 / L)
                act.activation(dst, bank[k][:], ACT.Copy, scale=scale).then_inc(s["qk_evac"], 1)
            for b in range(B):
                act.wait_ge(s["sm2_step"], 2 * (b + 1))
                act.activation(xa[:, b, :], xa[:, b, :], ACT.Exp).then_inc(s["xa_exp"], 1)
            for b in range(B):
                act.wait_ge(s["xaT_mm"], b + 1)
                act.activation(xaT[:, b, :], bank[b][:, 0:PM], ACT.Copy).then_inc(s["xaT_evac"], 1)
            for k in range(2 * HEADS):
                act.wait_ge(s["fold_mm"], k + 1)
                dst, scale = (Aq, SCALE) if k < HEADS else (Bk, 1.0)
                act.activation(dst[:, :, k % HEADS, :], bank[k % 8][:].rearrange("p (b m) -> p b m", m=M),
                               ACT.Copy, scale=scale).then_inc(s["fold_evac"], 1)

            act.wait_ge(s["cmax_step"], 6)
            for b in range(B):
                ins = act.activation(SZ[:, b, :, 1, :], xa[:, b, :].rearrange("p (a m) -> p a m", m=M), ACT.Copy,
                                     scale=crc[:, 1:2])
            ins.then_inc(s["z0_done"], 1)

            def in_pairs(b):
                return bank[b][:].rearrange("p (a x m) -> p a x m", x=2, m=M)

            def even_heads(b):
                act.activation(Sb[half(0), b, :, 0:M], in_pairs(b)[half(0), :, 0, :], ACT.Copy)

            def pinv(j, last):
                for b in range(B):
                    act.wait_ge(s["S_mm"], 2 * j * B + (b + 1))
                    even_heads(b)
                    act.activation(SZ[:, b, :, 0, :], in_pairs(b)[:, :, 0, :], ACT.Copy).then_inc(s["S_done"], 1)
                for b in range(B):
                    act.wait_ge(s["S_mm"], (2 * j + 1) * B + (b + 1))
                    even_heads(b)
                    act.activation(SZ[:, b], in_pairs(b), ACT.Copy).then_inc(s["S_done"], 1)
                for b in range(B):
                    act.wait_ge(s["z_mm"], j * B + (b + 1))
                    if last:
                        act.activation(by_pair(ztt[:, b, :]), in_pairs(b)[:, :, 1, :], ACT.Copy)\
                            .then_inc(s["z_done"], 1)
                    else:
                        even_heads(b)
                        act.activation(SZ[:, b, :, 1, :], in_pairs(b)[:, :, 1, :], ACT.Copy).then_inc(s["zt_done"], 1)
                if not last:
                    for b in range(B):
                        act.wait_ge(s["zb_mm"], j * B + (b + 1))
                        act.activation(Pb[:, b].rearrange("p a m -> p (a m)"), bank[b][:], ACT.Copy)\
                            .then_inc(s["zb_done"], 1)
            pinv_rounds(act, pinv)

            def attend(b, par):
                for i in range(TPB):
                    act.wait_ge(s["v_mm"], TPB * b + (i + 1))
                    act.activation(vb[:, i, :], bank[3 + i][:], ACT.Copy).then_inc(s["v_evac"], 1)
                for i in range(TPB):
                    act.wait_ge(s["s1_sub"], 2 * TPB * b + (2 * i + 2))
                    act.activation(e1[:, i], e1[:, i], ACT.Exp).then_inc(s["e1_exp"], 1)
                for p in range(PAIRS):
                    act.wait_ge(s["e3_max"], PAIRS * b + (p + 1))
                    act.activation(e3[:, p, :], bank[6 + p % 2][:, 0:NP], ACT.Exp, bias=m3[:, p:p + 1],
                                   accum_out=s3[:, p:p + 1]).then_inc(s["e3_exp"], 1)
                for p in range(PAIRS):
                    act.wait_ge(s["conv_mm"], PAIRS * b + (p + 1))
                    act.activation(resT[:, p, :], bank[3 + p % 3][:, 0:NP], ACT.Copy).then_inc(s["conv_evac"], 1)
                for i in range(TPB):
                    if i == 2:
                        act.wait_ge(s["gw_mm"], b + 1)
                        act.activation(gw.rearrange("p a c -> p (a c)"), bank[6][:], ACT.Copy).then_inc(s["gw_evac"], 1)
                    act.wait_ge(s["a1T_mm"], TPB * b + (i + 1))
                    act.activation(a1T[:, :, i * P:(i + 1) * P], bank[i][:].rearrange("p (a t) -> p a t", t=P),
                                   ACT.Copy).then_inc(s["a1T_evac"], 1)

            def two(it):
                for par in range(2):
                    attend(2 * it + par, par)
            rounds(act, B // 2, two)

            act.wait_ge(s["f_stat"], 1)
            act.activation(sq[:], tsm[:], ACT.Sqrt).then_inc(s["f_root"], 1)
            act.wait_ge(s["h1_done"], B)
            for b in range(B):
                act.wait_ge(s["u_done"], b + 1)
                for i in range(TPB):
                    t = TPB * b + i
                    act.activation(junk[:, i, :], usc[:, b % 2, i, :], ACT.Square,
                                   accum_out=u2[:, t:t + 1]).then_inc(s["u2_done"], 1)
                    act.wait_ge(s["u2_done"], t + 1)
                act.wait_ge(s["u_mm"], b + 1)
                act.activation(uT[:, TPB * b:TPB * (b + 1), :].rearrange("p i c -> p (i c)"), bank[b % 2][:, 0:NP],
                               ACT.Copy).then_inc(s["uT_done"], 1)
            for b in range(B):
                act.wait_ge(s["d2_step"], 2 * (b + 1))
                blk = at_all[:, TPB * b:TPB * (b + 1), :]
                act.activation(blk, blk, ACT.Sqrt).then_inc(s["d_root"], 1)
            for b in range(B):
                act.wait_ge(s["f_step"], 5 * (b + 1))
                blk = at_all[:, TPB * b:TPB * (b + 1), :]
                act.activation(blk, blk, ACT.Exp).then_inc(s["f_exp"], 1)

            act.wait_ge(s["ld_v"], 16 * 8)
            act.wait_ge(s["a_done"], B)
            act.wait_ge(s["pad_tile"], 1)

            def stage(tau, k):
                act.activation(xhi[:, k, :], uT[:, bass.ds(tau, 1), :].rearrange("p a c -> p (a c)"), ACT.Copy)\
                    .then_inc(s["xhi_done"], 1)
            stage(0, 0)
            for c in range(CHUNKS):
                n = slice(GRP * c, GRP * c + GRP)
                act.activation(v_hi[:, n, :], v_raw[:, n, :], ACT.Copy).then_inc(s["vhi_done"], 1)

            def weigh(it, k):
                tau = TPB * it + k
                act.wait_ge(s["ast_done"], tau + 1)
                for m in range(DCH):
                    c = 2 * m + 1
                    act.wait_ge(s["y_done_f"], CHUNKS * tau + (c + 1))
                    need(act, "accp_step", (DCH - 1) * tau + (max(m - ZR, 1) if m >= ZR else m + 1 - ZR))
                    for j in range(GRP):
                        n = GRP * c + j
                        ins = act.activation(zring[:, m % ZR, j * P:(j + 1) * P],
                                             bank[(2 * k + c) % YBANKS][:, j * P:(j + 1) * P], ACT.Copy,
                                             scale=a_st[:, k, n:n + 1])
                    ins.then_inc(s["zact_done"], 1)
                    if m == 7 and not (isinstance(it, int) and k == 0):
                        turn_out(tau - 1)
                    if m == 10:
                        need(act, "y_done_f", CHUNKS * (tau - 1))
                        stage(tau + 1, (k + 1) % TPB)

            def turn_out(tau):
                act.wait_ge(s["oT_mm"], tau + 1)
                need(act, "o_mm", tau)
                act.activation(oT[:], bank[6][:, 0:P], ACT.Copy).then_inc(s["oT_evac"], 1)

            def three(it):
                for k in range(TPB):
                    weigh(it, k)
            rounds(act, B, three)
            turn_out(TILES - 1)

        @block.gpsimd
        def _(pool):
            pool.memset(hT[:, :, 0:PAD], 0.0).then_inc(s["const_done"], 1)
            pool.memset(yT[:, :, 0:PAD], 0.0).then_inc(s["pads_zero"], 1)
            pool.memset(ones[:], 1.0).then_inc(s["p2_in"], 1)
            pool.wait_ge(s["ld_vec"], 16 * 4)
            for b in range(B):
                pool.wait_ge(s["yn_done"], TPB * (b + 1))
                blk = slice(TPB * b, TPB * (b + 1))
                pool.tensor_tensor(h[:, blk, :], h[:, blk, :], xin[:, blk, :], ALU.add).then_inc(s["h_plus"], 1)
                pool.wait_ge(s["h_plus"], 2 * b + 1)
                pool.tensor_tensor(h[:, blk, :], h[:, blk, :], bout[:, None, :].to_broadcast([P, TPB, P]), ALU.add)\
                    .then_inc(s["h_plus"], 1)
            pool.wait_ge(s["cmax_step"], 4)
            pool.partition_all_reduce(cmxa[:], cmx[:], P, RMAX).then_inc(s["cmax_all"], 1)
            pool.wait_ge(s["qk_mm"], 2 * PAIRS)
            pool.wait_ge(s["cmax_all"], 1)
            for x in range(2):
                ins = pool.memset(Pb[half(x), :, :, (1 - x) * M:(2 - x) * M], 0.0)
            pool.wait_ge(s["fold_mm"], 2 * HEADS)
            for x in range(2):
                ins = pool.memset(Sb[half(x), :, :, (1 - x) * M:(2 - x) * M], 0.0)
            for j, value in enumerate((7.0, 15.0, 3.25)):
                for r in (half(0), half(1)):
                    ins = pool.tensor_scalar(eyes[r, j, :], ident[r, r], value, None, ALU.mult)
            ins.then_inc(s["const_done"], 1)

            def stage(b, par):
                need(pool, "out1_mm", b - 1)
                one = bass.ds(b, 1)
                pool.tensor_copy(yTb[:, par:par + 1, :], yT[:, one, :])
                pool.tensor_copy(Ab[:, par:par + 1, :], Aq[:, one].rearrange("p a h m -> p a (h m)"))
                pool.tensor_copy(Bb[:, par:par + 1, :], Bk[:, one].rearrange("p a h m -> p a (h m)"))
                pool.tensor_copy(ztb[:, par:par + 1, :], ztt[:, one, :]).then_inc(s["staged"], 1)

            def attend(b, par):
                stage(b, par)
                for i in range(TPB):
                    pool.wait_ge(s["s1_norm"], 2 * TPB * b + (2 * i + 2))
                    pool.tensor_tensor(e1[:, i], e1[:, i], rr1[:, i, :, None].to_broadcast([P, HEADS, M]), ALU.mult)\
                        .then_inc(s["a1_norm"], 1)

            def two(it):
                for par in range(2):
                    attend(2 * it + par, par)
            pool.wait_ge(s["z_done"], B)
            rounds(pool, B // 2, two)

            pool.wait_ge(s["out1_mm"], B)
            pool.wait_ge(s["h1_done"], B)
            pool.memset(uT[:, TILES, :], 0.0)
            pool.memset(at_all[:, TILES, :], 0.0).then_inc(s["pad_tile"], 1)
            pool.wait_ge(s["pad_tile"], 1)

            def stage_a(tau, k):
                pool.tensor_copy(a_st[:, k, :], at_all[:, bass.ds(tau, 1), :].rearrange("p a c -> p (a c)"))\
                    .then_inc(s["ast_done"], 1)

            def add_up(it, k):
                tau = TPB * it + k
                part = acc[:, k, 8:12, :].rearrange("p j c -> p (j c)")
                need(pool, "o_sum_done", tau - 2)
                for m in range(1, DCH):
                    pool.wait_ge(s["zact_done"], DCH * tau + (m + 1))
                    if m == 1:
                        ins = pool.tensor_tensor(part, zring[:, 0, :], zring[:, 1, :], ALU.add)
                    else:
                        pool.wait_ge(s["accp_step"], (DCH - 1) * tau + (m - 1))
                        ins = pool.tensor_tensor(part, part, zring[:, m % ZR, :], ALU.add)
                    ins.then_inc(s["accp_step"], 1)
                    if m == 8:
                        need(pool, "acc_step", DCH * (tau - 1))
                        need(pool, "zact_done", DCH * (tau - 1))
                        stage_a(tau + 1, (k + 1) % TPB)
            pool.wait_ge(s["a_done"], B)
            stage_a(0, 0)

            def three(it):
                for k in range(TPB):
                    add_up(it, k)
            rounds(pool, B, three)

        @block.vector
        def _(dve):
            dve.wait_ge(s["ld_ffn"], 16 * 4)
            dve.tensor_scalar(posT2[:], posT[:], -2.0, None, ALU.mult).then_inc(s["p2_in"], 1)
            dve.tensor_tensor(possq[:], posT[:], posT[:], ALU.mult).then_inc(s["p2_in"], 1)
            dve.wait_ge(s["const_done"], 1)
            bn = linker(dve, "bn_step")
            for b in range(B):
                dve.wait_ge(s["relu_done"], b + 1)
                dve.bn_stats(bnst[:, b, :], hT[:, b, PAD:NP]).then_inc(s["bn_step"], 1)
            dve.wait_ge(s["bn_step"], B)
            dve.bn_aggr(bnmv[:], bnst[:].rearrange("p b k -> p (b k)")).then_inc(s["bn_step"], 1)
            dve.wait_ge(s["bn_step"], B + 1)
            dve.tensor_scalar(bnr[:, 0:1], bnmv[:, 1:2], EPS, None, ALU.add).then_inc(s["bn_step"], 1)
            dve.wait_ge(s["p2_mm"], 1)
            dve.tensor_copy(p2row[:], bank[0][:, 0:P]).then_inc(s["p2_done"], 1)
            dve.wait_ge(s["bn_root"], 1)
            dve.reciprocal(bnr[:, 0:1], bnr[:, 1:2]).then_inc(s["bn_step"], 1)
            dve.wait_ge(s["bn_step"], B + 3)
            for b in range(B):
                dve.tensor_scalar(hT[:, b, PAD:NP], hT[:, b, PAD:NP], bnmv[:, 0:1], bnr[:, 0:1],
                                  ALU.subtract, ALU.mult).then_inc(s["hn_done"], 1)
            for b in range(B):
                dve.wait_ge(s["h_copied"], b + 1)
                for i in range(TPB):
                    t = TPB * b + i
                    ins = dve.bn_stats(st6[:, t, :], h[:, t, :])
            ins.then_inc(s["xin_done"], 1)
            dve.wait_ge(s["xin_done"], 1)
            for t in range(TILES):
                ins = dve.bn_aggr(mv[:, t, :], st6[:, t, :])
            ins.then_inc(s["xin_done"], 1)
            dve.wait_ge(s["xin_done"], 2)
            ln = linker(dve, "ln_step")
            ln(dve.tensor_scalar(tsm[:], mv[:, :, 1], EPS, None, ALU.add))
            dve.wait_ge(s["ln_root"], 1)
            ln(dve.reciprocal(r0[:], sq[:]))
            ln(dve.tensor_tensor(tsm[:], r0[:], r0[:], ALU.mult))
            ln(dve.tensor_tensor(tsm[:], tsm[:], mv[:, :, 1], ALU.mult))
            ln(dve.tensor_scalar(tsm[:], tsm[:], EPS, None, ALU.add))
            dve.wait_ge(s["ln_root"], 2)
            ln(dve.reciprocal(r1[:], sq[:]))
            for b in range(B):
                for i in range(TPB):
                    t = TPB * b + i
                    ins = dve.tensor_scalar(xin[:, t, :], h[:, t, :], mv[:, t, 0:1], r0[:, t:t + 1],
                                            ALU.subtract, ALU.mult)
                ins.then_inc(s["xin_done"], 1)
            dve.wait_ge(s["hT_mm"], B)
            for b in range(B):
                dve.wait_ge(s["xin_done"], b + 3)
                for i in range(TPB):
                    t = TPB * b + i
                    dve.tensor_scalar(yn[:, b, i, :], xin[:, t, :], r1[:, t:t + 1], None, ALU.mult)\
                        .then_inc(s["yn_done"], 1)
            dve.wait_ge(s["pads_zero"], 1)
            for b in range(B):
                dve.wait_ge(s["y_evac"], b + 1)
                dve.tensor_reduce(ylT[:, b * M:(b + 1) * M], yT[:, b, :].rearrange("p (m l) -> p m l", l=L),
                                  AX_X, ALU.add).then_inc(s["yl_done"], 1)
            sm = linker(dve, "sm2_step")
            for b in range(B):
                dve.wait_ge(s["sim2_mm"], b + 1)
                sims = bank[b][:, 0:PM].rearrange("p (a m) -> p a m", m=M)
                blk = xa[:, b, :].rearrange("p (a m) -> p a m", m=M)
                sm(dve.tensor_reduce(rsx[:, 0, b * PAIRS:(b + 1) * PAIRS], sims, AX_X, ALU.max))
                sm(dve.tensor_tensor(blk, sims, rsx[:, 0, b * PAIRS:(b + 1) * PAIRS, None].to_broadcast([P, PAIRS, M]),
                                     ALU.subtract))
            for b in range(B):
                dve.wait_ge(s["xa_exp"], b + 1)
                blk = xa[:, b, :].rearrange("p (a m) -> p a m", m=M)
                tot = rsx[:, 1, b * PAIRS:(b + 1) * PAIRS]
                sm(dve.tensor_reduce(tot, blk, AX_X, ALU.add))
                sm(dve.reciprocal(tot, tot))
                dve.tensor_tensor(blk, blk, tot[:, :, None].to_broadcast([P, PAIRS, M]), ALU.mult)\
                    .then_inc(s["xa_done"], 1)
            dve.wait_ge(s["xa_done"], B)
            cm = linker(dve, "cmax_step")
            cm(dve.tensor_reduce(rsx[:, 0, :], xa.rearrange("p b (a m) -> p (b a) m", m=M), AX_X, ALU.add))
            dve.wait_ge(s["xaT_evac"], B)
            cm(dve.tensor_reduce(rsx[:, 1, :], xaT.rearrange("p b (a m) -> p (b a) m", m=M), AX_X, ALU.add))
            cm(dve.tensor_reduce(cmx[:], rsx[:], AX_X, ALU.max))
            cm(dve.tensor_copy(crc[:], cmx[:]))
            dve.wait_ge(s["cmax_all"], 1)
            cm(dve.tensor_tensor(crc[:, 0:1], cmxa[:, 0:1], cmxa[:, 1:2], ALU.mult))
            cm(dve.reciprocal(crc[:, 1:2], crc[:, 0:1]))
            dve.wait_ge(s["cmax_step"], 6)
            for b in range(B):
                for x in range(2):
                    ins = dve.tensor_scalar(Pb[half(x), b, :, x * M:(x + 1) * M], by_pair(xaT[half(x), b, :]),
                                            crc[half(x), 1:2], None, ALU.mult)
                ins.then_inc(s["zb_done"], 1)

            def times_eye(j, r=slice(0, P)):
                return eyes[r, j, None, :].to_broadcast([r.stop - r.start, PAIRS, M])

            def first_of(b, r=slice(0, P)):
                return bank[b][r, :].rearrange("p (a m) -> p a m", m=P)[:, :, 0:M]

            def odd_heads(b, which):
                return dve.tensor_copy(Sb[half(1), b, :, M:P], SZ[half(1), b, :, which, :])

            def polynomial(n):
                for b in range(B):
                    dve.wait_ge(s["S_done"], n * B + (b + 1))
                    odd_heads(b, 0)
                    dve.tensor_tensor(by_pair(Tm[:, b, :]), times_eye(0), SZ[:, b, :, 0, :], ALU.subtract)\
                        .then_inc(s["T1_done"], 1)
                for b in range(B):
                    dve.wait_ge(s["T2_mm"], n * B + (b + 1))
                    dve.tensor_tensor(by_pair(Tm[:, b, :]), times_eye(1), first_of(b), ALU.subtract)\
                        .then_inc(s["T2_done"], 1)
                for b in range(B):
                    dve.wait_ge(s["P_mm"], n * B + (b + 1))
                    for x in range(2):
                        ins = dve.scalar_tensor_tensor(Pb[half(x), b, :, x * M:(x + 1) * M], first_of(b, half(x)),
                                                       -0.25, times_eye(2, half(x)), ALU.mult, ALU.add)
                    ins.then_inc(s["P_done"], 1)

            def pinv(j, last):
                polynomial(2 * j)
                polynomial(2 * j + 1)
                if not last:
                    for b in range(B):
                        dve.wait_ge(s["zt_done"], j * B + (b + 1))
                        odd_heads(b, 1).then_inc(s["zt_odd"], 1)
            dve.wait_ge(s["const_done"], 2)
            pinv_rounds(dve, pinv)

            def attend(b, par):
                for i in range(TPB):
                    sims = bank[i][:].rearrange("p (a m) -> p a m", m=M)
                    dve.wait_ge(s["sim1_mm"], TPB * b + (i + 1))
                    dve.tensor_reduce(m1[:, i, :], sims, AX_X, ALU.max).then_inc(s["s1_sub"], 1)
                    dve.wait_ge(s["s1_sub"], 2 * TPB * b + (2 * i + 1))
                    dve.tensor_tensor(e1[:, i], sims, m1[:, i, :, None].to_broadcast([P, HEADS, M]), ALU.subtract)\
                        .then_inc(s["s1_sub"], 1)
                for p in range(PAIRS):
                    dve.wait_ge(s["sim3_mm"], PAIRS * b + (p + 1))
                    dve.tensor_reduce(m3[:, p:p + 1], bank[6 + p % 2][:, 0:NP], AX_X, ALU.max, negate=True)\
                        .then_inc(s["e3_max"], 1)
                for i in range(TPB):
                    dve.wait_ge(s["e1_exp"], TPB * b + (i + 1))
                    dve.tensor_reduce(s1[:, i, :], e1[:, i], AX_X, ALU.add).then_inc(s["s1_norm"], 1)
                    dve.wait_ge(s["s1_norm"], 2 * TPB * b + (2 * i + 1))
                    dve.reciprocal(rr1[:, i, :], s1[:, i, :]).then_inc(s["s1_norm"], 1)
                dve.wait_ge(s["e3_exp"], PAIRS * b + PAIRS)
                dve.reciprocal(rr3, s3).then_inc(s["rr3_done"], 1)
                for p in range(PAIRS):
                    dve.wait_ge(s["e3T_mm"], PAIRS * b + (p + 1))
                    dve.tensor_copy(e3T[:, :, p, :], bank[6 + p % 2][:, 0:NP].rearrange("p (i m) -> p i m", m=P))\
                        .then_inc(s["e3T_evac"], 1)
                dve.wait_ge(s["uT_mm"], b + 1)
                for x in range(2):
                    dve.tensor_copy(uTb[half(x), :, :],
                                    bank[4][half(x), :].rearrange("p (a m) -> p a m", m=P)[:, :, x * M:(x + 1) * M])\
                        .then_inc(s["uT_evac"], 1)
                dve.wait_ge(s["uw_mm"], b + 1)
                dve.wait_ge(s["rr3_done"], b + 1)
                dve.tensor_tensor(uw, bank[5][:].rearrange("p (a c) -> p a c", c=P),
                                  rr3[:, :, None].to_broadcast([P, PAIRS, P]), ALU.mult).then_inc(s["uw_evac"], 1)
                dve.wait_ge(s["out1_mm"], b + 1)
                blk = h[:, bass.ds(TPB * b, TPB), :]
                dve.tensor_tensor(blk, blk, bank[7][:, 0:NP].rearrange("p (i c) -> p i c", c=P), ALU.add)\
                    .then_inc(s["h1_done"], 1)

            def two(it):
                for par in range(2):
                    attend(2 * it + par, par)
            dve.wait_ge(s["h_plus"], 2 * B)
            rounds(dve, B // 2, two)

            def squared_distance(b):
                for i in range(TPB):
                    t = TPB * b + i
                    dve.wait_ge(s["d_mm"], b + 1)
                    dve.wait_ge(s["u2_done"], t + 1)
                    ins = dve.scalar_tensor_tensor(at_all[:, t, :], bank[2 + b % 2][:, i * P:(i + 1) * P],
                                                   u2[:, t:t + 1], p2row[:], ALU.add, ALU.add)
                ins.then_inc(s["d2_step"], 1)
                dve.wait_ge(s["d2_step"], 2 * b + 1)
                blk = at_all[:, TPB * b:TPB * (b + 1), :]
                dve.tensor_scalar(blk, blk, 0.0, None, ALU.max).then_inc(s["d2_step"], 1)

            dve.wait_ge(s["h1_done"], B)
            for t in range(TILES):
                ins = dve.bn_stats(st6[:, t, :], h[:, t, :])
            fst = linker(dve, "fs_step")
            fst(ins)
            for t in range(TILES):
                ins = dve.bn_aggr(mv[:, t, :], st6[:, t, :])
            fst(ins)
            dve.tensor_scalar(tsm[:], mv[:, :, 1], EPS, None, ALU.add).then_inc(s["f_stat"], 1)
            dve.wait_ge(s["f_root"], 1)
            fst(dve.reciprocal(r0[:], sq[:]))
            for b in range(B):
                need(dve, "u_mm", b - 1)
                need(dve, "u2_done", TPB * (b - 1))
                for i in range(TPB):
                    t = TPB * b + i
                    ins = dve.tensor_scalar(usc[:, b % 2, i, :], h[:, t, :], mv[:, t, 0:1], r0[:, t:t + 1],
                                            ALU.subtract, ALU.mult)
                ins.then_inc(s["u_done"], 1)
                if b > 0:
                    squared_distance(b - 1)
            squared_distance(B - 1)
            f = linker(dve, "f_step")
            for b in range(B):
                blk = at_all[:, TPB * b:TPB * (b + 1), :]
                dve.wait_ge(s["d_root"], b + 1)
                f(dve.tensor_scalar(blk, blk, 0.1, None, ALU.add))
                f(dve.reciprocal(blk, blk))
                f(dve.tensor_tensor(blk, blk, scrow[:, None, :].to_broadcast([P, TPB, P]), ALU.mult))
                mx = mx24[:, TPB * b:TPB * (b + 1)]
                f(dve.tensor_reduce(mx, blk, AX_X, ALU.max))
                f(dve.tensor_tensor(blk, blk, mx[:, :, None].to_broadcast([P, TPB, P]), ALU.subtract))
            for b in range(B):
                blk = at_all[:, TPB * b:TPB * (b + 1), :]
                tot = mx24[:, TPB * b:TPB * (b + 1)]
                dve.wait_ge(s["f_exp"], b + 1)
                fst(dve.tensor_reduce(tot, blk, AX_X, ALU.add))
                fst(dve.reciprocal(tot, tot))
                dve.tensor_tensor(blk, blk, tot[:, :, None].to_broadcast([P, TPB, P]), ALU.mult)\
                    .then_inc(s["a_done"], 1)
            dve.tensor_tensor(h[:], h[:], outb[:, None, :].to_broadcast([P, TILES, P]), ALU.add)\
                .then_inc(s["hb_done"], 1)
            dve.wait_ge(s["hb_done"], 1)

            def stage(tau, k):
                dve.wait_ge(s["xhi_done"], tau + 1)
                dve.tensor_tensor(xlo[:, k, :], uT[:, bass.ds(tau, 1), :].rearrange("p a c -> p (a c)"),
                                  xhi[:, k, :].bitcast(F32), ALU.subtract).then_inc(s["xlo_done"], 1)
            dve.wait_ge(s["pad_tile"], 1)
            stage(0, 0)
            for c in range(CHUNKS):
                n = slice(GRP * c, GRP * c + GRP)
                dve.wait_ge(s["vhi_done"], c + 1)
                dve.tensor_tensor(v_lo[:, n, :], v_raw[:, n, :], v_hi[:, n, :].bitcast(F32), ALU.subtract)\
                    .then_inc(s["vlo_done"], 1)

            def weigh(it, k):
                tau = TPB * it + k
                first = isinstance(it, int) and k == 0
                dve.wait_ge(s["ast_done"], tau + 1)
                need(dve, "o_sum_done", tau - 2)
                for d in range(DCH):
                    c = 2 * d
                    dve.wait_ge(s["y_done_f"], CHUNKS * tau + (c + 1))
                    if d >= 2:
                        dve.wait_ge(s["acc_step"], DCH * tau + (d - 1))
                    for j in range(GRP):
                        y = bank[(2 * k + c) % YBANKS][:, j * P:(j + 1) * P]
                        to = acc[:, k, GRP * (d % 2) + j, :]
                        w = a_st[:, k, GRP * c + j:GRP * c + j + 1]
                        if d < 2:
                            ins = dve.tensor_scalar(to, y, w, None, ALU.mult)
                        else:
                            ins = dve.scalar_tensor_tensor(to, y, w, to, ALU.mult, ALU.add)
                    ins.then_inc(s["acc_step"], 1)
                    if d == 4 and not first:
                        sum_up(tau - 1, (k - 1) % TPB)
                    if d == 11 and not first:
                        finish(tau - 1, (k - 1) % TPB, it - 1 if k == 0 else it)
                    if d == 12:
                        need(dve, "y_done_f", CHUNKS * (tau - 1))
                        stage(tau + 1, (k + 1) % TPB)

            def sum_up(tau, k):
                dve.wait_ge(s["acc_step"], DCH * (tau + 1))
                dve.wait_ge(s["accp_step"], (DCH - 1) * (tau + 1))
                need(dve, "oT_mm", tau - 2)
                dve.tensor_reduce(o_sum[:, k, :], acc[:, k].rearrange("p j c -> p c j"), AX_X, ALU.add)\
                    .then_inc(s["o_sum_done"], 1)

            def finish(tau, k, it):
                dve.wait_ge(s["o_mm"], tau + 1)
                need(dve, f"stored{k}", 16 * it)
                dve.tensor_tensor(o_fin[:, k, :], bank[7][:, 0:P],
                                  h[:, bass.ds(tau, 1), :].rearrange("p a c -> p (a c)"), ALU.add)\
                    .then_inc(s["fin_done"], 1)

            def three(it):
                for k in range(TPB):
                    weigh(it, k)
            rounds(dve, B, three)
            sum_up(TILES - 1, TPB - 1)
            finish(TILES - 1, TPB - 1, B - 1)


def kernel(**inputs):
    import numpy as np
    import concourse.bacc as bacc
    from concourse.bass_utils import run_bass_kernel_spmd

    x = {n: np.asarray(a) for n, a in inputs.items()}
    w_qkv = x["L0_attn_w_qkv"]
    taps = x["L0_attn_w_res"].reshape(HEADS, TAPS)
    padded = np.zeros((HEADS, WPAD), np.float32)
    padded[:, P - 1:P - 1 + TAPS] = taps[:, ::-1]
    band = np.stack([padded[:, P - 1 - p:P - 1 - p + CW] for p in range(P)])
    arrays = {
        "xt": x["x"].transpose(2, 0, 1),
        "tok_wt": x["L0_tok_W"].T,
        "tok_b": x["L0_tok_b"].reshape(P, 1),
        "ln_g": x["L0_attn_ln_g"].reshape(P, 1),
        "ln_b": x["L0_attn_ln_b"].reshape(P, 1),
        "w_qkv": w_qkv,
        "w_qk_t": w_qkv[:, 0:2 * HM].T.reshape(2 * PAIRS, P, P).transpose(1, 0, 2),
        "w_out": x["L0_attn_w_out"],
        "b_out": x["L0_attn_b_out"],
        "w_res": band,
        "pos_t": x["L0_ffn_positions"].T,
        "scales": x["L0_ffn_scales"],
        "vw": x["L0_ffn_value_weight"],
        "out_wt": x["L0_ffn_out_W"].T,
        "out_b": x["L0_ffn_out_b"],
        "ident_in": np.eye(P, dtype=np.float32),
    }
    arrays = {n: np.ascontiguousarray(a) for n, a in arrays.items()}
    nc = bacc.Bacc("TRN2", target_bir_lowering=False, num_devices=1)
    args = {n: nc.dram_tensor(n, a.shape, F32, kind="ExternalInput").ap() for n, a in arrays.items()}
    args["out"] = nc.dram_tensor("out", (B, T, P), F32, kind="ExternalOutput").ap()
    audio_tower(nc, **args)
    r = run_bass_kernel_spmd(nc, [arrays], core_ids=[0])
    return r.results[0]["out"]
```

```python
from contextlib import ExitStack

import concourse.bass as bass
from concourse import mybir

F32 = mybir.dt.float32
F32R = mybir.dt.float32r
ALU = mybir.AluOpType
ACT = mybir.ActivationFunctionType
AX_X = mybir.AxisListType.X
RMAX = bass.bass_isa.ReduceOp.max

P = 128
B, T, CTX, DIN = 8, 371, 5, 23
KW = CTX * DIN
HEADS, DH, M = 8, 64, 64
PAIRS = HEADS // 2
HM = HEADS * M
PM = PAIRS * M
NP = 384
PAD = NP - T
L = NP // M
TPB = NP // P
TILES = B * TPB
TAPS = 33
HALF = TAPS // 2
CW = P + TAPS - 1
WPAD = P - 1 + TAPS + P - 1
ITERS = 6
EPS = 1e-5
GRP = 4
CHUNKS = P // GRP
YBANKS = 6
SIM3_BANK = (6, 7, 1, 2)
CONV_BANK = (3, 4, 5, 0)
SCALE = DH ** -0.5
ZR = 4
DCH = CHUNKS // 2


def audio_tower(nc, xt, tok_wt, tok_b, ln_g, ln_b, w_qkv, w_qk_t, w_out, b_out, w_res, pos_t,
                scales, vw, out_wt, out_b, ident_in, out):
    with ExitStack() as ctx:
        def sb(name, shape, dt=F32, at=ctx):
            return at.enter_context(nc.sbuf_tensor(name, shape, dt))

        def sem(name):
            return ctx.enter_context(nc.semaphore(name))

        bank = [ctx.enter_context(nc.psum_tensor(f"bank{i}", [P, 512], F32)) for i in range(8)]

        ident = sb("ident", [P, P])
        h = sb("h", [P, TILES, P])
        posT2 = sb("posT2", [P, P])
        p2row = sb("p2row", [P, P])
        scrow = sb("scrow", [P, P])
        outWT = sb("outWT", [P, P])
        outb = sb("outb", [P, P])
        bout = sb("bout", [P, P])
        vec = sb("vec", [P, 3])
        bnst = sb("bnst", [P, B, 6])
        bnmv = sb("bnmv", [P, 2])
        bnr = sb("bnr", [P, 2])
        cmx = sb("cmx", [P, 2])
        cmxa = sb("cmxa", [P, 2])
        crc = sb("crc", [P, 2])
        rsx = sb("rsx", [P, 2, B * PAIRS])
        uT = sb("uT", [P, TILES + 1, P])
        yT = uT[:, 0:TILES, :].rearrange("p (b i) t -> p b (i t)", b=B)
        at_all = sb("at_all", [P, TILES + 1, P])
        f_st6 = sb("f_st6", [P, TPB, 6])
        f_mv = sb("f_mv", [P, TPB, 2])
        f_var = sb("f_var", [P, TPB])
        f_sd = sb("f_sd", [P, TPB])
        f_r = sb("f_r", [P, TPB])
        u2 = sb("u2", [P, TPB])
        f_mx = sb("f_mx", [P, TPB])
        f_tot = sb("f_tot", [P, TPB])
        f_rt = sb("f_rt", [P, TPB])
        u_tok = sb("u_tok", [P, TPB, P])
        uTs = sb("uTs", [P, TPB, P])
        fa = sb("fa", [P, TPB, P])
        o_sum = u_tok
        oT = uTs[:, 0, :]
        o_fin = fa

        early = ExitStack()
        v_raw = sb("v_raw", [P, P, P], at=early)
        ARENA = 24930
        arena = sb("arena", [P, ARENA], at=early)
        early.close()
        v_lo = sb("v_lo", [P, P, P], F32R)
        v_hi = sb("v_hi", [P, P, P], F32R)
        zring = sb("zring", [P, ZR, GRP * P])
        xhi = sb("xhi", [P, TPB, P], F32R)
        xlo = sb("xlo", [P, TPB, P], F32R)
        a_st = sb("a_st", [P, TPB, P])
        acc = sb("acc", [P, TPB, 12, P])

        cursor = [0]

        def take(*dims):
            n = 1
            for d in dims:
                n *= d
            at = cursor[0]
            cursor[0] += n
            assert cursor[0] <= ARENA, cursor[0]
            v = arena[:, at:at + n]
            if len(dims) == 2:
                v = v.rearrange("p (a b) -> p a b", b=dims[1])
            elif len(dims) == 3:
                v = v.rearrange("p (a b c) -> p a b c", b=dims[1], c=dims[2])
            elif len(dims) == 4:
                v = v.rearrange("p (a b c d) -> p a b c d", b=dims[1], c=dims[2], d=dims[3])
            return v

        Aq = take(B, HEADS, M)
        Bk = take(B, HEADS, M)
        xaT = take(B, PM)
        ztt = xaT
        wv = take(HM)
        wo = take(PAIRS, P)
        toe = take(HEADS, CW)
        mark = cursor[0]
        spare = at_all[:].rearrange("p t n -> p (t n)")
        xa = spare[:, 0:B * PM].rearrange("p (b c) -> p b c", b=B)
        eyes = spare[:, B * PM:B * PM + 3 * M].rearrange("p (j m) -> p j m", m=M)
        klT = take(PAIRS, B * M)
        wqk = take(2 * HM)
        wqkT = take(2 * PAIRS, P)
        hT = take(B, NP)
        tokW = take(P)
        posT = take(P)
        possq = take(P)
        ones = take(P)
        st6 = take(TILES, 6)
        mv = take(TILES, 2)
        r0 = take(TILES)
        r1 = take(TILES)
        tsm = take(TILES)
        sq = take(TILES)
        cursor[0] = mark + 2 * B * PAIRS * P
        win = take(B, T)
        cursor[0] -= B * T
        xin = take(TILES, P)
        ylT = take(B * M)
        qlT = hT.rearrange("p b t -> p (b t)")[:, 0:PAIRS * B * M].rearrange("p (a m) -> p a m", m=B * M)
        yn = hT.rearrange("p b (i c) -> p b i c", c=P)
        cursor[0] = mark
        Tm = xa
        SZ = take(B, PAIRS, 2, M)
        Sb = take(B, PAIRS, P)
        Pb = take(B, PAIRS, P)
        cursor[0] = mark
        yTb = take(2, NP)
        Ab = take(2, HM)
        Bb = take(2, HM)
        ztb = take(2, PM)
        e1 = take(TPB, HEADS, M)
        e3 = take(PAIRS, NP)
        a1T = e3
        e3T = take(TPB, PAIRS, P)
        vb = take(TPB, HM)
        resT = take(PAIRS, NP)
        uTb = take(PAIRS, M)
        uw = take(PAIRS, P)
        gw = take(PAIRS, P)
        m1 = take(TPB, HEADS)
        s1 = take(TPB, HEADS)
        rr1 = take(TPB, HEADS)
        m3 = take(PAIRS)
        s3 = take(PAIRS)
        rr3 = take(PAIRS)

        def half(x):
            return slice(64 * (x % 2), 64 * (x % 2) + 64)

        s = {n: sem(n) for n in """ld_x ld_id ld_vec ld_attn ld_ffn ld_v
        tok_mm relu_done bn_step bn_root hn_done hT_mm h_copied ln_step ln_root
        xin_done yn_done h_plus y_mm y_evac pads_zero yl_done
        qk_mm qk_evac fold_mm fold_evac sim2_mm sm2_step xa_exp xa_done xaT_mm xaT_evac
        cmax_step cmax_all z0_done const_done
        S_mm S_done T1_done T2_mm T2_done P_mm P_done z_mm zt_done zt_odd zb_mm zb_done z_done
        staged sim1_mm v_mm sim3_mm conv_mm e3T_mm uT_mm a1T_mm uw_mm gw_mm out1_mm
        s1_sub s1_norm e1_exp e3_max e3_exp v_evac conv_evac e3T_evac e3T_evac_v uT_evac rr3_done a1_norm a1T_evac
        uw_evac gw_evac h1_done
        p2_in p2_mm p2_done waits_passed
        f_step f_var_done f_root u_done u2_done u_mm uTs_done uT_done d_mm d2_done d_root f_inv f_scaled f_max f_exp
        f_sum a_done hb_done
        vhi_done vlo_done vlop_done xhi_done xlo_done ast_done pad_tile y_done_f acc_step zact_done accp_step
        o_sum_done oT_mm oT_evac o_mm fin_done stored0 stored1 stored2""".split()}

        def need(eng, name, value):
            if not isinstance(value, int) or value > 0:
                eng.wait_ge(s[name], value)

        def settle(eng):
            eng.sem_inc(s["waits_passed"], 1)

        def linker(eng, name):
            count = [0]

            def link(ins):
                count[0] += 1
                ins.then_inc(s[name], 1)
                eng.wait_ge(s[name], count[0])
            return link

        def batch_pairs(eng, body):
            def two(it):
                for par in range(2):
                    body(2 * it + par, par)
            two(0)
            with eng.Fori(1, B // 2 - 1) as it:
                two(it)
            two(B // 2 - 1)

        def has_before(b):
            return not isinstance(b, int) or b > 0

        def has_after(b):
            return not isinstance(b, int) or b < B - 1

        def rounds(eng, n, body):
            body(0)
            with eng.Fori(1, n) as i:
                body(i)

        def pinv_rounds(eng, body):
            with eng.Fori(0, ITERS // 2 - 1) as j:
                body(j, False)
            body(ITERS // 2 - 1, True)

        def by_pair(x):
            return x.rearrange("p (a m) -> p a m", m=M)

        def pool_takes(c):
            return c % 3 == 2

        def low_part_wait(eng, c):
            if pool_takes(c):
                eng.wait_ge(s["vlop_done"], (c + 1) // 3)
            else:
                eng.wait_ge(s["vlo_done"], c + 1 - (c + 1) // 3)

        reach = [(max(0, P * i - HALF), min(NP, P * i + P + HALF), P * i - HALF) for i in range(TPB)]

        block = ctx.enter_context(nc.Block())

        @block.sync
        def _(sp):
            for i in range(CTX):
                sp.dma_start(win[i * DIN:(i + 1) * DIN], xt[:, :, i:i + T]).then_inc(s["ld_x"], 16)
            sp.dma_start(tokW[0:KW], tok_wt).then_inc(s["ld_x"], 16)
            sp.dma_start(vec[:, 0:1], tok_b).then_inc(s["ld_vec"], 16)
            sp.dma_start(ident[:], ident_in).then_inc(s["ld_id"], 16)
            sp.dma_start(vec[:, 1:2], ln_g).then_inc(s["ld_vec"], 16)
            sp.dma_start(vec[:, 2:3], ln_b).then_inc(s["ld_vec"], 16)
            sp.dma_start(bout[:], b_out.partition_broadcast(P)).then_inc(s["ld_vec"], 16)
            sp.dma_start(posT, pos_t).then_inc(s["ld_ffn"], 16)
            sp.dma_start(outWT[:], out_wt).then_inc(s["ld_ffn"], 16)
            sp.dma_start(scrow[:], scales.partition_broadcast(P)).then_inc(s["ld_ffn"], 16)
            sp.dma_start(outb[:], out_b.partition_broadcast(P)).then_inc(s["ld_ffn"], 16)
            sp.dma_start(wqk, w_qkv[:, 0:2 * HM]).then_inc(s["ld_attn"], 16)
            sp.dma_start(wqkT, w_qk_t).then_inc(s["ld_attn"], 16)
            sp.dma_start(wv, w_qkv[:, 2 * HM:3 * HM]).then_inc(s["ld_attn"], 16)
            sp.dma_start(wo, w_out.rearrange("(a p) n -> p a n", p=P)).then_inc(s["ld_attn"], 16)
            sp.dma_start(toe, w_res).then_inc(s["ld_attn"], 16)
            for k in range(8):
                n = P // 8
                sp.dma_start(v_raw[:, k * n:(k + 1) * n, :],
                             vw[k * n:(k + 1) * n].rearrange("n d e -> d n e")).then_inc(s["ld_v"], 16)
            with sp.Fori(0, B) as b:
                for k in range(TPB):
                    sp.wait_ge(s["fin_done"], TPB * b + (k + 1))
                    lo = PAD if k == 0 else 0
                    sp.dma_start(out[bass.ds(b, 1), k * P + lo - PAD:(k + 1) * P - PAD, :]
                                 .rearrange("a t c -> (a t) c"),
                                 o_fin[lo:P, k, :]).then_inc(s[f"stored{k}"], 16)
            for k in range(TPB):
                sp.wait_ge(s[f"stored{k}"], 16 * B)

        @block.tensor
        def _(pe):
            pe.wait_ge(s["ld_x"], 16 * (CTX + 1))
            for b in range(B):
                pe.matmul(bank[b][:, 0:T], tokW[0:KW], win[0:KW, b, :], start=True, stop=True).then_inc(s["tok_mm"], 1)
            pe.wait_ge(s["relu_done"], 1)
            pe.wait_ge(s["p2_in"], 3)
            pe.matmul(bank[0][:, 0:P], ones, possq, start=True, stop=True).then_inc(s["p2_mm"], 1)
            pe.wait_ge(s["ld_id"], 16)
            pe.wait_ge(s["p2_done"], 1)
            for b in range(B):
                pe.wait_ge(s["hn_done"], b + 1)
                for i in range(TPB):
                    mm = pe.transpose(bank[b][:, i * P:(i + 1) * P], hT[:, b, i * P:(i + 1) * P], ident[:])
                mm.then_inc(s["hT_mm"], 1)
            for b in range(B):
                pe.wait_ge(s["h_copied"], b + 1)
                pe.wait_ge(s["yn_done"], TPB * (b + 1))
                for i in range(TPB):
                    mm = pe.transpose(bank[b][:, i * P:(i + 1) * P], yn[:, b, i, :], ident[:])
                mm.then_inc(s["y_mm"], 1)
            pe.wait_ge(s["ld_attn"], 16 * 5)
            pe.wait_ge(s["yl_done"], B)
            for k in range(2 * PAIRS):
                pe.wait_ge(s["y_evac"], k + 1)
                pe.matmul(bank[k][:], wqk[:, k * P:(k + 1) * P], ylT, start=True, stop=True).then_inc(s["qk_mm"], 1)
            pe.wait_ge(s["qk_evac"], 2 * PAIRS)
            for b in range(B):
                for hd in range(HEADS):
                    r, p = half(hd), hd // 2
                    mm = pe.matmul(bank[b][r, p * M:(p + 1) * M], qlT[r, p, b * M:(b + 1) * M],
                                   klT[r, p, b * M:(b + 1) * M], start=True, stop=True)
                mm.then_inc(s["sim2_mm"], 1)
            for b in range(B):
                pe.wait_ge(s["xa_done"], b + 1)
                for hd in range(HEADS):
                    r, p = half(hd), hd // 2
                    mm = pe.matmul(bank[b][r, p * M:(p + 1) * M], xa[r, b, p * M:(p + 1) * M],
                                   ident[r, r], start=True, stop=True)
                mm.then_inc(s["xaT_mm"], 1)
            for k in range(2 * HEADS):
                hd = k % HEADS
                r, p = half(hd), hd // 2
                pe.wait_ge(s["xaT_evac"], k + 1 if k < B else B)
                if k >= 8:
                    pe.wait_ge(s["fold_evac"], k - 7)
                src, w0 = (klT, 0) if k < HEADS else (qlT, PAIRS)
                pe.matmul(bank[k % 8][:], wqkT[r, w0 + p, :], src[r, p, :], start=True, stop=True)\
                    .then_inc(s["fold_mm"], 1)

            def pair_products(b, left, right):
                for p in range(PAIRS):
                    mm = pe.matmul(bank[b][:, p * P:(p + 1) * P], left[:, b, p, :], right(p), start=True, stop=True)
                return mm

            def twice(x):
                return x[:, None, :].to_broadcast([P, 2, M])

            def polynomial(n):
                for b in range(B):
                    pe.wait_ge(s["S_done"], n * B + (b + 1))
                    pe.wait_ge(s["T1_done"], n * B + (b + 1))
                    pair_products(b, Sb, lambda p: twice(Tm[:, b, p * M:(p + 1) * M])).then_inc(s["T2_mm"], 1)
                for b in range(B):
                    pe.wait_ge(s["T2_done"], n * B + (b + 1))
                    pair_products(b, Sb, lambda p: twice(Tm[:, b, p * M:(p + 1) * M])).then_inc(s["P_mm"], 1)

            def pinv(j, last):
                for b in range(B):
                    pe.wait_ge(s["zb_done"], j * B + (b + 1))
                    pair_products(b, Pb, lambda p: twice(xaT[:, b, p * M:(p + 1) * M])).then_inc(s["S_mm"], 1)
                polynomial(2 * j)
                for b in range(B):
                    pe.wait_ge(s["P_done"], 2 * j * B + (b + 1))
                    pair_products(b, Pb, lambda p: SZ[:, b, p].rearrange("p x m -> p (x m)")).then_inc(s["S_mm"], 1)
                polynomial(2 * j + 1)
                for b in range(B):
                    pe.wait_ge(s["P_done"], (2 * j + 1) * B + (b + 1))
                    pair_products(b, Pb, lambda p: twice(SZ[:, b, p, 1, :])).then_inc(s["z_mm"], 1)
                if not last:
                    for b in range(B):
                        pe.wait_ge(s["zt_done"], j * B + (b + 1))
                        pe.wait_ge(s["zt_odd"], j * B + (b + 1))
                        for p in range(PAIRS):
                            t = pe.transpose(bank[b][:, p * P:(p + 1) * P], Sb[:, b, p, :], ident[:])
                        t.then_inc(s["zb_mm"], 1)
            pe.wait_ge(s["fold_evac"], 2 * HEADS)
            pe.wait_ge(s["z0_done"], 1)
            pe.wait_ge(s["const_done"], 2)
            pinv_rounds(pe, pinv)
            pe.wait_ge(s["z_done"], B)

            def ffn_transposes(c):
                pe.wait_ge(s["u_done"], c + 1)
                for i in range(TPB):
                    t = pe.transpose(bank[0][:, i * P:(i + 1) * P], u_tok[:, i, :], ident[:])
                t.then_inc(s["u_mm"], 1)

            def ffn_distances(c):
                pe.wait_ge(s["uTs_done"], c + 1)
                for i in range(TPB):
                    mm = pe.matmul(bank[0][:, i * P:(i + 1) * P], uTs[:, i, :], posT2[:], start=True, stop=True)
                mm.then_inc(s["d_mm"], 1)

            def attend(b, par):
                pe.wait_ge(s["staged"], b + 1)
                for i in range(TPB):
                    need(pe, "a1T_evac", TPB * b + (i + 1 - TPB))
                    pe.matmul(bank[i][:], yTb[:, par, i * P:(i + 1) * P], Ab[:, par, :],
                              start=True, stop=True).then_inc(s["sim1_mm"], 1)
                need(pe, "uw_evac", b)
                need(pe, "uT_evac", 2 * b)
                for i in range(TPB):
                    if i == TPB - 1:
                        need(pe, "h1_done", b)
                    pe.matmul(bank[3 + i][:], yTb[:, par, i * P:(i + 1) * P], wv, start=True, stop=True)\
                        .then_inc(s["v_mm"], 1)
                need(pe, "gw_evac", b)
                def sim3(p):
                    if p == 2:
                        pe.wait_ge(s["s1_sub"], 2 * TPB * b + 4)
                    if p == 3:
                        pe.wait_ge(s["s1_sub"], 2 * TPB * b + 6)
                    pe.matmul(bank[SIM3_BANK[p]][:, 0:NP], Bb[:, par, p * P:(p + 1) * P], yTb[:, par, :],
                              start=True, stop=True).then_inc(s["sim3_mm"], 1)

                def convolve(p):
                    if p == 3 and has_before(b):
                        pe.wait_ge(s["d2_done"], b)
                    for hd in (2 * p, 2 * p + 1):
                        for i in range(TPB):
                            t0, t1, tc = reach[i]
                            mm = pe.matmul(bank[CONV_BANK[p]][half(hd), t0:t1], vb[:, i, hd * DH:(hd + 1) * DH],
                                           toe[:, hd, t0 - tc:t1 - tc], start=(i == 0), stop=(i == TPB - 1),
                                           skip_group_check=True)
                    mm.then_inc(s["conv_mm"], 1)

                def e3_transposed(p):
                    for i in range(TPB):
                        t = pe.transpose(bank[6 + p % 2][:, i * P:(i + 1) * P], e3[:, p, i * P:(i + 1) * P], ident[:])
                    t.then_inc(s["e3T_mm"], 1)

                def a1_transposed(i):
                    pe.wait_ge(s["a1_norm"], TPB * b + (i + 1))
                    for p in range(PAIRS):
                        t = pe.transpose(bank[i][:, p * P:(p + 1) * P],
                                         e1[:, i, 2 * p:2 * p + 2, :].rearrange("p a m -> p (a m)"), ident[:])
                    t.then_inc(s["a1T_mm"], 1)

                def project_convolved(steps):
                    for n in steps:
                        i, p = n // PAIRS, n % PAIRS
                        pe.matmul(bank[5][:, i * P:(i + 1) * P], resT[:, p, i * P:(i + 1) * P], wo[:, p, :],
                                  start=(n == 0), stop=False, skip_group_check=True)

                sim3(0)
                if has_before(b):
                    pe.wait_ge(s["s1_sub"], 2 * TPB * b + 2)
                    ffn_transposes(b - 1)
                sim3(1)
                if has_before(b):
                    ffn_distances(b - 1)
                sim3(2)
                sim3(3)
                pe.wait_ge(s["v_evac"], TPB * b + TPB)
                for p in range(PAIRS):
                    convolve(p)
                pe.wait_ge(s["e3_exp"], PAIRS * b + 2)
                e3_transposed(0)
                e3_transposed(1)
                pe.wait_ge(s["conv_evac"], PAIRS * b + PAIRS)
                project_convolved(range(0, 3))
                for p in (2, 3):
                    pe.wait_ge(s["e3_exp"], PAIRS * b + (p + 1))
                    pe.wait_ge(s["e3T_evac_v"], 2 * b + (p - 1))
                    e3_transposed(p)
                project_convolved(range(3, 6))
                pe.wait_ge(s["e3T_evac"], 2 * b + 2)
                for p in range(PAIRS):
                    for i in range(TPB):
                        mm = pe.matmul(bank[4][:, p * P:(p + 1) * P], vb[:, i, p * P:(p + 1) * P],
                                       e3T[:, i, p, :], start=(i == 0), stop=(i == TPB - 1))
                mm.then_inc(s["uT_mm"], 1)
                a1_transposed(0)
                a1_transposed(1)
                pe.wait_ge(s["uT_evac"], 2 * b + 2)
                settle(pe)
                for hd in range(HEADS):
                    r, p = half(hd), hd // 2
                    mm = pe.matmul(bank[3][r, p * P:(p + 1) * P], uTb[r, p, :], wo[r, p, :], start=True, stop=True)
                mm.then_inc(s["uw_mm"], 1)
                a1_transposed(2)
                project_convolved(range(6, 9))
                pe.wait_ge(s["uw_evac"], b + 1)
                settle(pe)
                for hd in range(HEADS):
                    r, p = half(hd), hd // 2
                    mm = pe.matmul(bank[6][r, p * P:(p + 1) * P], ztb[r, par, p * M:(p + 1) * M], uw[r, p, :],
                                   start=True, stop=True)
                mm.then_inc(s["gw_mm"], 1)
                project_convolved(range(9, 12))
                pe.wait_ge(s["gw_evac"], b + 1)
                for i in range(TPB):
                    pe.wait_ge(s["a1T_evac"], TPB * b + (i + 1))
                    for p in range(PAIRS):
                        mm = pe.matmul(bank[5][:, i * P:(i + 1) * P], a1T[:, p, i * P:(i + 1) * P], gw[:, p, :],
                                       start=False, stop=(i == TPB - 1 and p == PAIRS - 1), skip_group_check=True)
                mm.then_inc(s["out1_mm"], 1)

            batch_pairs(pe, attend)
            pe.wait_ge(s["a1T_evac"], TPB * B)
            ffn_transposes(B - 1)
            ffn_distances(B - 1)
            pe.wait_ge(s["d2_done"], B)

            def tile_products(it, k):
                tau = TPB * it + k
                first = isinstance(it, int) and k == 0
                pe.wait_ge(s["xhi_done"], tau + 1)
                pe.wait_ge(s["xlo_done"], tau + 1)
                for c in range(CHUNKS):
                    d = c // 2
                    if first:
                        low_part_wait(pe, c)
                    if c % 2 == 0:
                        need(pe, "acc_step", DCH * tau + (d - 2))
                    else:
                        need(pe, "zact_done", DCH * tau + (d - 2))
                    bk = bank[(2 * k + c) % YBANKS]
                    n = slice(GRP * c, GRP * c + GRP)
                    pe.matmul(bk[:], xhi[:, k, :], v_hi[:, n, :], start=True, stop=False)
                    pe.matmul(bk[:], xhi[:, k, :], v_lo[:, n, :], start=False, stop=False)
                    pe.matmul(bk[:], xlo[:, k, :], v_hi[:, n, :], start=False, stop=True).then_inc(s["y_done_f"], 1)
                    if c == 12 and not first:
                        turn_out(tau - 1, (k - 1) % TPB)
                    if c == 18 and not first:
                        project_out(tau - 1)

            def turn_out(tau, k):
                pe.wait_ge(s["o_sum_done"], tau + 1)
                need(pe, "oT_evac", tau)
                pe.transpose(bank[6][:, 0:P], o_sum[:, k, :], ident[:]).then_inc(s["oT_mm"], 1)

            def project_out(tau):
                pe.wait_ge(s["oT_evac"], tau + 1)
                need(pe, "fin_done", tau)
                pe.matmul(bank[7][:, 0:P], oT, outWT[:], start=True, stop=True).then_inc(s["o_mm"], 1)

            def three(it):
                for k in range(TPB):
                    tile_products(it, k)
            rounds(pe, B, three)
            turn_out(TILES - 1, TPB - 1)
            project_out(TILES - 1)

        @block.scalar
        def _(act):
            act.wait_ge(s["ld_vec"], 16 * 4)
            for b in range(B):
                act.wait_ge(s["tok_mm"], b + 1)
                act.activation(hT[:, b, PAD:NP], bank[b][:, 0:T], ACT.Relu, bias=vec[:, 0:1]).then_inc(s["relu_done"], 1)
            act.wait_ge(s["bn_step"], B + 2)
            act.activation(bnr[:, 1:2], bnr[:, 0:1], ACT.Sqrt).then_inc(s["bn_root"], 1)
            for b in range(B):
                act.wait_ge(s["hT_mm"], b + 1)
                act.activation(h[:, TPB * b:TPB * (b + 1), :].rearrange("p i c -> p (i c)"), bank[b][:, 0:NP],
                               ACT.Copy).then_inc(s["h_copied"], 1)
            act.wait_ge(s["ln_step"], 1)
            act.activation(sq, tsm, ACT.Sqrt).then_inc(s["ln_root"], 1)
            act.wait_ge(s["ln_step"], 5)
            act.activation(sq, tsm, ACT.Sqrt).then_inc(s["ln_root"], 1)
            for b in range(B):
                act.wait_ge(s["y_mm"], b + 1)
                act.activation(yT[:, b, PAD:NP], bank[b][:, PAD:NP], ACT.Identity, bias=vec[:, 2:3],
                               scale=vec[:, 1:2]).then_inc(s["y_evac"], 1)
            for k in range(2 * PAIRS):
                act.wait_ge(s["qk_mm"], k + 1)
                dst, scale = (qlT[:, k, :], SCALE / L) if k < PAIRS else (klT[:, k - PAIRS, :], 1.0 / L)
                act.activation(dst, bank[k][:], ACT.Copy, scale=scale).then_inc(s["qk_evac"], 1)
            for b in range(B):
                act.wait_ge(s["sm2_step"], 2 * (b + 1))
                act.activation(xa[:, b, :], xa[:, b, :], ACT.Exp).then_inc(s["xa_exp"], 1)
            for b in range(B):
                act.wait_ge(s["xaT_mm"], b + 1)
                act.activation(xaT[:, b, :], bank[b][:, 0:PM], ACT.Copy).then_inc(s["xaT_evac"], 1)
            for k in range(2 * HEADS):
                act.wait_ge(s["fold_mm"], k + 1)
                dst, scale = (Aq, SCALE) if k < HEADS else (Bk, 1.0)
                act.activation(dst[:, :, k % HEADS, :], bank[k % 8][:].rearrange("p (b m) -> p b m", m=M),
                               ACT.Copy, scale=scale).then_inc(s["fold_evac"], 1)

            act.wait_ge(s["cmax_step"], 6)
            for b in range(B):
                ins = act.activation(SZ[:, b, :, 1, :], xa[:, b, :].rearrange("p (a m) -> p a m", m=M), ACT.Copy,
                                     scale=crc[:, 1:2])
            ins.then_inc(s["z0_done"], 1)

            def in_pairs(b):
                return bank[b][:].rearrange("p (a x m) -> p a x m", x=2, m=M)

            def even_heads(b):
                act.activation(Sb[half(0), b, :, 0:M], in_pairs(b)[half(0), :, 0, :], ACT.Copy)

            def pinv(j, last):
                for b in range(B):
                    act.wait_ge(s["S_mm"], 2 * j * B + (b + 1))
                    even_heads(b)
                    act.activation(SZ[:, b, :, 0, :], in_pairs(b)[:, :, 0, :], ACT.Copy).then_inc(s["S_done"], 1)
                for b in range(B):
                    act.wait_ge(s["S_mm"], (2 * j + 1) * B + (b + 1))
                    even_heads(b)
                    act.activation(SZ[:, b], in_pairs(b), ACT.Copy).then_inc(s["S_done"], 1)
                for b in range(B):
                    act.wait_ge(s["z_mm"], j * B + (b + 1))
                    if last:
                        act.activation(by_pair(ztt[:, b, :]), in_pairs(b)[:, :, 1, :], ACT.Copy)\
                            .then_inc(s["z_done"], 1)
                    else:
                        even_heads(b)
                        act.activation(SZ[:, b, :, 1, :], in_pairs(b)[:, :, 1, :], ACT.Copy).then_inc(s["zt_done"], 1)
                if not last:
                    for b in range(B):
                        act.wait_ge(s["zb_mm"], j * B + (b + 1))
                        act.activation(Pb[:, b].rearrange("p a m -> p (a m)"), bank[b][:], ACT.Copy)\
                            .then_inc(s["zb_done"], 1)
            pinv_rounds(act, pinv)

            def ffn_root(c):
                act.wait_ge(s["f_var_done"], c + 1)
                act.activation(f_sd[:], f_var[:], ACT.Sqrt).then_inc(s["f_root"], 1)

            def ffn_squares(c):
                act.wait_ge(s["u_done"], c + 1)
                need(act, "a_done", c)
                for i in range(TPB):
                    ins = act.activation(fa[:, i, :], u_tok[:, i, :], ACT.Square, accum_out=u2[:, i:i + 1])
                ins.then_inc(s["u2_done"], 1)

            def ffn_transposed(c):
                act.wait_ge(s["u_mm"], c + 1)
                need(act, "uT_done", c)
                act.activation(uTs[:].rearrange("p i c -> p (i c)"), bank[0][:, 0:NP], ACT.Copy)\
                    .then_inc(s["uTs_done"], 1)

            def ffn_distance_root(c):
                act.wait_ge(s["d2_done"], c + 1)
                act.activation(fa[:], fa[:], ACT.Sqrt).then_inc(s["d_root"], 1)

            def ffn_exp(c):
                act.wait_ge(s["f_max"], c + 1)
                for i in range(TPB):
                    ins = act.activation(fa[:, i, :], fa[:, i, :], ACT.Exp, bias=f_mx[:, i:i + 1],
                                         accum_out=f_tot[:, i:i + 1])
                ins.then_inc(s["f_exp"], 1)

            def attend(b, par):
                def values(i):
                    act.wait_ge(s["v_mm"], TPB * b + (i + 1))
                    act.activation(vb[:, i, :], bank[3 + i][:], ACT.Copy).then_inc(s["v_evac"], 1)

                def convolved(p):
                    act.wait_ge(s["conv_mm"], PAIRS * b + (p + 1))
                    act.activation(resT[:, p, :], bank[CONV_BANK[p]][:, 0:NP], ACT.Copy).then_inc(s["conv_evac"], 1)

                def e3_exponentials(p):
                    act.wait_ge(s["e3_max"], PAIRS * b + (p + 1))
                    act.activation(e3[:, p, :], bank[SIM3_BANK[p]][:, 0:NP], ACT.Exp, bias=m3[:, p:p + 1],
                                   accum_out=s3[:, p:p + 1]).then_inc(s["e3_exp"], 1)

                def e1_exponentials(i):
                    act.wait_ge(s["s1_sub"], 2 * TPB * b + (2 * i + 2))
                    act.activation(e1[:, i], e1[:, i], ACT.Exp).then_inc(s["e1_exp"], 1)

                def e3_evacuated(p):
                    act.wait_ge(s["e3T_mm"], PAIRS * b + (p + 1))
                    act.activation(e3T[:, :, p, :], bank[6 + p % 2][:, 0:NP].rearrange("p (i m) -> p i m", m=P),
                                   ACT.Copy).then_inc(s["e3T_evac"], 1)

                def a1_evacuated(i):
                    act.wait_ge(s["a1T_mm"], TPB * b + (i + 1))
                    act.activation(a1T[:, :, i * P:(i + 1) * P], bank[i][:].rearrange("p (a t) -> p a t", t=P),
                                   ACT.Copy).then_inc(s["a1T_evac"], 1)

                if has_before(b):
                    ffn_root(b - 1)
                values(0)
                values(1)
                if has_before(b):
                    ffn_squares(b - 1)
                    ffn_transposed(b - 1)
                values(2)
                if has_before(b):
                    ffn_distance_root(b - 1)
                e3_exponentials(0)
                convolved(0)
                e3_exponentials(1)
                for p in (1, 2, 3):
                    convolved(p)
                e3_exponentials(2)
                e3_exponentials(3)
                e1_exponentials(0)
                e3_evacuated(2)
                e3_evacuated(3)
                e1_exponentials(1)
                e1_exponentials(2)
                for i in range(TPB):
                    a1_evacuated(i)
                act.wait_ge(s["gw_mm"], b + 1)
                act.activation(gw.rearrange("p a c -> p (a c)"), bank[6][:], ACT.Copy).then_inc(s["gw_evac"], 1)
                if has_before(b):
                    ffn_exp(b - 1)

            batch_pairs(act, attend)

            act.wait_ge(s["ld_v"], 16 * 8)
            act.wait_ge(s["out1_mm"], B)

            def high_part(chunks):
                for c in chunks:
                    n = slice(GRP * c, GRP * c + GRP)
                    act.activation(v_hi[:, n, :], v_raw[:, n, :], ACT.Copy).then_inc(s["vhi_done"], 1)
            high_part(range(0, 3))
            ffn_root(B - 1)
            high_part(range(3, 5))
            ffn_squares(B - 1)
            ffn_transposed(B - 1)
            high_part(range(5, 7))
            ffn_distance_root(B - 1)
            high_part(range(7, 16))
            ffn_exp(B - 1)

            def stage(tau, k):
                act.activation(xhi[:, k, :], uT[:, bass.ds(tau, 1), :].rearrange("p a c -> p (a c)"), ACT.Copy)\
                    .then_inc(s["xhi_done"], 1)
            act.wait_ge(s["uT_done"], B)
            act.wait_ge(s["pad_tile"], 1)
            stage(0, 0)
            high_part(range(16, CHUNKS))

            def weigh(it, k):
                tau = TPB * it + k
                act.wait_ge(s["ast_done"], tau + 1)
                for m in range(DCH):
                    c = 2 * m + 1
                    act.wait_ge(s["y_done_f"], CHUNKS * tau + (c + 1))
                    need(act, "accp_step", (DCH - 1) * tau + (max(m - ZR, 1) if m >= ZR else m + 1 - ZR))
                    for j in range(GRP):
                        n = GRP * c + j
                        ins = act.activation(zring[:, m % ZR, j * P:(j + 1) * P],
                                             bank[(2 * k + c) % YBANKS][:, j * P:(j + 1) * P], ACT.Copy,
                                             scale=a_st[:, k, n:n + 1])
                    ins.then_inc(s["zact_done"], 1)
                    if m == 7 and not (isinstance(it, int) and k == 0):
                        turn_out(tau - 1)
                    if m == 10:
                        need(act, "y_done_f", CHUNKS * (tau - 1))
                        stage(tau + 1, (k + 1) % TPB)

            def turn_out(tau):
                act.wait_ge(s["oT_mm"], tau + 1)
                need(act, "o_mm", tau)
                act.activation(oT, bank[6][:, 0:P], ACT.Copy).then_inc(s["oT_evac"], 1)

            def three(it):
                for k in range(TPB):
                    weigh(it, k)
            rounds(act, B, three)
            turn_out(TILES - 1)

        @block.gpsimd
        def _(pool):
            pool.memset(hT[:, :, 0:PAD], 0.0).then_inc(s["const_done"], 1)
            pool.memset(yT[:, :, 0:PAD], 0.0).then_inc(s["pads_zero"], 1)
            pool.memset(ones, 1.0).then_inc(s["p2_in"], 1)
            pool.wait_ge(s["ld_vec"], 16 * 4)
            for b in range(B):
                pool.wait_ge(s["yn_done"], TPB * (b + 1))
                blk = slice(TPB * b, TPB * (b + 1))
                pool.tensor_tensor(h[:, blk, :], h[:, blk, :], xin[:, blk, :], ALU.add).then_inc(s["h_plus"], 1)
                pool.wait_ge(s["h_plus"], 2 * b + 1)
                pool.tensor_tensor(h[:, blk, :], h[:, blk, :], bout[:, None, :].to_broadcast([P, TPB, P]), ALU.add)\
                    .then_inc(s["h_plus"], 1)
            pool.wait_ge(s["cmax_step"], 4)
            pool.partition_all_reduce(cmxa[:], cmx[:], P, RMAX).then_inc(s["cmax_all"], 1)
            pool.wait_ge(s["qk_mm"], 2 * PAIRS)
            pool.wait_ge(s["cmax_all"], 1)
            for x in range(2):
                ins = pool.memset(Pb[half(x), :, :, (1 - x) * M:(2 - x) * M], 0.0)
            pool.wait_ge(s["fold_mm"], 2 * HEADS)
            for x in range(2):
                ins = pool.memset(Sb[half(x), :, :, (1 - x) * M:(2 - x) * M], 0.0)
            for j, value in enumerate((7.0, 15.0, 3.25)):
                for r in (half(0), half(1)):
                    ins = pool.tensor_scalar(eyes[r, j, :], ident[r, r], value, None, ALU.mult)
            ins.then_inc(s["const_done"], 1)

            def stage(b, par):
                one = bass.ds(b, 1)
                pool.tensor_copy(yTb[:, par:par + 1, :], yT[:, one, :])
                pool.tensor_copy(Ab[:, par:par + 1, :], Aq[:, one].rearrange("p a h m -> p a (h m)"))
                pool.tensor_copy(Bb[:, par:par + 1, :], Bk[:, one].rearrange("p a h m -> p a (h m)"))
                pool.tensor_copy(ztb[:, par:par + 1, :], ztt[:, one, :]).then_inc(s["staged"], 1)

            def tiles_of(x, c):
                return x[:, bass.ds(TPB * c, TPB), :]

            def ffn_keep(c):
                pool.wait_ge(s["uTs_done"], c + 1)
                pool.tensor_copy(tiles_of(uT, c), uTs[:]).then_inc(s["uT_done"], 1)

            def ffn_bias(c):
                pool.tensor_tensor(tiles_of(h, c), tiles_of(h, c), outb[:, None, :].to_broadcast([P, TPB, P]),
                                   ALU.add).then_inc(s["hb_done"], 1)

            def ffn_scale(c):
                pool.wait_ge(s["f_inv"], c + 1)
                pool.tensor_tensor(fa[:], fa[:], scrow[:, None, :].to_broadcast([P, TPB, P]), ALU.mult)\
                    .then_inc(s["f_scaled"], 1)

            def ffn_normalise(c):
                pool.wait_ge(s["f_sum"], c + 1)
                pool.tensor_tensor(tiles_of(at_all, c), fa[:], f_rt[:, :, None].to_broadcast([P, TPB, P]), ALU.mult)\
                    .then_inc(s["a_done"], 1)

            def attend(b, par):
                if has_after(b):
                    need(pool, "out1_mm", b)
                    stage(b + 1, 1 - par)
                if has_before(b):
                    ffn_keep(b - 1)
                for i in range(TPB):
                    pool.wait_ge(s["s1_norm"], 2 * TPB * b + (2 * i + 2))
                    pool.tensor_tensor(e1[:, i], e1[:, i], rr1[:, i, :, None].to_broadcast([P, HEADS, M]), ALU.mult)\
                        .then_inc(s["a1_norm"], 1)
                if has_before(b):
                    ffn_scale(b - 1)
                    ffn_bias(b - 1)
                    ffn_normalise(b - 1)

            pool.wait_ge(s["z_done"], B)
            stage(0, 0)
            batch_pairs(pool, attend)
            pool.memset(uT[:, TILES, :], 0.0)
            pool.memset(at_all[:, TILES, :], 0.0).then_inc(s["pad_tile"], 1)

            def low_part(chunks):
                for c in chunks:
                    if pool_takes(c):
                        n = slice(GRP * c, GRP * c + GRP)
                        pool.wait_ge(s["vhi_done"], c + 1)
                        pool.tensor_tensor(v_lo[:, n, :], v_raw[:, n, :], v_hi[:, n, :].bitcast(F32), ALU.subtract)\
                            .then_inc(s["vlop_done"], 1)
            low_part(range(0, 6))
            ffn_keep(B - 1)
            ffn_bias(B - 1)
            low_part(range(6, 15))
            ffn_scale(B - 1)
            low_part(range(15, 18))
            ffn_normalise(B - 1)

            def stage_a(tau, k):
                pool.tensor_copy(a_st[:, k, :], at_all[:, bass.ds(tau, 1), :].rearrange("p a c -> p (a c)"))\
                    .then_inc(s["ast_done"], 1)

            def add_up(it, k):
                tau = TPB * it + k
                part = acc[:, k, 8:12, :].rearrange("p j c -> p (j c)")
                need(pool, "o_sum_done", tau - 2)
                for m in range(1, DCH):
                    pool.wait_ge(s["zact_done"], DCH * tau + (m + 1))
                    if m == 1:
                        ins = pool.tensor_tensor(part, zring[:, 0, :], zring[:, 1, :], ALU.add)
                    else:
                        pool.wait_ge(s["accp_step"], (DCH - 1) * tau + (m - 1))
                        ins = pool.tensor_tensor(part, part, zring[:, m % ZR, :], ALU.add)
                    ins.then_inc(s["accp_step"], 1)
                    if m == 8:
                        need(pool, "acc_step", DCH * (tau - 1))
                        need(pool, "zact_done", DCH * (tau - 1))
                        stage_a(tau + 1, (k + 1) % TPB)
            pool.wait_ge(s["a_done"], B)
            pool.wait_ge(s["pad_tile"], 1)
            stage_a(0, 0)
            low_part(range(18, CHUNKS))

            def three(it):
                for k in range(TPB):
                    add_up(it, k)
            rounds(pool, B, three)

        @block.vector
        def _(dve):
            dve.wait_ge(s["ld_ffn"], 16 * 4)
            dve.tensor_scalar(posT2[:], posT, -2.0, None, ALU.mult).then_inc(s["p2_in"], 1)
            dve.tensor_tensor(possq, posT, posT, ALU.mult).then_inc(s["p2_in"], 1)
            dve.wait_ge(s["const_done"], 1)
            bn = linker(dve, "bn_step")
            for b in range(B):
                dve.wait_ge(s["relu_done"], b + 1)
                dve.bn_stats(bnst[:, b, :], hT[:, b, PAD:NP]).then_inc(s["bn_step"], 1)
            dve.wait_ge(s["bn_step"], B)
            dve.bn_aggr(bnmv[:], bnst[:].rearrange("p b k -> p (b k)")).then_inc(s["bn_step"], 1)
            dve.wait_ge(s["bn_step"], B + 1)
            dve.tensor_scalar(bnr[:, 0:1], bnmv[:, 1:2], EPS, None, ALU.add).then_inc(s["bn_step"], 1)
            dve.wait_ge(s["p2_mm"], 1)
            dve.tensor_copy(p2row[:], bank[0][:, 0:P]).then_inc(s["p2_done"], 1)
            dve.wait_ge(s["bn_root"], 1)
            dve.reciprocal(bnr[:, 0:1], bnr[:, 1:2]).then_inc(s["bn_step"], 1)
            dve.wait_ge(s["bn_step"], B + 3)
            for b in range(B):
                dve.tensor_scalar(hT[:, b, PAD:NP], hT[:, b, PAD:NP], bnmv[:, 0:1], bnr[:, 0:1],
                                  ALU.subtract, ALU.mult).then_inc(s["hn_done"], 1)
            for b in range(B):
                dve.wait_ge(s["h_copied"], b + 1)
                for i in range(TPB):
                    t = TPB * b + i
                    ins = dve.bn_stats(st6[:, t, :], h[:, t, :])
            ins.then_inc(s["xin_done"], 1)
            dve.wait_ge(s["xin_done"], 1)
            for t in range(TILES):
                ins = dve.bn_aggr(mv[:, t, :], st6[:, t, :])
            ins.then_inc(s["xin_done"], 1)
            dve.wait_ge(s["xin_done"], 2)
            ln = linker(dve, "ln_step")
            ln(dve.tensor_scalar(tsm, mv[:, :, 1], EPS, None, ALU.add))
            dve.wait_ge(s["ln_root"], 1)
            ln(dve.reciprocal(r0, sq))
            ln(dve.tensor_tensor(tsm, r0, r0, ALU.mult))
            ln(dve.tensor_tensor(tsm, tsm, mv[:, :, 1], ALU.mult))
            ln(dve.tensor_scalar(tsm, tsm, EPS, None, ALU.add))
            dve.wait_ge(s["ln_root"], 2)
            ln(dve.reciprocal(r1, sq))
            for b in range(B):
                for i in range(TPB):
                    t = TPB * b + i
                    ins = dve.tensor_scalar(xin[:, t, :], h[:, t, :], mv[:, t, 0:1], r0[:, t:t + 1],
                                            ALU.subtract, ALU.mult)
                ins.then_inc(s["xin_done"], 1)
            dve.wait_ge(s["hT_mm"], B)
            for b in range(B):
                dve.wait_ge(s["xin_done"], b + 3)
                for i in range(TPB):
                    t = TPB * b + i
                    dve.tensor_scalar(yn[:, b, i, :], xin[:, t, :], r1[:, t:t + 1], None, ALU.mult)\
                        .then_inc(s["yn_done"], 1)
            dve.wait_ge(s["pads_zero"], 1)
            for b in range(B):
                dve.wait_ge(s["y_evac"], b + 1)
                dve.tensor_reduce(ylT[:, b * M:(b + 1) * M], yT[:, b, :].rearrange("p (m l) -> p m l", l=L),
                                  AX_X, ALU.add).then_inc(s["yl_done"], 1)
            sm = linker(dve, "sm2_step")
            for b in range(B):
                dve.wait_ge(s["sim2_mm"], b + 1)
                sims = bank[b][:, 0:PM].rearrange("p (a m) -> p a m", m=M)
                blk = xa[:, b, :].rearrange("p (a m) -> p a m", m=M)
                sm(dve.tensor_reduce(rsx[:, 0, b * PAIRS:(b + 1) * PAIRS], sims, AX_X, ALU.max))
                sm(dve.tensor_tensor(blk, sims, rsx[:, 0, b * PAIRS:(b + 1) * PAIRS, None].to_broadcast([P, PAIRS, M]),
                                     ALU.subtract))
            for b in range(B):
                dve.wait_ge(s["xa_exp"], b + 1)
                blk = xa[:, b, :].rearrange("p (a m) -> p a m", m=M)
                tot = rsx[:, 1, b * PAIRS:(b + 1) * PAIRS]
                sm(dve.tensor_reduce(tot, blk, AX_X, ALU.add))
                sm(dve.reciprocal(tot, tot))
                dve.tensor_tensor(blk, blk, tot[:, :, None].to_broadcast([P, PAIRS, M]), ALU.mult)\
                    .then_inc(s["xa_done"], 1)
            dve.wait_ge(s["xa_done"], B)
            cm = linker(dve, "cmax_step")
            cm(dve.tensor_reduce(rsx[:, 0, :], xa.rearrange("p b (a m) -> p (b a) m", m=M), AX_X, ALU.add))
            dve.wait_ge(s["xaT_evac"], B)
            cm(dve.tensor_reduce(rsx[:, 1, :], xaT.rearrange("p b (a m) -> p (b a) m", m=M), AX_X, ALU.add))
            cm(dve.tensor_reduce(cmx[:], rsx[:], AX_X, ALU.max))
            cm(dve.tensor_copy(crc[:], cmx[:]))
            dve.wait_ge(s["cmax_all"], 1)
            cm(dve.tensor_tensor(crc[:, 0:1], cmxa[:, 0:1], cmxa[:, 1:2], ALU.mult))
            cm(dve.reciprocal(crc[:, 1:2], crc[:, 0:1]))
            dve.wait_ge(s["cmax_step"], 6)
            for b in range(B):
                for x in range(2):
                    ins = dve.tensor_scalar(Pb[half(x), b, :, x * M:(x + 1) * M], by_pair(xaT[half(x), b, :]),
                                            crc[half(x), 1:2], None, ALU.mult)
                ins.then_inc(s["zb_done"], 1)

            def times_eye(j, r=slice(0, P)):
                return eyes[r, j, None, :].to_broadcast([r.stop - r.start, PAIRS, M])

            def first_of(b, r=slice(0, P)):
                return bank[b][r, :].rearrange("p (a m) -> p a m", m=P)[:, :, 0:M]

            def odd_heads(b, which):
                return dve.tensor_copy(Sb[half(1), b, :, M:P], SZ[half(1), b, :, which, :])

            def polynomial(n):
                for b in range(B):
                    dve.wait_ge(s["S_done"], n * B + (b + 1))
                    odd_heads(b, 0)
                    dve.tensor_tensor(by_pair(Tm[:, b, :]), times_eye(0), SZ[:, b, :, 0, :], ALU.subtract)\
                        .then_inc(s["T1_done"], 1)
                for b in range(B):
                    dve.wait_ge(s["T2_mm"], n * B + (b + 1))
                    dve.tensor_tensor(by_pair(Tm[:, b, :]), times_eye(1), first_of(b), ALU.subtract)\
                        .then_inc(s["T2_done"], 1)
                for b in range(B):
                    dve.wait_ge(s["P_mm"], n * B + (b + 1))
                    for x in range(2):
                        ins = dve.scalar_tensor_tensor(Pb[half(x), b, :, x * M:(x + 1) * M], first_of(b, half(x)),
                                                       -0.25, times_eye(2, half(x)), ALU.mult, ALU.add)
                    ins.then_inc(s["P_done"], 1)

            def pinv(j, last):
                polynomial(2 * j)
                polynomial(2 * j + 1)
                if not last:
                    for b in range(B):
                        dve.wait_ge(s["zt_done"], j * B + (b + 1))
                        odd_heads(b, 1).then_inc(s["zt_odd"], 1)
            dve.wait_ge(s["const_done"], 2)
            pinv_rounds(dve, pinv)

            F_STEPS = 6

            def ffn_link(ins):
                ins.then_inc(s["f_step"], 1)

            def ffn_after(c, k):
                dve.wait_ge(s["f_step"], F_STEPS * c + k)

            def add_attention(c):
                dve.wait_ge(s["out1_mm"], c + 1)
                blk = h[:, bass.ds(TPB * c, TPB), :]
                dve.tensor_tensor(blk, blk, bank[5][:, 0:NP].rearrange("p (i c) -> p i c", c=P), ALU.add)\
                    .then_inc(s["h1_done"], 1)

            def one_tile(x, c, i):
                return x[:, bass.ds(TPB * c + i, 1), :].rearrange("p a c -> p (a c)")

            def ffn_stats(c):
                dve.wait_ge(s["h1_done"], c + 1)
                settle(dve)
                for i in range(TPB):
                    ins = dve.bn_stats(f_st6[:, i, :], one_tile(h, c, i))
                ffn_link(ins)

            def ffn_aggregate(c):
                ffn_after(c, 1)
                settle(dve)
                for i in range(TPB):
                    ins = dve.bn_aggr(f_mv[:, i, :], f_st6[:, i, :])
                ffn_link(ins)

            def ffn_variance(c):
                ffn_after(c, 2)
                dve.tensor_scalar(f_var[:], f_mv[:, :, 1], EPS, None, ALU.add).then_inc(s["f_var_done"], 1)

            def ffn_reciprocal_root(c):
                dve.wait_ge(s["f_root"], c + 1)
                ffn_link(dve.reciprocal(f_r[:], f_sd[:]))

            def ffn_norm(c):
                ffn_after(c, 3)
                for i in range(TPB):
                    ins = dve.tensor_scalar(u_tok[:, i, :], one_tile(h, c, i), f_mv[:, i, 0:1], f_r[:, i:i + 1],
                                            ALU.subtract, ALU.mult)
                ins.then_inc(s["u_done"], 1)

            def ffn_squared_distances(c):
                dve.wait_ge(s["u2_done"], c + 1)
                dve.wait_ge(s["d_mm"], c + 1)
                for i in range(TPB):
                    ins = dve.scalar_tensor_tensor(fa[:, i, :], bank[0][:, i * P:(i + 1) * P], u2[:, i:i + 1],
                                                   p2row[:], ALU.add, ALU.add)
                ffn_link(ins)
                ffn_after(c, 4)
                dve.tensor_scalar(fa[:], fa[:], 0.0, None, ALU.max).then_inc(s["d2_done"], 1)

            def ffn_shift(c):
                dve.wait_ge(s["d_root"], c + 1)
                ffn_link(dve.tensor_scalar(fa[:], fa[:], 0.1, None, ALU.add))

            def ffn_invert(c, i):
                ffn_after(c, 5)
                ins = dve.reciprocal(fa[:, i, :], fa[:, i, :])
                if i == TPB - 1:
                    ins.then_inc(s["f_inv"], 1)

            def ffn_maximum(c):
                dve.wait_ge(s["f_scaled"], c + 1)
                dve.tensor_reduce(f_mx[:], fa[:], AX_X, ALU.max, negate=True).then_inc(s["f_max"], 1)

            def ffn_total(c):
                dve.wait_ge(s["f_exp"], c + 1)
                ffn_link(dve.reciprocal(f_rt[:], f_tot[:]))
                ffn_after(c, 6)
                dve.sem_inc(s["f_sum"], 1)

            def attend(b, par):
                def sims(i):
                    return bank[i][:].rearrange("p (a m) -> p a m", m=M)

                def sim1_max(i):
                    dve.wait_ge(s["sim1_mm"], TPB * b + (i + 1))
                    dve.tensor_reduce(m1[:, i, :], sims(i), AX_X, ALU.max).then_inc(s["s1_sub"], 1)

                def sim1_less_max(i):
                    dve.wait_ge(s["s1_sub"], 2 * TPB * b + (2 * i + 1))
                    dve.tensor_tensor(e1[:, i], sims(i), m1[:, i, :, None].to_broadcast([P, HEADS, M]), ALU.subtract)\
                        .then_inc(s["s1_sub"], 1)

                def sim3_max(p):
                    dve.wait_ge(s["sim3_mm"], PAIRS * b + (p + 1))
                    dve.tensor_reduce(m3[:, p:p + 1], bank[SIM3_BANK[p]][:, 0:NP], AX_X, ALU.max, negate=True)\
                        .then_inc(s["e3_max"], 1)

                def e1_sum(i):
                    dve.wait_ge(s["e1_exp"], TPB * b + (i + 1))
                    dve.tensor_reduce(s1[:, i, :], e1[:, i], AX_X, ALU.add).then_inc(s["s1_norm"], 1)
                    dve.wait_ge(s["s1_norm"], 2 * TPB * b + (2 * i + 1))
                    dve.reciprocal(rr1[:, i, :], s1[:, i, :]).then_inc(s["s1_norm"], 1)

                before = has_before(b)
                c = b - 1
                if before:
                    add_attention(c)
                    ffn_stats(c)
                    ffn_aggregate(c)
                    ffn_variance(c)
                sim1_max(0)
                sim1_less_max(0)
                sim1_max(1)
                if before:
                    ffn_reciprocal_root(c)
                    ffn_norm(c)
                sim1_less_max(1)
                sim1_max(2)
                sim1_less_max(2)
                sim3_max(0)
                sim3_max(1)
                if before:
                    ffn_squared_distances(c)
                sim3_max(2)
                sim3_max(3)
                if before:
                    ffn_shift(c)
                    ffn_invert(c, 0)
                for p in (0, 1):
                    dve.wait_ge(s["e3T_mm"], PAIRS * b + (p + 1))
                    dve.tensor_copy(e3T[:, :, p, :], bank[6 + p % 2][:, 0:NP].rearrange("p (i m) -> p i m", m=P))\
                        .then_inc(s["e3T_evac_v"], 1)
                e1_sum(0)
                if before:
                    ffn_invert(c, 1)
                e1_sum(1)
                e1_sum(2)
                if before:
                    ffn_invert(c, 2)
                dve.wait_ge(s["e3_exp"], PAIRS * b + PAIRS)
                dve.reciprocal(rr3, s3).then_inc(s["rr3_done"], 1)
                dve.wait_ge(s["uT_mm"], b + 1)
                for x in range(2):
                    dve.tensor_copy(uTb[half(x), :, :],
                                    bank[4][half(x), :].rearrange("p (a m) -> p a m", m=P)[:, :, x * M:(x + 1) * M])\
                        .then_inc(s["uT_evac"], 1)
                dve.wait_ge(s["uw_mm"], b + 1)
                dve.wait_ge(s["rr3_done"], b + 1)
                dve.tensor_tensor(uw, bank[3][:].rearrange("p (a c) -> p a c", c=P),
                                  rr3[:, :, None].to_broadcast([P, PAIRS, P]), ALU.mult).then_inc(s["uw_evac"], 1)
                if before:
                    ffn_maximum(c)
                    ffn_total(c)

            dve.wait_ge(s["h_plus"], 2 * B)
            batch_pairs(dve, attend)

            def low_part(chunks):
                for c in chunks:
                    if not pool_takes(c):
                        n = slice(GRP * c, GRP * c + GRP)
                        dve.wait_ge(s["vhi_done"], c + 1)
                        dve.tensor_tensor(v_lo[:, n, :], v_raw[:, n, :], v_hi[:, n, :].bitcast(F32), ALU.subtract)\
                            .then_inc(s["vlo_done"], 1)
            add_attention(B - 1)
            ffn_stats(B - 1)
            ffn_aggregate(B - 1)
            ffn_variance(B - 1)
            low_part(range(0, 3))
            ffn_reciprocal_root(B - 1)
            ffn_norm(B - 1)
            low_part(range(3, 7))
            ffn_squared_distances(B - 1)
            ffn_shift(B - 1)
            for i in range(TPB):
                ffn_invert(B - 1, i)
            low_part(range(7, 13))
            ffn_maximum(B - 1)
            low_part(range(13, 16))
            ffn_total(B - 1)
            dve.wait_ge(s["hb_done"], B)

            def stage(tau, k):
                dve.wait_ge(s["xhi_done"], tau + 1)
                dve.tensor_tensor(xlo[:, k, :], uT[:, bass.ds(tau, 1), :].rearrange("p a c -> p (a c)"),
                                  xhi[:, k, :].bitcast(F32), ALU.subtract).then_inc(s["xlo_done"], 1)
            dve.wait_ge(s["pad_tile"], 1)
            stage(0, 0)
            low_part(range(16, CHUNKS))

            def weigh(it, k):
                tau = TPB * it + k
                first = isinstance(it, int) and k == 0
                dve.wait_ge(s["ast_done"], tau + 1)
                need(dve, "o_sum_done", tau - 2)
                for d in range(DCH):
                    c = 2 * d
                    dve.wait_ge(s["y_done_f"], CHUNKS * tau + (c + 1))
                    if d >= 2:
                        dve.wait_ge(s["acc_step"], DCH * tau + (d - 1))
                    for j in range(GRP):
                        y = bank[(2 * k + c) % YBANKS][:, j * P:(j + 1) * P]
                        to = acc[:, k, GRP * (d % 2) + j, :]
                        w = a_st[:, k, GRP * c + j:GRP * c + j + 1]
                        if d < 2:
                            ins = dve.tensor_scalar(to, y, w, None, ALU.mult)
                        else:
                            ins = dve.scalar_tensor_tensor(to, y, w, to, ALU.mult, ALU.add)
                    ins.then_inc(s["acc_step"], 1)
                    if d == 4 and not first:
                        sum_up(tau - 1, (k - 1) % TPB)
                    if d == 11 and not first:
                        finish(tau - 1, (k - 1) % TPB, it - 1 if k == 0 else it)
                    if d == 12:
                        need(dve, "y_done_f", CHUNKS * (tau - 1))
                        stage(tau + 1, (k + 1) % TPB)

            def sum_up(tau, k):
                dve.wait_ge(s["acc_step"], DCH * (tau + 1))
                dve.wait_ge(s["accp_step"], (DCH - 1) * (tau + 1))
                need(dve, "oT_mm", tau - 2)
                dve.tensor_reduce(o_sum[:, k, :], acc[:, k].rearrange("p j c -> p c j"), AX_X, ALU.add)\
                    .then_inc(s["o_sum_done"], 1)

            def finish(tau, k, it):
                dve.wait_ge(s["o_mm"], tau + 1)
                need(dve, f"stored{k}", 16 * it)
                dve.tensor_tensor(o_fin[:, k, :], bank[7][:, 0:P],
                                  h[:, bass.ds(tau, 1), :].rearrange("p a c -> p (a c)"), ALU.add)\
                    .then_inc(s["fin_done"], 1)

            def three(it):
                for k in range(TPB):
                    weigh(it, k)
            rounds(dve, B, three)
            sum_up(TILES - 1, TPB - 1)
            finish(TILES - 1, TPB - 1, B - 1)


def kernel(**inputs):
    import numpy as np
    import concourse.bacc as bacc
    from concourse.bass_utils import run_bass_kernel_spmd

    x = {n: np.asarray(a) for n, a in inputs.items()}
    w_qkv = x["L0_attn_w_qkv"]
    taps = x["L0_attn_w_res"].reshape(HEADS, TAPS)
    padded = np.zeros((HEADS, WPAD), np.float32)
    padded[:, P - 1:P - 1 + TAPS] = taps[:, ::-1]
    band = np.stack([padded[:, P - 1 - p:P - 1 - p + CW] for p in range(P)])
    arrays = {
        "xt": x["x"].transpose(2, 0, 1),
        "tok_wt": x["L0_tok_W"].T,
        "tok_b": x["L0_tok_b"].reshape(P, 1),
        "ln_g": x["L0_attn_ln_g"].reshape(P, 1),
        "ln_b": x["L0_attn_ln_b"].reshape(P, 1),
        "w_qkv": w_qkv,
        "w_qk_t": w_qkv[:, 0:2 * HM].T.reshape(2 * PAIRS, P, P).transpose(1, 0, 2),
        "w_out": x["L0_attn_w_out"],
        "b_out": x["L0_attn_b_out"],
        "w_res": band,
        "pos_t": x["L0_ffn_positions"].T,
        "scales": x["L0_ffn_scales"],
        "vw": x["L0_ffn_value_weight"],
        "out_wt": x["L0_ffn_out_W"].T,
        "out_b": x["L0_ffn_out_b"],
        "ident_in": np.eye(P, dtype=np.float32),
    }
    arrays = {n: np.ascontiguousarray(a) for n, a in arrays.items()}
    nc = bacc.Bacc("TRN2", target_bir_lowering=False, num_devices=1)
    args = {n: nc.dram_tensor(n, a.shape, F32, kind="ExternalInput").ap() for n, a in arrays.items()}
    args["out"] = nc.dram_tensor("out", (B, T, P), F32, kind="ExternalOutput").ap()
    audio_tower(nc, **args)
    r = run_bass_kernel_spmd(nc, [arrays], core_ids=[0])
    return r.results[0]["out"]
```

```python
from contextlib import ExitStack

import concourse.bass as bass
from concourse import mybir

F32 = mybir.dt.float32
F32R = mybir.dt.float32r
ALU = mybir.AluOpType
ACT = mybir.ActivationFunctionType
AX_X = mybir.AxisListType.X
RMAX = bass.bass_isa.ReduceOp.max

P = 128
B, T, CTX, DIN = 8, 371, 5, 23
KW = CTX * DIN
HEADS, DH, M = 8, 64, 64
PAIRS = HEADS // 2
HM = HEADS * M
PM = PAIRS * M
NP = 384
PAD = NP - T
L = NP // M
TPB = NP // P
TILES = B * TPB
TAPS = 33
HALF = TAPS // 2
CW = P + TAPS - 1
WPAD = P - 1 + TAPS + P - 1
ITERS = 6
ROUNDS = 2
STEPS = ITERS // ROUNDS
EPS = 1e-5
GRP = 4
CHUNKS = P // GRP
YBANKS = 6
SIM3_BANK = (6, 7, 1, 2)
CONV_BANK = (3, 4, 0, 3)
SCALE = DH ** -0.5
ZR = 4
DCH = CHUNKS // 2


def audio_tower(nc, xt, tok_wt, tok_b, ln_g, ln_b, w_qkv, w_qk_t, w_out, b_out, w_res, pos_t,
                scales, vw, out_wt, out_b, ident_in, out):
    with ExitStack() as ctx:
        def sb(name, shape, dt=F32, at=ctx):
            return at.enter_context(nc.sbuf_tensor(name, shape, dt))

        def sem(name):
            return ctx.enter_context(nc.semaphore(name))

        bank = [ctx.enter_context(nc.psum_tensor(f"bank{i}", [P, 512], F32)) for i in range(8)]

        ident = sb("ident", [P, P])
        h = sb("h", [P, TILES, P])
        posT2 = sb("posT2", [P, P])
        p2row = sb("p2row", [P, P])
        scrow = sb("scrow", [P, P])
        outWT = sb("outWT", [P, P])
        outb = sb("outb", [P, P])
        vec = sb("vec", [P, 3])
        bnmv = sb("bnmv", [P, 2])
        bnr = sb("bnr", [P, 2])
        cmx = sb("cmx", [P, 2])
        cmxa = sb("cmxa", [P, 2])
        crc = sb("crc", [P, 2])
        rsx = sb("rsx", [P, 2, B * PAIRS])
        uT = sb("uT", [P, TILES + 1, P])
        yT = uT[:, 0:TILES, :].rearrange("p (b i) t -> p b (i t)", b=B)
        at_all = sb("at_all", [P, TILES + 1, P])
        f_st6 = sb("f_st6", [P, TPB, 6])
        f_mv = sb("f_mv", [P, TPB, 2])
        f_var = sb("f_var", [P, TPB])
        f_sd = sb("f_sd", [P, TPB])
        f_r = sb("f_r", [P, TPB])
        f_nmr = sb("f_nmr", [P, TPB])
        f_vr = sb("f_vr", [P, TPB])
        u2 = sb("u2", [P, TPB])
        f_mx = sb("f_mx", [P, TPB])
        f_tot = sb("f_tot", [P, TPB])
        f_rt = sb("f_rt", [P, TPB])
        u_tok = sb("u_tok", [P, TPB, P])
        uTs = sb("uTs", [P, TPB, P])
        fa = sb("fa", [P, TPB, P])
        o_sum = u_tok
        oT = uTs[:, 0, :]
        o_fin = fa

        early = ExitStack()
        v_raw = sb("v_raw", [P, P, P], at=early)
        ARENA = 25184
        arena = sb("arena", [P, ARENA], at=early)
        early.close()
        OPERANDS = 2 * B * HM + B * PM + PAIRS * P + HEADS * CW
        middle = ExitStack()
        sb("before_operands", [P, P * P + OPERANDS], at=middle)
        wv_lo, wv_hi, A_hi, A_lo, B_hi, B_lo = (sb(n, [P, HM], F32R, at=middle)[:] for n in
                                                ("wv_lo", "wv_hi", "A_hi", "A_lo", "B_hi", "B_lo"))
        y_hi, y_lo = (sb(n, [P, NP], F32R, at=middle)[:] for n in ("y_hi", "y_lo"))
        middle.close()
        v_lo = sb("v_lo", [P, P, P], F32R)
        v_hi = sb("v_hi", [P, P, P], F32R)
        zring = sb("zring", [P, ZR, GRP * P])
        xhi = sb("xhi", [P, TPB, P], F32R)
        xlo = sb("xlo", [P, TPB, P], F32R)
        a_st = sb("a_st", [P, TPB, P])
        acc = sb("acc", [P, TPB, 12, P])

        cursor = [0]

        def take(*dims):
            n = 1
            for d in dims:
                n *= d
            at = cursor[0]
            cursor[0] += n
            assert cursor[0] <= ARENA, cursor[0]
            v = arena[:, at:at + n]
            if len(dims) == 2:
                v = v.rearrange("p (a b) -> p a b", b=dims[1])
            elif len(dims) == 3:
                v = v.rearrange("p (a b c) -> p a b c", b=dims[1], c=dims[2])
            elif len(dims) == 4:
                v = v.rearrange("p (a b c d) -> p a b c d", b=dims[1], c=dims[2], d=dims[3])
            return v

        Aq = take(B, HEADS, M)
        Bk = take(B, HEADS, M)
        xaT = take(B, PM)
        ztt = xaT
        wo = take(PAIRS, P)
        toe = take(HEADS, CW)
        wv = take(HM)
        mark = cursor[0]
        spare = at_all[:].rearrange("p t n -> p (t n)")
        xa = spare[:, 0:B * PM].rearrange("p (b c) -> p b c", b=B)
        eyes = spare[:, B * PM:B * PM + 3 * M].rearrange("p (j m) -> p j m", m=M)
        before_v = v_raw[:].rearrange("p n e -> p (n e)")

        PART = PAIRS * B * M

        def early_part(n, count, width):
            return before_v[:, n * PART:n * PART + count * width].rearrange("p (a m) -> p a m", m=width)
        klX = [early_part(x, PAIRS, B * M) for x in (0, 1)]
        qlX = [early_part(x, PAIRS, B * M) for x in (2, 3)]
        wqk = before_v[:, 4 * PART:4 * PART + 2 * HM]
        wqkT = early_part(5, 2 * PAIRS, P)
        at = B * PM + 3 * M + B * M
        bout = spare[:, at:at + P]
        nm0 = spare[:, at + P:at + P + TILES]
        r0p = spare[:, at + P + TILES:at + P + 2 * TILES]
        bnst = spare[:, at + P + 2 * TILES:at + P + 2 * TILES + 6 * B].rearrange("p (b k) -> p b k", b=B)
        cursor[0] = mark + B * PAIRS * P
        hT = take(B, NP)
        tokW = take(P)
        posT = take(P)
        possq = take(P)
        ones = take(P)
        st6 = take(TILES, 6)
        mv = take(TILES, 2)
        r0 = take(TILES)
        r1 = take(TILES)
        nm1 = take(TILES)
        tsm = take(TILES)
        sq = take(TILES)
        cursor[0] = mark + 2 * B * PAIRS * P
        win = take(B, T)
        cursor[0] -= B * T
        ylT = spare[:, B * PM + 3 * M:B * PM + 3 * M + B * M]
        yn = hT.rearrange("p b (i c) -> p b i c", c=P)
        cursor[0] = mark
        Tm = xa
        SZ = take(B, PAIRS, 2, M)
        Sb = take(B, PAIRS, P)
        Pb = take(B, PAIRS, P)
        assert OPERANDS == mark - HM
        cursor[0] = OPERANDS + 6 * HM + 2 * NP
        ztb = take(PM)
        e1 = take(TPB, HEADS, M)
        e3 = take(PAIRS, NP)
        a1T = e3
        e3T = take(TPB, PAIRS, P)
        vb = take(TPB, HM)
        resT = take(PAIRS, NP)
        uTb = take(PAIRS, M)
        uw = take(PAIRS, P)
        gw = take(PAIRS, P)
        m1 = take(TPB, HEADS)
        s1 = take(TPB, HEADS)
        rr1 = take(TPB, HEADS)
        m3 = take(PAIRS)
        s3 = take(PAIRS)
        rr3 = take(PAIRS)

        def half(x):
            return slice(64 * (x % 2), 64 * (x % 2) + 64)

        s = {n: sem(n) for n in """ld_x ld_id ld_vec ld_attn ld_ffn ld_v
        tok_mm relu_done bn_step bn_root hn_done hT_mm h_copied stat_step ln_step ln_root
        hs_done h_twice yn_done yn_act h_plus y_mm y_evac pads_zero yl_done
        qk_mm qk_even qk_odd fold_mm fold_evac sim2_mm sm2_step xa_exp xa_sum xa_done xaT_mm xaT_evac
        cmax_step cmax_all zeros_kq zeros_b eyes_done hpad_zero
        S_mm S_done T1_done T2_mm T2_done P_mm P_done z_mm zt_done zt_odd zb_mm zb_done z_done
        hi_done staged z_staged first_hi first_hi_v first_lo sim1_mm v_mm sim3_mm conv_mm e3T_mm uT_mm a1T_mm uw_mm gw_mm out1_mm
        s1_sub s1_norm e1_exp e3_max e3_exp v_evac conv_evac e3T_evac e3T_evac_v uT_evac rr3_done a1_norm a1T_evac
        uw_evac gw_evac h1_done
        p2_in p2_mm p2_done waits_passed
        f_step f_var_done f_root f_norm u_done u2_done u_mm uTs_done uT_done d_mm d2_done d_root f_inv f_scaled f_max f_exp
        f_sum a_done hb_done
        vhi_done vlo_done vlop_done xhi_done xlo_done ast_done pad_tile y_done_f acc_step zact_done accp_step
        o_sum_done oT_mm oT_evac o_mm fin_done stored0 stored1 stored2""".split()}

        def need(eng, name, value):
            if not isinstance(value, int) or value > 0:
                eng.wait_ge(s[name], value)

        def settle(eng):
            eng.sem_inc(s["waits_passed"], 1)

        def batches(eng, body):
            body(0)
            with eng.Fori(1, B - 2) as b:
                body(b)
            body(B - 2)
            body(B - 1)

        def has_before(b):
            return not isinstance(b, int) or b > 0

        def has_after(b):
            return not isinstance(b, int) or b < B - 1

        def first_tile(it, k):
            return isinstance(it, int) and it == 0 and k == 0

        def rounds(eng, n, body):
            body(0)
            with eng.Fori(1, n) as i:
                body(i)

        def in_round(eng, j, step):
            with eng.Fori(STEPS * j, STEPS * j + STEPS - 1) as n:
                step(n)

        def part(n):
            return slice(TILES // 2 * (n % 2), TILES // 2 * (n % 2) + TILES // 2)

        def landmarks_to(x, k):
            if k < PAIRS:
                return qlX[x][half(x), k, :], SCALE / L
            return klX[x][half(x), k - PAIRS, :], 1.0 / L

        def by_pair(x):
            return x.rearrange("p (a m) -> p a m", m=M)

        EARLY = 14
        assert EARLY * GRP * P <= 2 * B * HM

        AHEAD = 2

        def split_during(m):
            return [c for c in (EARLY + 2 * m, EARLY + 2 * m + 1) if c < CHUNKS]

        def pool_takes(c):
            return c < 8 or c % 4 == 3

        def low_part_wait(eng, c):
            mine = sum(pool_takes(x) == pool_takes(c) for x in range(c + 1))
            eng.wait_ge(s["vlop_done" if pool_takes(c) else "vlo_done"], mine)

        reach = [(max(0, P * i - HALF), min(NP, P * i + P + HALF), P * i - HALF) for i in range(TPB)]

        block = ctx.enter_context(nc.Block())

        @block.sync
        def _(sp):
            for i in range(CTX):
                sp.dma_start(win[i * DIN:(i + 1) * DIN], xt[:, :, i:i + T]).then_inc(s["ld_x"], 16)
            sp.dma_start(tokW[0:KW], tok_wt).then_inc(s["ld_x"], 16)
            sp.dma_start(vec[:, 0:1], tok_b).then_inc(s["ld_vec"], 16)
            sp.dma_start(ident[:], ident_in).then_inc(s["ld_id"], 16)
            sp.dma_start(vec[:, 1:2], ln_g).then_inc(s["ld_vec"], 16)
            sp.dma_start(vec[:, 2:3], ln_b).then_inc(s["ld_vec"], 16)
            sp.dma_start(bout, b_out.partition_broadcast(P)).then_inc(s["ld_vec"], 16)
            sp.dma_start(posT, pos_t).then_inc(s["ld_ffn"], 16)
            sp.dma_start(outWT[:], out_wt).then_inc(s["ld_ffn"], 16)
            sp.dma_start(scrow[:], scales.partition_broadcast(P)).then_inc(s["ld_ffn"], 16)
            sp.dma_start(outb[:], out_b.partition_broadcast(P)).then_inc(s["ld_ffn"], 16)
            sp.dma_start(wqk, w_qkv[:, 0:2 * HM]).then_inc(s["ld_attn"], 16)
            sp.dma_start(wqkT, w_qk_t).then_inc(s["ld_attn"], 16)
            sp.dma_start(wv, w_qkv[:, 2 * HM:3 * HM]).then_inc(s["ld_attn"], 16)
            sp.dma_start(wo, w_out.rearrange("(a p) n -> p a n", p=P)).then_inc(s["ld_attn"], 16)
            sp.dma_start(toe, w_res).then_inc(s["ld_attn"], 16)
            sp.wait_ge(s["fold_mm"], 2 * HEADS)
            for k in range(8):
                n = P // 8
                sp.dma_start(v_raw[:, k * n:(k + 1) * n, :],
                             vw[k * n:(k + 1) * n].rearrange("n d e -> d n e")).then_inc(s["ld_v"], 16)
            with sp.Fori(0, B) as b:
                for k in range(TPB):
                    sp.wait_ge(s["fin_done"], TPB * b + (k + 1))
                    lo = PAD if k == 0 else 0
                    sp.dma_start(out[bass.ds(b, 1), k * P + lo - PAD:(k + 1) * P - PAD, :]
                                 .rearrange("a t c -> (a t) c"),
                                 o_fin[lo:P, k, :]).then_inc(s[f"stored{k}"], 16)
            for k in range(TPB):
                sp.wait_ge(s[f"stored{k}"], 16 * B)

        @block.tensor
        def _(pe):
            pe.wait_ge(s["ld_x"], 16 * (CTX + 1))
            for b in range(B):
                pe.matmul(bank[b][:, 0:T], tokW[0:KW], win[0:KW, b, :], start=True, stop=True).then_inc(s["tok_mm"], 1)
            pe.wait_ge(s["relu_done"], 1)
            pe.wait_ge(s["p2_in"], 3)
            pe.matmul(bank[0][:, 0:P], ones, possq, start=True, stop=True).then_inc(s["p2_mm"], 1)
            pe.wait_ge(s["ld_id"], 16)
            pe.wait_ge(s["p2_done"], 1)
            for b in range(B):
                pe.wait_ge(s["hn_done"], b + 1)
                for i in range(TPB):
                    mm = pe.transpose(bank[b][:, i * P:(i + 1) * P], hT[:, b, i * P:(i + 1) * P], ident[:])
                mm.then_inc(s["hT_mm"], 1)
            for b in range(B):
                pe.wait_ge(s["h_copied"], b + 1)
                pe.wait_ge(s["yn_act" if b % 2 else "yn_done"], b // 2 + 1)
                for i in range(TPB):
                    mm = pe.transpose(bank[b][:, i * P:(i + 1) * P], yn[:, b, i, :], ident[:])
                mm.then_inc(s["y_mm"], 1)
            pe.wait_ge(s["ld_attn"], 16 * 5)
            pe.wait_ge(s["yl_done"], B)
            for k in range(2 * PAIRS):
                pe.wait_ge(s["y_evac"], k + 1)
                pe.matmul(bank[k][:], wqk[:, k * P:(k + 1) * P], ylT, start=True, stop=True).then_inc(s["qk_mm"], 1)
            pe.wait_ge(s["qk_even"], 2 * PAIRS)
            pe.wait_ge(s["qk_odd"], 2 * PAIRS)
            for b in range(B):
                for hd in range(HEADS):
                    r, p = half(hd), hd // 2
                    mm = pe.matmul(bank[b][r, p * M:(p + 1) * M], qlX[hd % 2][r, p, b * M:(b + 1) * M],
                                   klX[hd % 2][r, p, b * M:(b + 1) * M], start=True, stop=True)
                mm.then_inc(s["sim2_mm"], 1)

            def fold(hd, w0, src, k):
                pe.matmul(bank[k][:], wqkT[:, w0 + hd // 2, :], src[hd % 2][:, hd // 2, :], start=True, stop=True)\
                    .then_inc(s["fold_mm"], 1)
            pe.wait_ge(s["zeros_kq"], 1)
            for hd in range(HEADS):
                pe.wait_ge(s["sm2_step"], 2 * (hd + 1))
                fold(hd, 0, klX, hd)
            for b in range(B):
                pe.wait_ge(s["fold_evac"], b + 1)
                pe.wait_ge(s["xa_done"], b + 1)
                for hd in range(HEADS):
                    r, p = half(hd), hd // 2
                    mm = pe.matmul(bank[b][r, p * M:(p + 1) * M], xa[r, b, p * M:(p + 1) * M],
                                   ident[r, r], start=True, stop=True)
                mm.then_inc(s["xaT_mm"], 1)
            for hd in range(HEADS):
                pe.wait_ge(s["xaT_evac"], hd + 1)
                fold(hd, PAIRS, qlX, hd)

            def pair_products(b, left, right):
                for p in range(PAIRS):
                    mm = pe.matmul(bank[b][:, p * P:(p + 1) * P], left[:, b, p, :], right(p), start=True, stop=True)
                return mm

            def twice(x):
                return x[:, None, :].to_broadcast([P, 2, M])

            def polynomial(n):
                for b in range(B):
                    pe.wait_ge(s["S_done"], n * B + (b + 1))
                    pe.wait_ge(s["T1_done"], n * B + (b + 1))
                    pair_products(b, Sb, lambda p: twice(Tm[:, b, p * M:(p + 1) * M])).then_inc(s["T2_mm"], 1)
                for b in range(B):
                    pe.wait_ge(s["T2_done"], n * B + (b + 1))
                    pair_products(b, Sb, lambda p: twice(Tm[:, b, p * M:(p + 1) * M])).then_inc(s["P_mm"], 1)

            def pinv(j, last):
                for b in range(B):
                    pe.wait_ge(s["zb_done"], j * B + (b + 1))
                    pair_products(b, Pb, lambda p: twice(xaT[:, b, p * M:(p + 1) * M])).then_inc(s["S_mm"], 1)

                def step(n):
                    polynomial(n)
                    for b in range(B):
                        pe.wait_ge(s["P_done"], n * B + (b + 1))
                        pair_products(b, Pb, lambda p: SZ[:, b, p].rearrange("p x m -> p (x m)"))\
                            .then_inc(s["S_mm"], 1)
                in_round(pe, j, step)
                n = STEPS * j + STEPS - 1
                polynomial(n)
                for b in range(B):
                    pe.wait_ge(s["P_done"], n * B + (b + 1))
                    pair_products(b, Pb, lambda p: twice(SZ[:, b, p, 1, :])).then_inc(s["z_mm"], 1)
                if not last:
                    for b in range(B):
                        pe.wait_ge(s["zt_done"], j * B + (b + 1))
                        pe.wait_ge(s["zt_odd"], j * B + (b + 1))
                        for p in range(PAIRS):
                            t = pe.transpose(bank[b][:, p * P:(p + 1) * P], Sb[:, b, p, :], ident[:])
                        t.then_inc(s["zb_mm"], 1)
            pe.wait_ge(s["fold_evac"], 2 * HEADS)
            pe.wait_ge(s["zeros_b"], 1)
            for j in range(ROUNDS):
                pinv(j, j == ROUNDS - 1)
            pe.wait_ge(s["z_done"], B)

            def ffn_transposes(c, at=bank[0]):
                pe.wait_ge(s["u_done"], c + 1)
                for i in range(TPB):
                    t = pe.transpose(at[:, i * P:(i + 1) * P], u_tok[:, i, :], ident[:])
                t.then_inc(s["u_mm"], 1)

            def ffn_distances(c, at=bank[0]):
                pe.wait_ge(s["uTs_done"], c + 1)
                for i in range(TPB):
                    mm = pe.matmul(at[:, i * P:(i + 1) * P], uTs[:, i, :], posT2[:], start=True, stop=True)
                mm.then_inc(s["d_mm"], 1)

            def attend(b):
                first = isinstance(b, int) and b == 0
                if first:
                    pe.wait_ge(s["first_hi"], 2)
                    pe.wait_ge(s["first_lo"], 1)
                else:
                    pe.wait_ge(s["staged"], b)

                def split_product(out, left, right):
                    pe.matmul(out, left[0], right[0], start=True, stop=False)
                    pe.matmul(out, left[0], right[1], start=False, stop=False)
                    return pe.matmul(out, left[1], right[0], start=False, stop=True)

                def tokens(i):
                    return y_hi[:, i * P:(i + 1) * P], y_lo[:, i * P:(i + 1) * P]

                for i in range(TPB):
                    need(pe, "a1T_evac", TPB * b + (i + 1 - TPB))
                    split_product(bank[i][:], tokens(i), (A_hi, A_lo)).then_inc(s["sim1_mm"], 1)
                need(pe, "uw_evac", b)
                need(pe, "uT_evac", 2 * b)
                if first:
                    pe.wait_ge(s["first_lo"], 2)
                for i in range(TPB):
                    if i == TPB - 1:
                        need(pe, "h1_done", b)
                    split_product(bank[3 + i][:], tokens(i), (wv_hi, wv_lo)).then_inc(s["v_mm"], 1)
                need(pe, "gw_evac", b)
                if first:
                    pe.wait_ge(s["first_lo"], 3)

                def sim3(p):
                    if p == 2:
                        pe.wait_ge(s["s1_sub"], 2 * TPB * b + 4)
                    if p == 3:
                        pe.wait_ge(s["s1_sub"], 2 * TPB * b + 6)
                    c = slice(p * P, (p + 1) * P)
                    split_product(bank[SIM3_BANK[p]][:, 0:NP], (B_hi[:, c], B_lo[:, c]), (y_hi, y_lo))\
                        .then_inc(s["sim3_mm"], 1)

                def convolve(p):
                    if p == 2 and has_before(b):
                        pe.wait_ge(s["d2_done"], b)
                    if p == 3:
                        pe.wait_ge(s["conv_evac"], PAIRS * b + 1)
                    for hd in (2 * p, 2 * p + 1):
                        for i in range(TPB):
                            t0, t1, tc = reach[i]
                            mm = pe.matmul(bank[CONV_BANK[p]][half(hd), t0:t1], vb[:, i, hd * DH:(hd + 1) * DH],
                                           toe[:, hd, t0 - tc:t1 - tc], start=(i == 0), stop=(i == TPB - 1),
                                           skip_group_check=True)
                    mm.then_inc(s["conv_mm"], 1)

                def e3_transposed(p):
                    for i in range(TPB):
                        t = pe.transpose(bank[6 + p % 2][:, i * P:(i + 1) * P], e3[:, p, i * P:(i + 1) * P], ident[:])
                    t.then_inc(s["e3T_mm"], 1)

                def a1_transposed(i):
                    pe.wait_ge(s["a1_norm"], TPB * b + (i + 1))
                    for p in range(PAIRS):
                        t = pe.transpose(bank[i][:, p * P:(p + 1) * P],
                                         e1[:, i, 2 * p:2 * p + 2, :].rearrange("p a m -> p (a m)"), ident[:])
                    t.then_inc(s["a1T_mm"], 1)

                def project_convolved(steps):
                    for n in steps:
                        p, i = n // TPB, n % TPB
                        pe.matmul(bank[5][:, i * P:(i + 1) * P], resT[:, p, i * P:(i + 1) * P], wo[:, p, :],
                                  start=(n == 0), stop=False, skip_group_check=True)

                sim3(0)
                sim3(1)
                if has_before(b):
                    pe.wait_ge(s["s1_sub"], 2 * TPB * b + 2)
                    ffn_transposes(b - 1)
                pe.wait_ge(s["v_evac"], TPB * b + TPB)
                convolve(0)
                if has_before(b):
                    ffn_distances(b - 1)
                sim3(2)
                sim3(3)
                for p in (1, 2, 3):
                    convolve(p)
                project_convolved(range(0, 2))
                pe.wait_ge(s["e3_exp"], PAIRS * b + 2)
                e3_transposed(0)
                e3_transposed(1)
                pe.wait_ge(s["conv_evac"], PAIRS * b + 2)
                project_convolved(range(2, 4))
                for p in (2, 3):
                    pe.wait_ge(s["e3_exp"], PAIRS * b + (p + 1))
                    pe.wait_ge(s["e3T_evac_v"], 2 * b + (p - 1))
                    e3_transposed(p)
                project_convolved(range(4, 6))
                pe.wait_ge(s["e3T_evac"], 2 * b + 2)
                for p in range(PAIRS):
                    for i in range(TPB):
                        mm = pe.matmul(bank[4][:, p * P:(p + 1) * P], vb[:, i, p * P:(p + 1) * P],
                                       e3T[:, i, p, :], start=(i == 0), stop=(i == TPB - 1))
                mm.then_inc(s["uT_mm"], 1)
                pe.wait_ge(s["conv_evac"], PAIRS * b + 3)
                a1_transposed(0)
                a1_transposed(1)
                pe.wait_ge(s["uT_evac"], 2 * b + 2)
                pe.wait_ge(s["conv_evac"], PAIRS * b + PAIRS)
                settle(pe)
                for hd in range(HEADS):
                    r, p = half(hd), hd // 2
                    mm = pe.matmul(bank[3][r, p * P:(p + 1) * P], uTb[r, p, :], wo[r, p, :], start=True, stop=True)
                mm.then_inc(s["uw_mm"], 1)
                a1_transposed(2)
                project_convolved(range(6, 9))
                pe.wait_ge(s["uw_evac"], b + 1)
                need(pe, "z_staged", b)
                settle(pe)
                for hd in range(HEADS):
                    r, p = half(hd), hd // 2
                    mm = pe.matmul(bank[6][r, p * P:(p + 1) * P], ztb[r, p * M:(p + 1) * M], uw[r, p, :],
                                   start=True, stop=True)
                mm.then_inc(s["gw_mm"], 1)
                project_convolved(range(9, 12))
                pe.wait_ge(s["gw_evac"], b + 1)
                for i in range(TPB):
                    pe.wait_ge(s["a1T_evac"], TPB * b + (i + 1))
                    for p in range(PAIRS):
                        mm = pe.matmul(bank[5][:, i * P:(i + 1) * P], a1T[:, p, i * P:(i + 1) * P], gw[:, p, :],
                                       start=False, stop=(i == TPB - 1 and p == PAIRS - 1), skip_group_check=True)
                mm.then_inc(s["out1_mm"], 1)

            batches(pe, attend)
            ffn_transposes(B - 1, bank[7])
            ffn_distances(B - 1, bank[7])

            def tile_products(it, k):
                tau = TPB * it + k
                first = isinstance(it, int) and k == 0
                pe.wait_ge(s["xhi_done"], tau + 1)
                pe.wait_ge(s["xlo_done"], tau + 1)
                for c in range(CHUNKS):
                    d = c // 2
                    if first:
                        low_part_wait(pe, c)
                    if c % 2 == 0:
                        need(pe, "acc_step", DCH * tau + (d - 2))
                    else:
                        need(pe, "zact_done", DCH * tau + (d - 2))
                    bk = bank[(2 * k + c) % YBANKS]
                    n = slice(GRP * c, GRP * c + GRP)
                    pe.matmul(bk[:], xhi[:, k, :], v_hi[:, n, :], start=True, stop=False)
                    pe.matmul(bk[:], xhi[:, k, :], v_lo[:, n, :], start=False, stop=False)
                    pe.matmul(bk[:], xlo[:, k, :], v_hi[:, n, :], start=False, stop=True).then_inc(s["y_done_f"], 1)
                    if c == 14 and not first:
                        turn_out(tau - 1, (k - 1) % TPB)
                    if c == 22 and not first:
                        project_out(tau - 1)

            def turn_out(tau, k):
                pe.wait_ge(s["o_sum_done"], tau + 1)
                need(pe, "oT_evac", tau)
                pe.transpose(bank[6][:, 0:P], o_sum[:, k, :], ident[:]).then_inc(s["oT_mm"], 1)

            def project_out(tau):
                pe.wait_ge(s["oT_evac"], tau + 1)
                need(pe, "fin_done", tau)
                pe.matmul(bank[7][:, 0:P], oT, outWT[:], start=True, stop=True).then_inc(s["o_mm"], 1)

            def three(it):
                for k in range(TPB):
                    tile_products(it, k)
            rounds(pe, B, three)
            turn_out(TILES - 1, TPB - 1)
            project_out(TILES - 1)

        @block.scalar
        def _(act):
            act.wait_ge(s["ld_vec"], 16 * 4)
            for b in range(B):
                act.wait_ge(s["tok_mm"], b + 1)
                act.activation(hT[:, b, PAD:NP], bank[b][:, 0:T], ACT.Relu, bias=vec[:, 0:1]).then_inc(s["relu_done"], 1)
            act.wait_ge(s["bn_step"], B + 2)
            act.activation(bnr[:, 1:2], bnr[:, 0:1], ACT.Sqrt).then_inc(s["bn_root"], 1)
            for b in range(B):
                act.wait_ge(s["hT_mm"], b + 1)
                act.activation(h[:, TPB * b:TPB * (b + 1), :].rearrange("p i c -> p (i c)"), bank[b][:, 0:NP],
                               ACT.Copy).then_inc(s["h_copied"], 1)
            for n, step in enumerate((1, 2, 6, 10)):
                act.wait_ge(s["ln_step"], step)
                act.activation(sq[:, part(n)], tsm[:, part(n)], ACT.Sqrt).then_inc(s["ln_root"], 1)
            for b in range(1, B, 2):
                act.wait_ge(s["ln_step"], 13 if b < B // 2 else 16)
                act.wait_ge(s["h_copied"], b + 1)
                for i in range(TPB):
                    t = TPB * b + i
                    ins = act.activation(yn[:, b, i, :], h[:, t, :], ACT.Identity, bias=nm1[:, t:t + 1],
                                         scale=r1[:, t:t + 1])
                ins.then_inc(s["yn_act"], 1)
            for b in range(B):
                act.wait_ge(s["y_mm"], b + 1)
                act.activation(yT[:, b, PAD:NP], bank[b][:, PAD:NP], ACT.Identity, bias=vec[:, 2:3],
                               scale=vec[:, 1:2]).then_inc(s["y_evac"], 1)
            for k in range(2 * PAIRS):
                act.wait_ge(s["qk_mm"], k + 1)
                dst, scale = landmarks_to(0, k)
                act.activation(dst, bank[k][half(0), :], ACT.Copy, scale=scale).then_inc(s["qk_even"], 1)
            for b in range(B):
                act.wait_ge(s["sm2_step"], 2 * (b + 1))
                act.activation(xa[:, b, :], xa[:, b, :], ACT.Exp).then_inc(s["xa_exp"], 1)

            def folded(k):
                act.wait_ge(s["fold_mm"], k + 1)
                dst, scale = (Aq, SCALE) if k < HEADS else (Bk, 1.0)
                act.activation(dst[:, :, k % HEADS, :], bank[k % 8][:].rearrange("p (b m) -> p b m", m=M),
                               ACT.Copy, scale=scale).then_inc(s["fold_evac"], 1)
            for k in range(HEADS):
                folded(k)
            for b in range(B):
                act.wait_ge(s["xaT_mm"], b + 1)
                act.activation(xaT[:, b, :], bank[b][:, 0:PM], ACT.Copy).then_inc(s["xaT_evac"], 1)
            for k in range(HEADS, 2 * HEADS):
                folded(k)
            act.wait_ge(s["cmax_step"], 2 * B + 4)
            for b in range(B):
                act.activation(SZ[:, b, :, 1, :], by_pair(xa[:, b, :]), ACT.Copy, scale=crc[:, 1:2])

            def in_pairs(b):
                return bank[b][:].rearrange("p (a x m) -> p a x m", x=2, m=M)

            def even_heads(b):
                act.activation(Sb[half(0), b, :, 0:M], in_pairs(b)[half(0), :, 0, :], ACT.Copy)

            def pinv(j, last):
                for b in range(B):
                    act.wait_ge(s["S_mm"], STEPS * j * B + (b + 1))
                    even_heads(b)
                    act.activation(SZ[:, b, :, 0, :], in_pairs(b)[:, :, 0, :], ACT.Copy).then_inc(s["S_done"], 1)
                if last:
                    act.wait_ge(s["hs_done"], 2)
                    for b in range(B):
                        for t in range(TPB * b, TPB * (b + 1)):
                            ins = act.activation(h[:, t, :], h[:, t, :], ACT.Identity, bias=nm0[:, t:t + 1],
                                                 scale=r0p[:, t:t + 1])
                        ins.then_inc(s["h_twice"], 1)

                def step(n):
                    for b in range(B):
                        act.wait_ge(s["S_mm"], n * B + (B + b + 1))
                        even_heads(b)
                        act.activation(SZ[:, b], in_pairs(b), ACT.Copy).then_inc(s["S_done"], 1)
                in_round(act, j, step)
                for b in range(B):
                    act.wait_ge(s["z_mm"], j * B + (b + 1))
                    if last:
                        act.activation(by_pair(ztt[:, b, :]), in_pairs(b)[:, :, 1, :], ACT.Copy)\
                            .then_inc(s["z_done"], 1)
                    else:
                        even_heads(b)
                        act.activation(SZ[:, b, :, 1, :], in_pairs(b)[:, :, 1, :], ACT.Copy).then_inc(s["zt_done"], 1)
                if not last:
                    for b in range(B):
                        act.wait_ge(s["zb_mm"], j * B + (b + 1))
                        act.activation(Pb[:, b].rearrange("p a m -> p (a m)"), bank[b][:], ACT.Copy)\
                            .then_inc(s["zb_done"], 1)
            for j in range(ROUNDS):
                pinv(j, j == ROUNDS - 1)
            act.wait_ge(s["fold_evac"], 2 * HEADS)
            act.activation(y_hi, yT[:, 0, :], ACT.Copy)
            act.activation(A_hi, Aq[:, 0].rearrange("p h m -> p (h m)"), ACT.Copy).then_inc(s["first_hi"], 1)
            act.activation(wv_hi, wv, ACT.Copy).then_inc(s["first_hi"], 1)

            def ffn_root(c):
                act.wait_ge(s["f_var_done"], c + 1)
                act.activation(f_sd[:], f_var[:], ACT.Sqrt).then_inc(s["f_root"], 1)

            def ffn_norm(c):
                act.wait_ge(s["f_norm"], c + 1)
                for i in range(TPB):
                    ins = act.activation(u_tok[:, i, :], h[:, bass.ds(TPB * c + i, 1), :].rearrange("p a c -> p (a c)"),
                                         ACT.Identity, bias=f_nmr[:, i:i + 1], scale=f_r[:, i:i + 1])
                ins.then_inc(s["u_done"], 1)

            def ffn_transposed(c, at=bank[0]):
                act.wait_ge(s["u_mm"], c + 1)
                need(act, "uT_done", c)
                act.activation(uTs[:].rearrange("p i c -> p (i c)"), at[:, 0:NP], ACT.Copy)\
                    .then_inc(s["uTs_done"], 1)

            def ffn_distance_root(c):
                act.wait_ge(s["d2_done"], c + 1)
                act.activation(fa[:], fa[:], ACT.Sqrt).then_inc(s["d_root"], 1)

            def ffn_exp(c):
                act.wait_ge(s["f_max"], c + 1)
                for i in range(TPB):
                    ins = act.activation(fa[:, i, :], fa[:, i, :], ACT.Exp, bias=f_mx[:, i:i + 1],
                                         accum_out=f_tot[:, i:i + 1])
                ins.then_inc(s["f_exp"], 1)

            def high_part(chunks):
                for c in chunks:
                    n = slice(GRP * c, GRP * c + GRP)
                    act.activation(v_hi[:, n, :], v_raw[:, n, :], ACT.Copy).then_inc(s["vhi_done"], 1)

            def attend(b):
                def split(n, chunks):
                    if isinstance(b, int) and b == n:
                        high_part(chunks)

                def values(i):
                    act.wait_ge(s["v_mm"], TPB * b + (i + 1))
                    act.activation(vb[:, i, :], bank[3 + i][:], ACT.Copy).then_inc(s["v_evac"], 1)

                def convolved(p):
                    act.wait_ge(s["conv_mm"], PAIRS * b + (p + 1))
                    act.activation(resT[:, p, :], bank[CONV_BANK[p]][:, 0:NP], ACT.Copy).then_inc(s["conv_evac"], 1)

                def e3_exponentials(p):
                    act.wait_ge(s["e3_max"], PAIRS * b + (p + 1))
                    act.activation(e3[:, p, :], bank[SIM3_BANK[p]][:, 0:NP], ACT.Exp, bias=m3[:, p:p + 1],
                                   accum_out=s3[:, p:p + 1]).then_inc(s["e3_exp"], 1)

                def e1_exponentials(i):
                    act.wait_ge(s["s1_sub"], 2 * TPB * b + (2 * i + 2))
                    act.activation(e1[:, i], e1[:, i], ACT.Exp).then_inc(s["e1_exp"], 1)

                def e3_evacuated(p):
                    act.wait_ge(s["e3T_mm"], PAIRS * b + (p + 1))
                    act.activation(e3T[:, :, p, :], bank[6 + p % 2][:, 0:NP].rearrange("p (i m) -> p i m", m=P),
                                   ACT.Copy).then_inc(s["e3T_evac"], 1)

                def a1_evacuated(i):
                    act.wait_ge(s["a1T_mm"], TPB * b + (i + 1))
                    act.activation(a1T[:, :, i * P:(i + 1) * P], bank[i][:].rearrange("p (a t) -> p a t", t=P),
                                   ACT.Copy).then_inc(s["a1T_evac"], 1)

                if has_before(b):
                    ffn_root(b - 1)
                values(0)
                if has_before(b):
                    ffn_norm(b - 1)
                values(1)
                values(2)
                if has_before(b):
                    ffn_transposed(b - 1)
                convolved(0)
                if has_before(b):
                    ffn_distance_root(b - 1)
                e3_exponentials(0)
                e3_exponentials(1)
                convolved(1)
                e3_exponentials(2)
                e3_exponentials(3)
                e1_exponentials(0)
                e3_evacuated(2)
                e3_evacuated(3)
                convolved(2)
                convolved(3)
                e1_exponentials(1)
                e1_exponentials(2)
                split(B - 1, range(3, 8))
                for i in range(TPB):
                    a1_evacuated(i)
                act.wait_ge(s["gw_mm"], b + 1)
                act.activation(gw.rearrange("p a c -> p (a c)"), bank[6][:], ACT.Copy).then_inc(s["gw_evac"], 1)
                if has_before(b):
                    ffn_exp(b - 1)
                if isinstance(b, int) and b == B - 2:
                    act.wait_ge(s["ld_v"], 16 * 8)
                    act.wait_ge(s["staged"], B - 1)
                    act.wait_ge(s["z_staged"], B - 1)
                split(B - 2, range(0, 3))
                split(B - 1, range(8, 11))

            batches(act, attend)

            act.wait_ge(s["out1_mm"], B)

            def stage(tau, k):
                act.activation(xhi[:, k, :], uT[:, bass.ds(tau, 1), :].rearrange("p a c -> p (a c)"), ACT.Copy)\
                    .then_inc(s["xhi_done"], 1)
            stage(0, 0)
            high_part(range(11, 13))
            ffn_root(B - 1)
            ffn_norm(B - 1)
            high_part(range(13, EARLY))
            ffn_transposed(B - 1, bank[7])
            for m in range(AHEAD):
                high_part(split_during(m))
            ffn_distance_root(B - 1)
            act.wait_ge(s["uT_done"], B)
            act.wait_ge(s["pad_tile"], 1)

            def weigh(it, k):
                tau = TPB * it + k
                act.wait_ge(s["ast_done"], tau + 1)
                for m in range(DCH):
                    c = 2 * m + 1
                    if first_tile(it, k):
                        if m >= AHEAD:
                            high_part(split_during(m))
                        if m == 7:
                            ffn_exp(B - 1)
                    act.wait_ge(s["y_done_f"], CHUNKS * tau + (c + 1))
                    need(act, "accp_step", (DCH - 1) * tau + (max(m - ZR, 1) if m >= ZR else m + 1 - ZR))
                    for j in range(GRP):
                        n = GRP * c + j
                        ins = act.activation(zring[:, m % ZR, j * P:(j + 1) * P],
                                             bank[(2 * k + c) % YBANKS][:, j * P:(j + 1) * P], ACT.Copy,
                                             scale=a_st[:, k, n:n + 1])
                    ins.then_inc(s["zact_done"], 1)
                    if m == 8 and not (isinstance(it, int) and k == 0):
                        turn_out(tau - 1)
                    if m == 10:
                        need(act, "y_done_f", CHUNKS * (tau - 1))
                        stage(tau + 1, (k + 1) % TPB)

            def turn_out(tau):
                act.wait_ge(s["oT_mm"], tau + 1)
                need(act, "o_mm", tau)
                act.activation(oT, bank[6][:, 0:P], ACT.Copy).then_inc(s["oT_evac"], 1)

            def three(it):
                for k in range(TPB):
                    weigh(it, k)
            rounds(act, B, three)
            turn_out(TILES - 1)

        @block.gpsimd
        def _(pool):
            pool.memset(hT[:, :, 0:PAD], 0.0).then_inc(s["hpad_zero"], 1)
            pool.memset(ones, 1.0).then_inc(s["p2_in"], 1)
            pool.memset(yT[:, :, 0:PAD], 0.0).then_inc(s["pads_zero"], 1)
            pool.wait_ge(s["pads_zero"], 1)
            for x in range(2):
                pool.memset(klX[x][half(1 - x)], 0.0)
                ins = pool.memset(qlX[x][half(1 - x)], 0.0)
            ins.then_inc(s["zeros_kq"], 1)
            pool.wait_ge(s["ld_id"], 16)
            for j, value in enumerate((7.0, 15.0, 3.25)):
                for r in (half(0), half(1)):
                    ins = pool.tensor_scalar(eyes[r, j, :], ident[r, r], value, None, ALU.mult)
            ins.then_inc(s["eyes_done"], 1)
            pool.wait_ge(s["eyes_done"], 1)
            pool.wait_ge(s["y_mm"], B)
            pool.wait_ge(s["hs_done"], 2)
            for blocks in (Pb, Sb):
                for x in range(2):
                    ins = pool.memset(blocks[half(x), :, :, (1 - x) * M:(2 - x) * M], 0.0)
            ins.then_inc(s["zeros_b"], 1)
            pool.wait_ge(s["zeros_b"], 1)
            for b in range(B):
                pool.wait_ge(s["xa_sum"], 2 * (b + 1))
                pool.tensor_tensor(by_pair(xa[:, b, :]), by_pair(xa[:, b, :]),
                                   rsx[:, 1, b * PAIRS:(b + 1) * PAIRS, None].to_broadcast([P, PAIRS, M]),
                                   ALU.mult).then_inc(s["xa_done"], 1)
            pool.wait_ge(s["cmax_step"], 2 * B + 2)
            pool.partition_all_reduce(cmxa[:], cmx[:], P, RMAX).then_inc(s["cmax_all"], 1)

            def of_batch(x, b):
                flat = x[:, bass.ds(b, 1)]
                return flat.rearrange("p a h m -> p (a h m)") if x is not yT else flat.rearrange("p a t -> p (a t)")

            def high(dst, src):
                pool.tensor_copy(dst, src).then_inc(s["hi_done"], 1)

            def low(dst, src, hi):
                return pool.tensor_tensor(dst, src, hi.bitcast(F32), ALU.subtract)

            def tiles_of(x, c):
                return x[:, bass.ds(TPB * c, TPB), :]

            def ffn_keep(c):
                pool.wait_ge(s["uTs_done"], c + 1)
                pool.tensor_copy(tiles_of(uT, c), uTs[:]).then_inc(s["uT_done"], 1)

            def ffn_bias(c):
                pool.tensor_tensor(tiles_of(h, c), tiles_of(h, c), outb[:, None, :].to_broadcast([P, TPB, P]),
                                   ALU.add).then_inc(s["hb_done"], 1)

            def ffn_scale(c):
                pool.wait_ge(s["f_inv"], c + 1)
                pool.tensor_tensor(fa[:], fa[:], scrow[:, None, :].to_broadcast([P, TPB, P]), ALU.mult)\
                    .then_inc(s["f_scaled"], 1)

            def ffn_normalise(c):
                pool.wait_ge(s["f_sum"], c + 1)
                pool.tensor_tensor(tiles_of(at_all, c), fa[:], f_rt[:, :, None].to_broadcast([P, TPB, P]), ALU.mult)\
                    .then_inc(s["a_done"], 1)

            def low_part(chunks):
                for c in chunks:
                    if pool_takes(c):
                        n = slice(GRP * c, GRP * c + GRP)
                        pool.wait_ge(s["vhi_done"], c + 1)
                        pool.tensor_tensor(v_lo[:, n, :], v_raw[:, n, :], v_hi[:, n, :].bitcast(F32), ALU.subtract)\
                            .then_inc(s["vlop_done"], 1)

            def attend(b):
                if has_before(b):
                    ffn_keep(b - 1)
                if has_after(b):
                    pool.wait_ge(s["sim3_mm"], PAIRS * b + PAIRS)
                    high(y_hi, of_batch(yT, b + 1))
                    high(A_hi, of_batch(Aq, b + 1))
                    high(B_hi, of_batch(Bk, b + 1))
                    pool.wait_ge(s["hi_done"], 3 * b + 3)
                    settle(pool)
                    low(y_lo, of_batch(yT, b + 1), y_hi)
                for i in range(TPB):
                    pool.wait_ge(s["s1_norm"], 2 * TPB * b + (2 * i + 2))
                    pool.tensor_tensor(e1[:, i], e1[:, i], rr1[:, i, :, None].to_broadcast([P, HEADS, M]), ALU.mult)\
                        .then_inc(s["a1_norm"], 1)
                if has_before(b):
                    ffn_scale(b - 1)
                if has_after(b):
                    low(A_lo, of_batch(Aq, b + 1), A_hi)
                    low(B_lo, of_batch(Bk, b + 1), B_hi).then_inc(s["staged"], 1)
                if has_before(b):
                    ffn_bias(b - 1)
                if has_after(b):
                    pool.wait_ge(s["gw_mm"], b + 1)
                    pool.tensor_copy(ztb, ztt[:, bass.ds(b + 1, 1), :].rearrange("p a m -> p (a m)"))\
                        .then_inc(s["z_staged"], 1)
                if has_before(b):
                    ffn_normalise(b - 1)
                if isinstance(b, int) and b == B - 2:
                    low_part(range(0, 3))
                if isinstance(b, int) and b == B - 1:
                    low_part(range(3, 8))

            pool.wait_ge(s["ld_vec"], 16 * 4)
            for b in range(B):
                pool.wait_ge(s["h_twice"], b + 1)
                blk = slice(TPB * b, TPB * (b + 1))
                pool.tensor_tensor(h[:, blk, :], h[:, blk, :], bout[:, None, :].to_broadcast([P, TPB, P]), ALU.add)\
                    .then_inc(s["h_plus"], 1)
            pool.wait_ge(s["z_done"], B)
            batches(pool, attend)
            pool.memset(uT[:, TILES, :], 0.0)
            pool.memset(at_all[:, TILES, :], 0.0).then_inc(s["pad_tile"], 1)

            def stage_a(tau, k):
                pool.tensor_copy(a_st[:, k, :], at_all[:, bass.ds(tau, 1), :].rearrange("p a c -> p (a c)"))\
                    .then_inc(s["ast_done"], 1)

            def add_up(it, k):
                tau = TPB * it + k
                part = acc[:, k, 8:12, :].rearrange("p j c -> p (j c)")
                need(pool, "o_sum_done", tau - 2)
                for m in range(1, DCH):
                    if first_tile(it, k):
                        if m == 1:
                            low_part(split_during(0))
                        low_part(split_during(m))
                        if m == 3:
                            ffn_scale(B - 1)
                        if m == 6:
                            ffn_bias(B - 1)
                        if m == 9:
                            ffn_normalise(B - 1)
                    pool.wait_ge(s["zact_done"], DCH * tau + (m + 1))
                    if m == 1:
                        ins = pool.tensor_tensor(part, zring[:, 0, :], zring[:, 1, :], ALU.add)
                    else:
                        pool.wait_ge(s["accp_step"], (DCH - 1) * tau + (m - 1))
                        ins = pool.tensor_tensor(part, part, zring[:, m % ZR, :], ALU.add)
                    ins.then_inc(s["accp_step"], 1)
                    if m == 8:
                        need(pool, "acc_step", DCH * (tau - 1))
                        need(pool, "zact_done", DCH * (tau - 1))
                        stage_a(tau + 1, (k + 1) % TPB)
            pool.wait_ge(s["a_done"], 1)
            pool.wait_ge(s["out1_mm"], B)
            stage_a(0, 0)
            low_part(range(8, 12))
            ffn_keep(B - 1)
            low_part(range(12, EARLY))

            def three(it):
                for k in range(TPB):
                    add_up(it, k)
            rounds(pool, B, three)

        @block.vector
        def _(dve):
            dve.wait_ge(s["ld_ffn"], 16 * 4)
            dve.tensor_scalar(posT2[:], posT, -2.0, None, ALU.mult).then_inc(s["p2_in"], 1)
            dve.tensor_tensor(possq, posT, posT, ALU.mult).then_inc(s["p2_in"], 1)
            dve.wait_ge(s["hpad_zero"], 1)
            for b in range(B):
                dve.wait_ge(s["relu_done"], b + 1)
                dve.bn_stats(bnst[:, b, :], hT[:, b, PAD:NP]).then_inc(s["bn_step"], 1)
            dve.wait_ge(s["bn_step"], B)
            dve.bn_aggr(bnmv[:], bnst.rearrange("p b k -> p (b k)")).then_inc(s["bn_step"], 1)
            dve.wait_ge(s["bn_step"], B + 1)
            dve.tensor_scalar(bnr[:, 0:1], bnmv[:, 1:2], EPS, None, ALU.add).then_inc(s["bn_step"], 1)
            dve.wait_ge(s["p2_mm"], 1)
            dve.tensor_copy(p2row[:], bank[0][:, 0:P]).then_inc(s["p2_done"], 1)
            dve.wait_ge(s["bn_root"], 1)
            dve.reciprocal(bnr[:, 0:1], bnr[:, 1:2]).then_inc(s["bn_step"], 1)
            dve.wait_ge(s["bn_step"], B + 3)
            for b in range(B):
                dve.tensor_scalar(hT[:, b, PAD:NP], hT[:, b, PAD:NP], bnmv[:, 0:1], bnr[:, 0:1],
                                  ALU.subtract, ALU.mult).then_inc(s["hn_done"], 1)
            ln_count = [0]

            def ln(ins, wait=True):
                ln_count[0] += 1
                ins.then_inc(s["ln_step"], 1)
                if wait:
                    dve.wait_ge(s["ln_step"], ln_count[0])
            for n in range(2):
                for b in range(B // 2 * n, B // 2 * (n + 1)):
                    dve.wait_ge(s["h_copied"], b + 1)
                    for t in range(TPB * b, TPB * (b + 1)):
                        ins = dve.bn_stats(st6[:, t, :], h[:, t, :])
                ins.then_inc(s["stat_step"], 1)
                dve.wait_ge(s["stat_step"], 2 * n + 1)
                for t in range(part(n).start, part(n).stop):
                    ins = dve.bn_aggr(mv[:, t, :], st6[:, t, :])
                ins.then_inc(s["stat_step"], 1)
                dve.wait_ge(s["stat_step"], 2 * n + 2)
                ln(dve.tensor_scalar(tsm[:, part(n)], mv[:, part(n), 1], EPS, None, ALU.add), wait=False)
            for n in range(2):
                r, t2 = r0[:, part(n)], tsm[:, part(n)]
                dve.wait_ge(s["ln_root"], n + 1)
                ln(dve.reciprocal(r, sq[:, part(n)]))
                ln(dve.tensor_tensor(t2, r, r, ALU.mult))
                ln(dve.tensor_tensor(t2, t2, mv[:, part(n), 1], ALU.mult))
                ln(dve.tensor_scalar(t2, t2, EPS, None, ALU.add), wait=False)
            for n in range(2):
                r = r1[:, part(n)]
                dve.wait_ge(s["ln_root"], n + 3)
                ln(dve.reciprocal(r, sq[:, part(n)]))
                ln(dve.tensor_tensor(r, r0[:, part(n)], r, ALU.mult))
                ln(dve.scalar_tensor_tensor(nm1[:, part(n)], mv[:, part(n), 0], -1.0, r, ALU.mult, ALU.mult), wait=False)
                for b in range(B // 2 * n, B // 2 * (n + 1), 2):
                    dve.wait_ge(s["hT_mm"], b + 1)
                    for i in range(TPB):
                        t = TPB * b + i
                        ins = dve.tensor_scalar(yn[:, b, i, :], h[:, t, :], mv[:, t, 0:1], r1[:, t:t + 1],
                                                ALU.subtract, ALU.mult)
                    ins.then_inc(s["yn_done"], 1)
            dve.scalar_tensor_tensor(nm0, mv[:, :, 0], -1.0, r0, ALU.mult, ALU.mult).then_inc(s["hs_done"], 1)
            dve.tensor_scalar(r0p, r0, 1.0, None, ALU.add).then_inc(s["hs_done"], 1)
            dve.wait_ge(s["pads_zero"], 1)
            for b in range(B):
                dve.wait_ge(s["y_evac"], b + 1)
                dve.tensor_reduce(ylT[:, b * M:(b + 1) * M], yT[:, b, :].rearrange("p (m l) -> p m l", l=L),
                                  AX_X, ALU.add).then_inc(s["yl_done"], 1)
            for k in range(2 * PAIRS):
                dve.wait_ge(s["qk_mm"], k + 1)
                dst, scale = landmarks_to(1, k)
                dve.tensor_scalar(dst, bank[k][half(1), :], scale, None, ALU.mult).then_inc(s["qk_odd"], 1)
            for b in range(B):
                dve.wait_ge(s["sim2_mm"], b + 1)
                sims = by_pair(bank[b][:, 0:PM])
                top = rsx[:, 0, b * PAIRS:(b + 1) * PAIRS]
                dve.tensor_reduce(top, sims, AX_X, ALU.max).then_inc(s["sm2_step"], 1)
                dve.wait_ge(s["sm2_step"], 2 * b + 1)
                dve.tensor_tensor(by_pair(xa[:, b, :]), sims, top[:, :, None].to_broadcast([P, PAIRS, M]),
                                  ALU.subtract).then_inc(s["sm2_step"], 1)
            for b in range(B):
                dve.wait_ge(s["xa_exp"], b + 1)
                tot = rsx[:, 1, b * PAIRS:(b + 1) * PAIRS]
                dve.tensor_reduce(tot, by_pair(xa[:, b, :]), AX_X, ALU.add).then_inc(s["xa_sum"], 1)
                dve.wait_ge(s["xa_sum"], 2 * b + 1)
                dve.reciprocal(tot, tot).then_inc(s["xa_sum"], 1)
            for b in range(B):
                dve.wait_ge(s["xa_done"], b + 1)
                dve.tensor_reduce(rsx[:, 0, b * PAIRS:(b + 1) * PAIRS], by_pair(xa[:, b, :]), AX_X, ALU.add)\
                    .then_inc(s["cmax_step"], 1)
            for b in range(B):
                dve.wait_ge(s["xaT_evac"], b + 1)
                dve.tensor_reduce(rsx[:, 1, b * PAIRS:(b + 1) * PAIRS], by_pair(xaT[:, b, :]), AX_X, ALU.add)\
                    .then_inc(s["cmax_step"], 1)
            dve.wait_ge(s["cmax_step"], 2 * B)
            dve.tensor_reduce(cmx[:], rsx[:], AX_X, ALU.max).then_inc(s["cmax_step"], 1)
            dve.wait_ge(s["cmax_step"], 2 * B + 1)
            dve.tensor_copy(crc[:], cmx[:]).then_inc(s["cmax_step"], 1)
            dve.wait_ge(s["cmax_all"], 1)
            dve.tensor_tensor(crc[:, 0:1], cmxa[:, 0:1], cmxa[:, 1:2], ALU.mult).then_inc(s["cmax_step"], 1)
            dve.wait_ge(s["cmax_step"], 2 * B + 3)
            dve.reciprocal(crc[:, 1:2], crc[:, 0:1]).then_inc(s["cmax_step"], 1)
            dve.wait_ge(s["cmax_step"], 2 * B + 4)
            for b in range(B):
                for x in range(2):
                    ins = dve.tensor_scalar(Pb[half(x), b, :, x * M:(x + 1) * M], by_pair(xaT[half(x), b, :]),
                                            crc[half(x), 1:2], None, ALU.mult)
                ins.then_inc(s["zb_done"], 1)

            def times_eye(j, r=slice(0, P)):
                return eyes[r, j, None, :].to_broadcast([r.stop - r.start, PAIRS, M])

            def first_of(b, r=slice(0, P)):
                return bank[b][r, :].rearrange("p (a m) -> p a m", m=P)[:, :, 0:M]

            def odd_heads(b, which):
                return dve.tensor_copy(Sb[half(1), b, :, M:P], SZ[half(1), b, :, which, :])

            def polynomial(n):
                for b in range(B):
                    dve.wait_ge(s["S_done"], n * B + (b + 1))
                    odd_heads(b, 0)
                    dve.tensor_tensor(by_pair(Tm[:, b, :]), times_eye(0), SZ[:, b, :, 0, :], ALU.subtract)\
                        .then_inc(s["T1_done"], 1)
                for b in range(B):
                    dve.wait_ge(s["T2_mm"], n * B + (b + 1))
                    dve.tensor_tensor(by_pair(Tm[:, b, :]), times_eye(1), first_of(b), ALU.subtract)\
                        .then_inc(s["T2_done"], 1)
                for b in range(B):
                    dve.wait_ge(s["P_mm"], n * B + (b + 1))
                    for x in range(2):
                        ins = dve.scalar_tensor_tensor(Pb[half(x), b, :, x * M:(x + 1) * M], first_of(b, half(x)),
                                                       -0.25, times_eye(2, half(x)), ALU.mult, ALU.add)
                    ins.then_inc(s["P_done"], 1)

            def pinv(j, last):
                in_round(dve, j, polynomial)
                polynomial(STEPS * j + STEPS - 1)
                if not last:
                    for b in range(B):
                        dve.wait_ge(s["zt_done"], j * B + (b + 1))
                        odd_heads(b, 1).then_inc(s["zt_odd"], 1)
            dve.wait_ge(s["eyes_done"], 1)
            for j in range(ROUNDS):
                pinv(j, j == ROUNDS - 1)

            F_STEPS = 7

            def ffn_link(ins):
                ins.then_inc(s["f_step"], 1)

            def ffn_after(c, k):
                dve.wait_ge(s["f_step"], F_STEPS * c + k)

            def add_attention(c):
                dve.wait_ge(s["out1_mm"], c + 1)
                blk = h[:, bass.ds(TPB * c, TPB), :]
                dve.tensor_tensor(blk, blk, bank[5][:, 0:NP].rearrange("p (i c) -> p i c", c=P), ALU.add)\
                    .then_inc(s["h1_done"], 1)

            def one_tile(x, c, i):
                return x[:, bass.ds(TPB * c + i, 1), :].rearrange("p a c -> p (a c)")

            def ffn_stats(c):
                dve.wait_ge(s["h1_done"], c + 1)
                settle(dve)
                for i in range(TPB):
                    ins = dve.bn_stats(f_st6[:, i, :], one_tile(h, c, i))
                ffn_link(ins)

            def ffn_aggregate(c):
                ffn_after(c, 1)
                settle(dve)
                for i in range(TPB):
                    ins = dve.bn_aggr(f_mv[:, i, :], f_st6[:, i, :])
                ffn_link(ins)

            def ffn_variance(c):
                ffn_after(c, 2)
                dve.tensor_scalar(f_var[:], f_mv[:, :, 1], EPS, None, ALU.add).then_inc(s["f_var_done"], 1)

            def ffn_factors(c):
                dve.wait_ge(s["f_root"], c + 1)
                ffn_link(dve.reciprocal(f_r[:], f_sd[:]))
                ffn_after(c, 3)
                dve.scalar_tensor_tensor(f_nmr[:], f_mv[:, :, 0], -1.0, f_r[:], ALU.mult, ALU.mult)\
                    .then_inc(s["f_norm"], 1)

            def ffn_length(c):
                ffn_link(dve.tensor_tensor(f_vr[:], f_mv[:, :, 1], f_r[:], ALU.mult))
                ffn_after(c, 4)
                dve.scalar_tensor_tensor(u2[:], f_vr[:], float(P), f_r[:], ALU.mult, ALU.mult)\
                    .then_inc(s["u2_done"], 1)

            def ffn_squared_distances(c, at=bank[0]):
                dve.wait_ge(s["u2_done"], c + 1)
                need(dve, "a_done", c)
                dve.wait_ge(s["d_mm"], c + 1)
                for i in range(TPB):
                    ins = dve.scalar_tensor_tensor(fa[:, i, :], at[:, i * P:(i + 1) * P], u2[:, i:i + 1],
                                                   p2row[:], ALU.add, ALU.add)
                ffn_link(ins)
                ffn_after(c, 5)
                dve.tensor_scalar(fa[:], fa[:], 0.0, None, ALU.max).then_inc(s["d2_done"], 1)

            def ffn_shift(c):
                dve.wait_ge(s["d_root"], c + 1)
                ffn_link(dve.tensor_scalar(fa[:], fa[:], 0.1, None, ALU.add))

            def ffn_invert(c, i):
                ffn_after(c, 6)
                ins = dve.reciprocal(fa[:, i, :], fa[:, i, :])
                if i == TPB - 1:
                    ins.then_inc(s["f_inv"], 1)

            def ffn_maximum(c):
                dve.wait_ge(s["f_scaled"], c + 1)
                dve.tensor_reduce(f_mx[:], fa[:], AX_X, ALU.max, negate=True).then_inc(s["f_max"], 1)

            def ffn_total(c):
                dve.wait_ge(s["f_exp"], c + 1)
                ffn_link(dve.reciprocal(f_rt[:], f_tot[:]))
                ffn_after(c, 7)
                dve.sem_inc(s["f_sum"], 1)

            def attend(b):
                def sims(i):
                    return bank[i][:].rearrange("p (a m) -> p a m", m=M)

                def sim1_max(i):
                    dve.wait_ge(s["sim1_mm"], TPB * b + (i + 1))
                    dve.tensor_reduce(m1[:, i, :], sims(i), AX_X, ALU.max).then_inc(s["s1_sub"], 1)

                def sim1_less_max(i):
                    dve.wait_ge(s["s1_sub"], 2 * TPB * b + (2 * i + 1))
                    dve.tensor_tensor(e1[:, i], sims(i), m1[:, i, :, None].to_broadcast([P, HEADS, M]), ALU.subtract)\
                        .then_inc(s["s1_sub"], 1)

                def sim3_max(p):
                    dve.wait_ge(s["sim3_mm"], PAIRS * b + (p + 1))
                    dve.tensor_reduce(m3[:, p:p + 1], bank[SIM3_BANK[p]][:, 0:NP], AX_X, ALU.max, negate=True)\
                        .then_inc(s["e3_max"], 1)

                def e1_sum(i):
                    dve.wait_ge(s["e1_exp"], TPB * b + (i + 1))
                    dve.tensor_reduce(s1[:, i, :], e1[:, i], AX_X, ALU.add).then_inc(s["s1_norm"], 1)
                    dve.wait_ge(s["s1_norm"], 2 * TPB * b + (2 * i + 1))
                    dve.reciprocal(rr1[:, i, :], s1[:, i, :]).then_inc(s["s1_norm"], 1)

                before = has_before(b)
                c = b - 1
                if before:
                    add_attention(c)
                    ffn_stats(c)
                    ffn_aggregate(c)
                    ffn_variance(c)
                sim1_max(0)
                if before:
                    ffn_factors(c)
                sim1_less_max(0)
                sim1_max(1)
                sim1_less_max(1)
                if before:
                    ffn_length(c)
                sim1_max(2)
                sim1_less_max(2)
                sim3_max(0)
                if before:
                    ffn_squared_distances(c)
                sim3_max(1)
                sim3_max(2)
                sim3_max(3)
                if before:
                    ffn_shift(c)
                    ffn_invert(c, 0)
                for p in (0, 1):
                    dve.wait_ge(s["e3T_mm"], PAIRS * b + (p + 1))
                    dve.tensor_copy(e3T[:, :, p, :], bank[6 + p % 2][:, 0:NP].rearrange("p (i m) -> p i m", m=P))\
                        .then_inc(s["e3T_evac_v"], 1)
                e1_sum(0)
                if before:
                    ffn_invert(c, 1)
                e1_sum(1)
                e1_sum(2)
                dve.wait_ge(s["e3_exp"], PAIRS * b + PAIRS)
                dve.reciprocal(rr3, s3).then_inc(s["rr3_done"], 1)
                dve.wait_ge(s["uT_mm"], b + 1)
                for x in range(2):
                    dve.tensor_copy(uTb[half(x), :, :],
                                    bank[4][half(x), :].rearrange("p (a m) -> p a m", m=P)[:, :, x * M:(x + 1) * M])\
                        .then_inc(s["uT_evac"], 1)
                if before:
                    ffn_invert(c, 2)
                dve.wait_ge(s["uw_mm"], b + 1)
                dve.wait_ge(s["rr3_done"], b + 1)
                dve.tensor_tensor(uw, bank[3][:].rearrange("p (a c) -> p a c", c=P),
                                  rr3[:, :, None].to_broadcast([P, PAIRS, P]), ALU.mult).then_inc(s["uw_evac"], 1)
                if before:
                    ffn_maximum(c)
                    ffn_total(c)

            dve.wait_ge(s["z_done"], B)
            dve.tensor_copy(B_hi, Bk[:, 0].rearrange("p h m -> p (h m)")).then_inc(s["first_hi_v"], 1)
            dve.wait_ge(s["first_hi"], 1)
            dve.tensor_tensor(y_lo, yT[:, 0, :], y_hi.bitcast(F32), ALU.subtract)
            dve.tensor_tensor(A_lo, Aq[:, 0].rearrange("p h m -> p (h m)"), A_hi.bitcast(F32), ALU.subtract)\
                .then_inc(s["first_lo"], 1)
            dve.wait_ge(s["first_hi"], 2)
            dve.tensor_tensor(wv_lo, wv, wv_hi.bitcast(F32), ALU.subtract).then_inc(s["first_lo"], 1)
            dve.wait_ge(s["first_hi_v"], 1)
            dve.tensor_tensor(B_lo, Bk[:, 0].rearrange("p h m -> p (h m)"), B_hi.bitcast(F32), ALU.subtract)
            dve.tensor_copy(ztb, ztt[:, 0, :]).then_inc(s["first_lo"], 1)
            dve.wait_ge(s["h_plus"], B)
            batches(dve, attend)

            def low_part(chunks):
                for c in chunks:
                    if not pool_takes(c):
                        n = slice(GRP * c, GRP * c + GRP)
                        dve.wait_ge(s["vhi_done"], c + 1)
                        dve.tensor_tensor(v_lo[:, n, :], v_raw[:, n, :], v_hi[:, n, :].bitcast(F32), ALU.subtract)\
                            .then_inc(s["vlo_done"], 1)
            def stage(tau, k):
                dve.wait_ge(s["xhi_done"], tau + 1)
                dve.tensor_tensor(xlo[:, k, :], uT[:, bass.ds(tau, 1), :].rearrange("p a c -> p (a c)"),
                                  xhi[:, k, :].bitcast(F32), ALU.subtract).then_inc(s["xlo_done"], 1)
            add_attention(B - 1)
            ffn_stats(B - 1)
            ffn_aggregate(B - 1)
            ffn_variance(B - 1)
            stage(0, 0)
            low_part(range(0, 11))
            ffn_factors(B - 1)
            ffn_length(B - 1)
            low_part(range(11, EARLY))
            for d in range(AHEAD):
                low_part(split_during(d))
            ffn_squared_distances(B - 1, bank[7])
            dve.wait_ge(s["pad_tile"], 1)

            def weigh(it, k):
                tau = TPB * it + k
                first = isinstance(it, int) and k == 0
                dve.wait_ge(s["ast_done"], tau + 1)
                need(dve, "o_sum_done", tau - 2)
                for d in range(DCH):
                    c = 2 * d
                    if first_tile(it, k):
                        if d >= AHEAD:
                            low_part(split_during(d))
                        if d == 0:
                            ffn_shift(B - 1)
                        if d < TPB:
                            ffn_invert(B - 1, d)
                        if d == 5:
                            ffn_maximum(B - 1)
                        if d == 8:
                            ffn_total(B - 1)
                    dve.wait_ge(s["y_done_f"], CHUNKS * tau + (c + 1))
                    if d >= 2:
                        dve.wait_ge(s["acc_step"], DCH * tau + (d - 1))
                    for j in range(GRP):
                        y = bank[(2 * k + c) % YBANKS][:, j * P:(j + 1) * P]
                        to = acc[:, k, GRP * (d % 2) + j, :]
                        w = a_st[:, k, GRP * c + j:GRP * c + j + 1]
                        if d < 2:
                            ins = dve.tensor_scalar(to, y, w, None, ALU.mult)
                        else:
                            ins = dve.scalar_tensor_tensor(to, y, w, to, ALU.mult, ALU.add)
                    ins.then_inc(s["acc_step"], 1)
                    if d == 4 and not first:
                        sum_up(tau - 1, (k - 1) % TPB)
                    if d == 13 and not first:
                        finish(tau - 1, (k - 1) % TPB, it - 1 if k == 0 else it)
                    if d == 12:
                        need(dve, "y_done_f", CHUNKS * (tau - 1))
                        stage(tau + 1, (k + 1) % TPB)

            def sum_up(tau, k):
                dve.wait_ge(s["acc_step"], DCH * (tau + 1))
                dve.wait_ge(s["accp_step"], (DCH - 1) * (tau + 1))
                need(dve, "oT_mm", tau - 2)
                dve.tensor_reduce(o_sum[:, k, :], acc[:, k].rearrange("p j c -> p c j"), AX_X, ALU.add)\
                    .then_inc(s["o_sum_done"], 1)

            def finish(tau, k, it):
                if isinstance(it, int) and it == 0 and k == 0:
                    dve.wait_ge(s["a_done"], B)
                    dve.wait_ge(s["hb_done"], B)
                dve.wait_ge(s["o_mm"], tau + 1)
                need(dve, f"stored{k}", 16 * it)
                dve.tensor_tensor(o_fin[:, k, :], bank[7][:, 0:P],
                                  h[:, bass.ds(tau, 1), :].rearrange("p a c -> p (a c)"), ALU.add)\
                    .then_inc(s["fin_done"], 1)

            def three(it):
                for k in range(TPB):
                    weigh(it, k)
            rounds(dve, B, three)
            sum_up(TILES - 1, TPB - 1)
            finish(TILES - 1, TPB - 1, B - 1)


def kernel(**inputs):
    import numpy as np
    import concourse.bacc as bacc
    from concourse.bass_utils import run_bass_kernel_spmd

    x = {n: np.asarray(a) for n, a in inputs.items()}
    w_qkv = x["L0_attn_w_qkv"]
    taps = x["L0_attn_w_res"].reshape(HEADS, TAPS)
    padded = np.zeros((HEADS, WPAD), np.float32)
    padded[:, P - 1:P - 1 + TAPS] = taps[:, ::-1]
    band = np.stack([padded[:, P - 1 - p:P - 1 - p + CW] for p in range(P)])
    arrays = {
        "xt": x["x"].transpose(2, 0, 1),
        "tok_wt": x["L0_tok_W"].T,
        "tok_b": x["L0_tok_b"].reshape(P, 1),
        "ln_g": x["L0_attn_ln_g"].reshape(P, 1),
        "ln_b": x["L0_attn_ln_b"].reshape(P, 1),
        "w_qkv": w_qkv,
        "w_qk_t": w_qkv[:, 0:2 * HM].T.reshape(2 * PAIRS, P, P).transpose(1, 0, 2),
        "w_out": x["L0_attn_w_out"],
        "b_out": x["L0_attn_b_out"],
        "w_res": band,
        "pos_t": x["L0_ffn_positions"].T,
        "scales": x["L0_ffn_scales"],
        "vw": x["L0_ffn_value_weight"],
        "out_wt": x["L0_ffn_out_W"].T,
        "out_b": x["L0_ffn_out_b"],
        "ident_in": np.eye(P, dtype=np.float32),
    }
    arrays = {n: np.ascontiguousarray(a) for n, a in arrays.items()}
    nc = bacc.Bacc("TRN2", target_bir_lowering=False, num_devices=1)
    args = {n: nc.dram_tensor(n, a.shape, F32, kind="ExternalInput").ap() for n, a in arrays.items()}
    args["out"] = nc.dram_tensor("out", (B, T, P), F32, kind="ExternalOutput").ap()
    audio_tower(nc, **args)
    r = run_bass_kernel_spmd(nc, [arrays], core_ids=[0])
    return r.results[0]["out"]
```
